# Optimizing a Trainium2 kernel written in Bass

```python
import numpy as np
import jax
import jax.numpy as jnp

def _softmax(x, axis=-1):
    return jax.nn.softmax(x, axis=axis)

def _gelu(x):
    return jax.nn.gelu(x, approximate=True)

def _silu(x):
    return jax.nn.silu(x)

def _sigmoid(x):
    return jax.nn.sigmoid(x)

def _layernorm(x, axis=-1, eps=1e-05):
    m = jnp.mean(x, axis=axis, keepdims=True)
    v = jnp.var(x, axis=axis, keepdims=True)
    return (x - m) / jnp.sqrt(v + eps)

def _scatter_add(tgt, idx, src, axis=0):
    return tgt.at[idx].add(src)

def _segment_sum(src, seg, n):
    return jax.ops.segment_sum(src, seg, n)
kernel_name = 'mk_prb_d2_jaxref_r8_6572c2'

def setup_inputs(seed: int=0):
    np.random.seed(seed)
    _w = jnp.asarray

    def _L0_attn_setup():
        import jax, jax.numpy as jnp
        import numpy as np
        B, T, D, R = (8, 256, 256, 4)
        key = jax.random.key(seed)
        ks = jax.random.split(key, 9)
        u = jax.random.normal(ks[0], (B, T, D), dtype=jnp.float32)
        a = 3.0 + 0.2 * jax.random.uniform(ks[1], (D,), dtype=jnp.float32)
        b = 0.02 * jax.random.normal(ks[2], (D,), dtype=jnp.float32)
        c = 0.02 * jax.random.normal(ks[3], (D,), dtype=jnp.float32)
        d = 0.02 * jax.random.normal(ks[4], (D,), dtype=jnp.float32)
        gate_w = jax.random.normal(ks[5], (D, D), dtype=jnp.float32) / np.float32(np.sqrt(D))
        gate_b = jnp.zeros((D,), dtype=jnp.float32)
        d_lr_u = 0.02 * jax.random.normal(ks[6], (D, R), dtype=jnp.float32)
        d_lr_v = 0.02 * jax.random.normal(ks[7], (R, D), dtype=jnp.float32)
        return {'u': u, 'a': a, 'b': b, 'c': c, 'd': d, 'gate_w': gate_w, 'gate_b': gate_b, 'd_lr_u': d_lr_u, 'd_lr_v': d_lr_v}
    _L0_attn_in = _L0_attn_setup()

    def _L0_ffn_setup():
        import jax, jax.numpy as jnp
        import numpy as np
        TARGET_SPARSITY = 0.9
        LN_EPS = 1e-05

        def ternary_quant(W):
            scale = jnp.mean(jnp.abs(W))
            q = jnp.clip(jnp.round(W / (scale + 1e-08)), -1.0, 1.0) * scale
            return W + jax.lax.stop_gradient(q - W)

        def layernorm(x, gamma, beta):
            mu = jnp.mean(x, axis=-1, keepdims=True)
            var = jnp.var(x, axis=-1, keepdims=True)
            return (x - mu) * jax.lax.rsqrt(var + LN_EPS) * gamma + beta
        key = jax.random.key(seed)
        ks = jax.random.split(key, 3)
        B, S, D, N = (4, 256, 256, 1024)
        x = jax.random.normal(ks[0], (B, S, D), dtype=jnp.float32)
        W_syn = jax.random.normal(ks[1], (N, D), dtype=jnp.float32) * (1.0 / np.sqrt(D))
        b_syn = jnp.zeros((N,), dtype=jnp.float32)
        W_out = jax.random.normal(ks[2], (D, N), dtype=jnp.float32) * (1.0 / np.sqrt(N))
        b_out = jnp.zeros((D,), dtype=jnp.float32)
        gamma = jnp.ones((D,), dtype=jnp.float32)
        beta = jnp.zeros((D,), dtype=jnp.float32)
        return {'x': x, 'W_syn': W_syn, 'b_syn': b_syn, 'W_out': W_out, 'b_out': b_out, 'gamma': gamma, 'beta': beta}
    _L0_ffn_in = _L0_ffn_setup()

    def _L1_attn_setup():
        import jax, jax.numpy as jnp
        import numpy as np
        H = 16
        DK = 128
        DV = 128
        M = 64
        EPS = 1e-05
        CLAMP = 32.0
        ROPE_BASE = 10000.0

        def _rope(x, cos, sin):
            x1, x2 = jnp.split(x, 2, axis=-1)
            return jnp.concatenate([x1 * cos - x2 * sin, x2 * cos + x1 * sin], axis=-1)
        key = jax.random.key(seed)
        ks = jax.random.split(key, 9)
        B, T, D = (1, 256, 256)
        sc = 0.02
        return {'hidden_states': jax.random.normal(ks[0], (B, T, D), jnp.float32), 'Wq': jax.random.normal(ks[1], (H * DK, D), jnp.float32) * sc, 'Wk': jax.random.normal(ks[2], (H * DK, D), jnp.float32) * sc, 'Wv': jax.random.normal(ks[3], (H * DV, D), jnp.float32) * sc, 'Wg': jax.random.normal(ks[4], (H * DV, D), jnp.float32) * sc, 'Wo': jax.random.normal(ks[5], (D, H * DV), jnp.float32) * sc, 'Ws1': jax.random.normal(ks[6], (16, D), jnp.float32) * sc, 'Ws2': jax.random.normal(ks[7], (H * M, 16), jnp.float32) * sc, 'bs2': jnp.zeros((H * M,), jnp.float32), 'g_norm_weight': jnp.ones((DV,), jnp.float32)}
    _L1_attn_in = _L1_attn_setup()

    def _L1_ffn_setup():
        import jax, jax.numpy as jnp
        import numpy as np
        HIDDEN = 256
        INTER = 688
        LUT_SIZE = 16

        def _ghost_linear(x, idx, lut):
            w = lut[idx]
            return jnp.einsum('bsh,oh->bso', x, w)
        key = jax.random.key(seed)
        k_x, k_lut, k_g, k_u, k_d = jax.random.split(key, 5)
        x = jax.random.normal(k_x, (2, 512, HIDDEN), dtype=jnp.float32)
        lut = jax.random.normal(k_lut, (LUT_SIZE,), dtype=jnp.float32) * 0.02
        gate_idx = jax.random.randint(k_g, (INTER, HIDDEN), 0, LUT_SIZE, dtype=jnp.int32)
        up_idx = jax.random.randint(k_u, (INTER, HIDDEN), 0, LUT_SIZE, dtype=jnp.int32)
        down_idx = jax.random.randint(k_d, (HIDDEN, INTER), 0, LUT_SIZE, dtype=jnp.int32)
        return {'x': x, 'lut': lut, 'gate_idx': gate_idx, 'up_idx': up_idx, 'down_idx': down_idx}
    _L1_ffn_in = _L1_ffn_setup()
    _d = {'L0_attn_u': _L0_attn_in['u'], 'L0_attn_a': _L0_attn_in['a'], 'L0_attn_b': _L0_attn_in['b'], 'L0_attn_c': _L0_attn_in['c'], 'L0_attn_d': _L0_attn_in['d'], 'L0_attn_gate_w': _L0_attn_in['gate_w'], 'L0_attn_gate_b': _L0_attn_in['gate_b'], 'L0_attn_d_lr_u': _L0_attn_in['d_lr_u'], 'L0_attn_d_lr_v': _L0_attn_in['d_lr_v'], 'L0_ffn_W_syn': _L0_ffn_in['W_syn'], 'L0_ffn_b_syn': _L0_ffn_in['b_syn'], 'L0_ffn_W_out': _L0_ffn_in['W_out'], 'L0_ffn_b_out': _L0_ffn_in['b_out'], 'L0_ffn_gamma': _L0_ffn_in['gamma'], 'L0_ffn_beta': _L0_ffn_in['beta'], 'L1_attn_Wq': _L1_attn_in['Wq'], 'L1_attn_Wk': _L1_attn_in['Wk'], 'L1_attn_Wv': _L1_attn_in['Wv'], 'L1_attn_Wg': _L1_attn_in['Wg'], 'L1_attn_Wo': _L1_attn_in['Wo'], 'L1_attn_Ws1': _L1_attn_in['Ws1'], 'L1_attn_Ws2': _L1_attn_in['Ws2'], 'L1_attn_bs2': _L1_attn_in['bs2'], 'L1_attn_g_norm_weight': _L1_attn_in['g_norm_weight'], 'L1_ffn_lut': _L1_ffn_in['lut'], 'L1_ffn_gate_idx': _L1_ffn_in['gate_idx'], 'L1_ffn_up_idx': _L1_ffn_in['up_idx'], 'L1_ffn_down_idx': _L1_ffn_in['down_idx']}
    _x0 = _d['L0_attn_u']
    _d['L0_attn_u'] = jax.random.normal(jax.random.fold_in(jax.random.key(seed), 1), (2, 1024, 256), dtype=_x0.dtype)
    del _x0
    return _d

def reference(L0_attn_u, L0_attn_a, L0_attn_b, L0_attn_c, L0_attn_d, L0_attn_gate_w, L0_attn_gate_b, L0_attn_d_lr_u, L0_attn_d_lr_v, L0_ffn_W_syn, L0_ffn_b_syn, L0_ffn_W_out, L0_ffn_b_out, L0_ffn_gamma, L0_ffn_beta, L1_attn_Wq, L1_attn_Wk, L1_attn_Wv, L1_attn_Wg, L1_attn_Wo, L1_attn_Ws1, L1_attn_Ws2, L1_attn_bs2, L1_attn_g_norm_weight, L1_ffn_lut, L1_ffn_gate_idx, L1_ffn_up_idx, L1_ffn_down_idx):

    def _L0_attn_ref(u, a, b, c, d, gate_w, gate_b, d_lr_u, d_lr_v):
        import jax, jax.numpy as jnp
        import numpy as np
        B, T, D, R = (8, 256, 256, 4)
        Bs, Ts, Ds = u.shape
        rank = d_lr_u.shape[1]
        g = jax.nn.sigmoid(jnp.einsum('btd,ed->bte', u, gate_w) + gate_b)
        u_g = u * g
        aa = jnp.tanh(a)
        u_mean = jnp.mean(u_g, axis=1, keepdims=True)
        d_lr = u_mean @ d_lr_u @ d_lr_v / max(1.0, float(rank))
        d_eff = d + d_lr
        G = jnp.cumprod(jnp.broadcast_to(aa, (Ts, Ds)), axis=0)
        bu = b * u_g
        G_safe = G.at[0].set(jnp.maximum(G[0], 1e-06))
        z = bu / G_safe
        s = G * jnp.cumsum(z, axis=1)
        y = c * s + d_eff * u_g
        return y

    def _L0_ffn_ref(x, W_syn, b_syn, W_out, b_out, gamma, beta):
        import jax, jax.numpy as jnp
        import numpy as np
        TARGET_SPARSITY = 0.9
        LN_EPS = 1e-05

        def ternary_quant(W):
            scale = jnp.mean(jnp.abs(W))
            q = jnp.clip(jnp.round(W / (scale + 1e-08)), -1.0, 1.0) * scale
            return W + jax.lax.stop_gradient(q - W)

        def layernorm(x, gamma, beta):
            mu = jnp.mean(x, axis=-1, keepdims=True)
            var = jnp.var(x, axis=-1, keepdims=True)
            return (x - mu) * jax.lax.rsqrt(var + LN_EPS) * gamma + beta
        B, S, D = x.shape
        N = W_syn.shape[0]
        x_flat = x.reshape(-1, D)
        z = x_flat @ ternary_quant(W_syn).T + b_syn
        k = max(1, int(N * (1.0 - TARGET_SPARSITY)))
        topv, _ = jax.lax.top_k(z, k)
        thresh = topv[:, -1:]
        hidden = jnp.where(z >= thresh, jax.nn.relu(z), 0.0)
        out = hidden @ ternary_quant(W_out).T + b_out
        out = out.reshape(B, S, D)
        return layernorm(x + out, gamma, beta)

    def _L1_attn_ref(hidden_states, Wq, Wk, Wv, Wg, Wo, Ws1, Ws2, bs2, g_norm_weight):
        import jax, jax.numpy as jnp
        import numpy as np
        H = 16
        DK = 128
        DV = 128
        M = 64
        EPS = 1e-05
        CLAMP = 32.0
        ROPE_BASE = 10000.0

        def _rope(x, cos, sin):
            x1, x2 = jnp.split(x, 2, axis=-1)
            return jnp.concatenate([x1 * cos - x2 * sin, x2 * cos + x1 * sin], axis=-1)
        B, T, D = hidden_states.shape
        hs = hidden_states
        q = (hs @ Wq.T).reshape(B, T, H, DK)
        k = (hs @ Wk.T).reshape(B, T, H, DK)
        pos = jnp.arange(T, dtype=jnp.float32)
        inv_freq = 1.0 / ROPE_BASE ** (jnp.arange(0, DK, 2, dtype=jnp.float32) / DK)
        ang = pos[:, None] * inv_freq[None, :]
        cos = jnp.cos(ang)[None, :, None, :]
        sin = jnp.sin(ang)[None, :, None, :]
        q = _rope(q, cos, sin).transpose(0, 2, 1, 3)
        k = _rope(k, cos, sin).transpose(0, 2, 1, 3)
        v = (hs @ Wv.T).reshape(B, T, H, DV).transpose(0, 2, 1, 3)
        s = hs @ Ws1.T @ Ws2.T + bs2
        s = jnp.clip(s, -CLAMP, CLAMP).reshape(B, T, H, M).transpose(0, 2, 1, 3)
        z = jax.lax.cumlogsumexp(s, axis=2)
        es = jnp.exp(s)
        enz = jnp.exp(-z)
        scale = DK ** (-0.5)
        mask = jnp.tril(jnp.ones((T, T), dtype=bool))
        A = jnp.einsum('bhtd,bhjd->bhtj', q, k) * scale
        A = jnp.where(mask, A, 0.0)
        ok = enz * jnp.einsum('bhtj,bhjm->bhtm', A, es)
        qv = jax.nn.softmax(ok, axis=-1)
        W2 = jnp.einsum('bhtm,bhjm->bhtj', qv * enz, es)
        W2 = jnp.where(mask, W2, 0.0)
        o = jnp.einsum('bhtj,bhjd->bhtd', W2, v)
        o = o.transpose(0, 2, 1, 3)
        g = (hs @ Wg.T).reshape(B, T, H, DV)
        o_n = o * jax.lax.rsqrt(jnp.mean(o * o, axis=-1, keepdims=True) + EPS) * g_norm_weight
        o_g = o_n * (g * jax.nn.sigmoid(g))
        return o_g.reshape(B, T, H * DV) @ Wo.T

    def _L1_ffn_ref(x, lut, gate_idx, up_idx, down_idx):
        import jax, jax.numpy as jnp
        import numpy as np
        HIDDEN = 256
        INTER = 688
        LUT_SIZE = 16

        def _ghost_linear(x, idx, lut):
            w = lut[idx]
            return jnp.einsum('bsh,oh->bso', x, w)
        gate = _ghost_linear(x, gate_idx, lut)
        up = _ghost_linear(x, up_idx, lut)
        h = jax.nn.silu(gate) * up
        return _ghost_linear(h, down_idx, lut)
    x = L0_attn_u
    xn = _layernorm(x, axis=-1)
    x = x + _L0_attn_ref(xn, L0_attn_a, L0_attn_b, L0_attn_c, L0_attn_d, L0_attn_gate_w, L0_attn_gate_b, L0_attn_d_lr_u, L0_attn_d_lr_v) + _L0_ffn_ref(xn, L0_ffn_W_syn, L0_ffn_b_syn, L0_ffn_W_out, L0_ffn_b_out, L0_ffn_gamma, L0_ffn_beta)
    xn = _layernorm(x, axis=-1)
    x = x + _L1_attn_ref(xn, L1_attn_Wq, L1_attn_Wk, L1_attn_Wv, L1_attn_Wg, L1_attn_Wo, L1_attn_Ws1, L1_attn_Ws2, L1_attn_bs2, L1_attn_g_norm_weight) + _L1_ffn_ref(xn, L1_ffn_lut, L1_ffn_gate_idx, L1_ffn_up_idx, L1_ffn_down_idx)
    return x

_drawn_inputs = setup_inputs


def setup_inputs(seed=0):
    import zlib

    import numpy as np

    out = dict(_drawn_inputs(seed))
    spreads = {'L0_attn_gate_b': (0.0, 2.0),
     'L0_ffn_b_syn': (0.0, 0.1),
     'L0_ffn_b_out': (0.0, 0.1),
     'L0_ffn_gamma': (1.0, 0.2),
     'L0_ffn_beta': (0.0, 0.1),
     'L1_attn_bs2': (0.0, 2.0),
     'L1_attn_g_norm_weight': (1.0, 0.6)}
    factors = {'L0_attn_a': 8.0,
     'L0_attn_b': 8.0,
     'L0_attn_c': 8.0,
     'L0_attn_d': 8.0,
     'L0_attn_gate_w': 8.0,
     'L0_attn_d_lr_u': 64.0,
     'L0_attn_d_lr_v': 64.0,
     'L1_attn_Wq': 8.0,
     'L1_attn_Wk': 8.0,
     'L1_attn_Ws1': 8.0,
     'L1_attn_Ws2': 8.0,
     'L1_ffn_lut': 2.724}
    for name, (base, spread) in spreads.items():
        noise = np.random.default_rng([zlib.crc32(name.encode()), seed]).standard_normal(out[name].shape)
        drawn = base * np.exp(spread * noise) if base else spread * noise
        out[name] = jnp.asarray(drawn.astype(out[name].dtype))
    for name, factor in factors.items():
        out[name] = (out[name] * factor).astype(out[name].dtype)
    return out
```

```python
from contextlib import ExitStack

import numpy as np
import concourse.bass as bass
from concourse import mybir

F32 = mybir.dt.float32
BF16 = mybir.dt.bfloat16
I32 = mybir.dt.int32
ALU = mybir.AluOpType
ACT = mybir.ActivationFunctionType
AX = mybir.AxisListType

P = 128
D = 256
KD = D // P
NB, T = 2, 1024
TILES = NB * T // P
SEQ_TILES = T // P
HEADS, DK, M = 16, 128, 64
GH = 4
GROUPS = HEADS // GH
HD = HEADS * DK
NSYN = 1024
KN = NSYN // P
TOPK = max(1, int(NSYN * (1.0 - 0.9)))
ROUNDS = (TOPK + 7) // 8
INTER = 688
KI = (INTER + P - 1) // P
LAST = INTER - (KI - 1) * P
LUT = 16
LN_EPS = 1e-5
CLAMP = 32.0
QK_SCALE = float(DK) ** -0.5
LOW = -3.0e38
LUT_AT = (0, KD * INTER, 2 * KD * INTER)
LUT_END = LUT_AT[2] + KI * D
ARENA = 11264
MISC = 14
Y_STEPS = 4
N_SOFT = 7
N_TOP = 2 * ROUNDS
LUT_PARTS = ((0, KD * INTER), (KD * INTER, KD * INTER), (2 * KD * INTER, KI * D))
F_PARTS = ((P, 0, 0, 3 * P, 0), (P, 1, 0, 2 * P, 3), (LAST, 1, 2 * P, P, KI - 1))
V_F = 2 * len(F_PARTS)
VZ = GZ = 7


def reached(eng, sem, tile, per_tile, nth):
    value = tile * per_tile + nth
    if isinstance(value, int) and value <= 0:
        return
    eng.wait_ge(sem, value)


def unit(eng, sem, tile, group, nth=1, per_unit=1):
    reached(eng, sem, tile, GROUPS * per_unit, group * per_unit + nth)


def slot(head):
    return 2 * (1 - head % 2) + head // 2


def build(nc, a, out):
    with ExitStack() as ctx:
        def sb(name, shape, dt=F32):
            return ctx.enter_context(nc.sbuf_tensor(name, shape, dt))

        def sem(name):
            return ctx.enter_context(nc.semaphore(name))

        bank = ctx.enter_context(nc.psum_tensor("bank", [P, 8, 512], F32))

        wq = sb("wq", [P, KD, HD])
        wk = sb("wk", [P, KD, HD])
        wv = sb("wv", [P, KD, HD])
        wg = sb("wg", [P, KD, HD])
        wo = sb("wo", [P, HEADS, D])
        ws1 = sb("ws1", [P, KD, 16])
        ws2 = sb("ws2", [17, HEADS * M])
        w_lut = sb("w_lut", [P, LUT_END])
        w_gate = w_lut[:, 0:LUT_AT[1]].rearrange("p (k o) -> p k o", k=KD)
        w_up = w_lut[:, LUT_AT[1]:LUT_AT[2]].rearrange("p (k o) -> p k o", k=KD)
        w_down = w_lut[:, LUT_AT[2]:LUT_END].rearrange("p (k o) -> p k o", k=KI)
        t_syn = sb("t_syn", [P, KD, NSYN], BF16)
        t_out = sb("t_out", [P, KN, D])
        rope_tab = sb("rope_tab", [P, SEQ_TILES, 2 * 64])
        b_syn = sb("b_syn", [P, NSYN])
        rows = sb("rows", [P, 3, D])
        tri = sb("tri", [P, P])
        last_row = sb("last_row", [P, P])
        ident = sb("ident", [P, P])
        ones_m = sb("ones_m", [P, P])
        ident_b = sb("ident_b", [P, P], BF16)
        cols = sb("cols", [P, 6, KD])
        gnorm = sb("gnorm", [P, 1])
        half_neg = sb("half_neg", [P, TILES])
        mean1 = sb("mean1", [P, TILES, 2])
        rstd1 = sb("rstd1", [P, TILES])
        scales = sb("scales", [P, 8])

        s_qk = sb("s_qk", [P, HEADS * M])
        s_v = sb("s_v", [P, HEADS // 2, DK])
        csum = sb("csum", [P, HEADS * M])

        zbuf = sb("zbuf", [P, 2, NSYN])
        z = zbuf[:, 0, :]
        zw = zbuf[:, 1, :]
        x_in = sb("x_in", [P, D])
        xy_in = sb("xy_in", [P, D])
        xn = sb("xn", [P, D])
        xn_b = sb("xn_b", [P, D])
        xnT = sb("xnT", [P, D])
        x_part = sb("x_part", [P, 3, D], BF16)
        top8 = sb("top8", [P, 2, 8])
        thr = sb("thr", [P, 1])
        r0 = sb("r0", [P, D])
        r1 = sb("r1", [P, D])
        r2 = sb("r2", [P, D])
        x1 = sb("x1", [P, 2, D])
        stat = sb("stat", [P, 2, 6])
        mv = sb("mv", [P, 2, 2])
        rs = sb("rs", [P, 2, 2])
        xn2 = sb("xn2", [P, D])
        xT = sb("xT", [P, KD, P])
        s16 = sb("s16", [17, P])
        rope_now = sb("rope_now", [P, 2 * 64])
        o_fin = sb("o_fin", [P, D])

        arena = sb("arena", [P, ARENA])
        used = [0]

        def cut(words):
            v = arena[:, used[0]:used[0] + words]
            used[0] += words
            return v

        t1 = cut(1024)
        t2 = cut(1024)
        qk = cut(1024)
        qkT = cut(1024)
        v_sb = cut(1024).rearrange("p (b n) -> p b n", b=2)
        sc = cut(256)
        es = cut(512).rearrange("p (b n) -> p b n", b=2)
        esT = cut(512).rearrange("p (b n) -> p b n", b=2)
        enz = cut(256)
        am = cut(512)
        wm = cut(512)
        ox = cut(256)
        pr = cut(256)
        pT = cut(256)
        osq = cut(512)
        o_sb = cut(512)
        ogT = cut(512)
        sg = cut(1024).rearrange("p (b n) -> p b n", b=2)
        hT = t1.rearrange("p (k t) -> p k t", k=KN)
        small = sb("small", [P, 6, GH])
        f_th = qk[:, 0:KI * P].rearrange("p (k t) -> p k t", k=KI)
        f_h = t2[:, 0:KI * P].rearrange("p (k t) -> p k t", k=KI)
        assert used[0] <= ARENA

        x_all = wo[:, :, :].rearrange("p h n -> p (h n)").rearrange("p (t n) -> p t n", t=TILES)
        xn_all = wv[:, :, :].rearrange("p k n -> p (k n)").rearrange("p (t n) -> p t n", t=TILES)
        xnT_all = wg[:, :, :]
        ug = arena[:, 0:4096].rearrange("p (k n) -> p k n", k=KD)
        ys = arena[:, 4096:8192].rearrange("p (k n) -> p k n", k=KD)
        bu = arena[:, 8192:10240].rearrange("p (s n) -> p s n", s=2)
        gate_wT = arena[:, 10240:10752].rearrange("p (k n) -> p k n", k=KD)
        lr_u = arena[:, 10752:10760].rearrange("p (k n) -> p k n", k=KD)
        lr_v = arena[0:4, 10768:11024]
        u_sum = arena[:, 11024:11028].rearrange("p (k n) -> p k n", k=KD)
        r42 = arena[0:4, 11028:11030]
        d_eff = arena[:, 11032:11036].rearrange("p (k n) -> p k n", k=KD)
        col_t = arena[:, 11040:11052].rearrange("p (s k) -> p s k", k=KD)
        aa = arena[:, 11056:11058]
        stat1 = arena[:, 11072:11168].rearrange("p (t n) -> p t n", t=TILES)
        idx_i = arena[:, 0:LUT_END].bitcast(I32)
        idx_b = arena[:, LUT_END:LUT_END + LUT_END // 2].bitcast(BF16)
        hot = arena[:, 6432:6432 + KI * D].bitcast(BF16).rearrange("p (s n) -> p s n", s=2)
        diag = arena[:, 7968:7968 + 3 * LUT * P // 2].bitcast(BF16).rearrange("p (s k n) -> p s k n", s=3, k=LUT)
        lut = sb("lut", [P, 3, LUT])
        lut_b = sb("lut_b", [P, 3, LUT], BF16)
        syn_raw = zbuf[:, :, :].rearrange("p a n -> p (a n)").rearrange("p (k n) -> p k n", k=KD)
        tern_tmp = wk[:, 0, :]

        xy_dram = nc.dram_tensor("xy_scratch", (TILES * P, D), F32, kind="Internal").ap()

        ld_x = [sem(f"ld_x{n}") for n in range(4)]
        ld_misc = sem("ld_misc")
        ld_gate = sem("ld_gate")
        ld_syn = sem("ld_syn")
        ld_qk = sem("ld_qk")
        ld_v = sem("ld_v")
        ld_g = sem("ld_g")
        ld_o = sem("ld_o")
        ld_lut = sem("ld_lut")
        st_xy = sem("st_xy")
        v_stat = sem("v_stat")
        g_rstd = sem("g_rstd")
        v_xn = sem("v_xn")
        t_xn = sem("t_xn")
        c_xn = sem("c_xn")
        t_gate = sem("t_gate")
        c_gate = sem("c_gate")
        v_ug = sem("v_ug")
        t_lr = sem("t_lr")
        c_lr = sem("c_lr")
        v_scan = sem("v_scan")
        t_y = sem("t_y")
        v_xy = sem("v_xy")
        v_tern = sem("v_tern")
        t_tern = sem("t_tern")
        v_wo = sem("v_wo")
        c_aa = sem("c_aa")
        v_const = sem("v_const")
        spare = sem("spare")
        v_lut = sem("v_lut")
        v_hot = sem("v_hot")
        t_hot = sem("t_hot")
        c_lut = sem("c_lut")

        l_x = sem("l_x")
        l_xy = sem("l_xy")
        z_xn = sem("z_xn")
        z_t = sem("z_t")
        z_c = sem("z_c")
        z_part = sem("z_part")
        z_xnb = sem("z_xnb")
        z_mm = sem("z_mm")
        z_sb = sem("z_sb")
        z_top = sem("z_top")
        z_hid = sem("z_hid")
        z_hT = sem("z_hT")
        z_hc = sem("z_hc")
        z_out = sem("z_out")
        z_v = sem("z_v")
        z_g = sem("z_g")
        z_x2t = sem("z_x2t")
        z_x2 = sem("z_x2")
        rope_ld = sem("rope_ld")
        reset = sem("reset")
        p_s1 = sem("p_s1")
        c_s1 = sem("c_s1")
        p_qk = sem("p_qk")
        v_rope = sem("v_rope")
        g_rope = sem("g_rope")
        p_v = sem("p_v")
        c_v = sem("c_v")
        p_s = sem("p_s")
        v_sc = sem("v_sc")
        c_es = sem("c_es")
        p_g = sem("p_g")
        c_th = sem("c_th")
        v_sg = sem("v_sg")
        p_qkT = sem("p_qkT")
        c_qkT = sem("c_qkT")
        p_cs = sem("p_cs")
        c_cs = sem("c_cs")
        v_enz = sem("v_enz")
        p_esT = sem("p_esT")
        c_esT = sem("c_esT")
        p_a = sem("p_a")
        v_a = sem("v_a")
        p_ok = sem("p_ok")
        p_su = sem("p_su")
        v_su = sem("v_su")
        v_soft = sem("v_soft")
        c_soft = sem("c_soft")
        p_pT = sem("p_pT")
        c_pT = sem("c_pT")
        p_w2 = sem("p_w2")
        v_w2 = sem("v_w2")
        p_o = sem("p_o")
        c_o = sem("c_o")
        v_oss = sem("v_oss")
        g_r = sem("g_r")
        v_og4 = sem("v_og4")
        v_og = sem("v_og")
        p_ogT = sem("p_ogT")
        c_ogT = sem("c_ogT")
        p_s2 = sem("p_s2")
        v_s2 = sem("v_s2")
        p_fin = sem("p_fin")
        p_wo = sem("p_wo")
        v_fin = sem("v_fin")
        p_gate = sem("p_gate")
        p_up = sem("p_up")
        c_fth = sem("c_fth")
        v_f = sem("v_f")
        st_out = sem("st_out")

        block = ctx.enter_context(nc.Block())

        def apart(eng):
            eng.sem_inc(spare, 1)

        def tiles(eng, body):
            body(0, False)
            with eng.Fori(1, TILES - 1) as i:
                body(i, False)
            body(TILES - 1, True)

        @block.sync
        def _(sp):
            x_t = a["u"].rearrange("(t p) d -> p t d", p=P)
            for n in range(4):
                sp.dma_start(x_all[:, 4 * n:4 * n + 4, :], x_t[:, 4 * n:4 * n + 4, :]).then_inc(ld_x[n], 16)
            for dst, src in (
                (ident[:], a["ident"]), (tri[:], a["tri"]), (last_row[:], a["last_row"]),
                (cols[:, 0:5, :], a["cols"]), (gnorm[:], a["gnorm"]), (lut[:, 0, :], a["lut"].to_broadcast([P, LUT])),
                (b_syn[:], a["b_syn"].to_broadcast([P, NSYN])),
                (rows[:, 0, :], a["b_out"].to_broadcast([P, D])), (rows[:, 1, :], a["gamma"].to_broadcast([P, D])),
                (rows[:, 2, :], a["beta"].to_broadcast([P, D])),
                (rope_tab[:], a["rope"].rearrange("(t p) n -> p t n", p=P)),
                (ws1[:], a["ws1T"].rearrange("(k p) n -> p k n", p=P)),
                (ws2[0:16, :], a["ws2T"]), (ws2[16:17, :], a["bs2"]),
            ):
                sp.dma_start(dst, src).then_inc(ld_misc, 16)
            sp.dma_start(gate_wT, a["gate_wT"].rearrange("(k p) n -> p k n", p=P)).then_inc(ld_gate, 16)
            sp.dma_start(lr_u, a["lr_u"].rearrange("(k p) n -> p k n", p=P)).then_inc(ld_gate, 16)
            sp.dma_start(lr_v, a["lr_v"]).then_inc(ld_gate, 16)
            sp.dma_start(syn_raw, a["w_synT"].rearrange("(k p) n -> p k n", p=P)).then_inc(ld_syn, 16)
            sp.dma_start(t_out[:], a["w_outT"].rearrange("(k p) n -> p k n", p=P)).then_inc(ld_syn, 16)
            sp.dma_start(wq[:], a["wqT"].rearrange("(k p) n -> p k n", p=P)).then_inc(ld_qk, 16)
            sp.wait_ge(v_tern, 9)
            sp.dma_start(wk[:], a["wkT"].rearrange("(k p) n -> p k n", p=P)).then_inc(ld_qk, 16)
            sp.wait_ge(t_xn, 8)
            sp.dma_start(wv[:], a["wvT"].rearrange("(k p) n -> p k n", p=P)).then_inc(ld_v, 16)
            sp.wait_ge(t_gate, 8)
            sp.wait_ge(v_ug, 4)
            sp.dma_start(wg[:], a["wgT"].rearrange("(k p) n -> p k n", p=P)).then_inc(ld_g, 16)
            xy_t = xy_dram.rearrange("(t p) d -> p t d", p=P)
            for n in range(4):
                sp.wait_ge(v_xy, 2 * n + 2)
                sp.dma_start(xy_t[:, 4 * n:4 * n + 4, :], x_all[:, 4 * n:4 * n + 4, :]).then_inc(st_xy, 16)
            sp.wait_ge(st_xy, 64)
            sp.dma_start(wo[:], a["woT"].rearrange("(h p) n -> p h n", p=P)).then_inc(ld_o, 16)
            sp.wait_ge(v_lut, 1)
            for n, name in enumerate(("gate_idx", "up_idx")):
                sp.dma_start(idx_i[:, LUT_AT[n]:LUT_AT[n + 1]].rearrange("p (k n) -> p k n", k=KD),
                             a[name].rearrange("(k p) n -> p k n", p=P)).then_inc(ld_lut, 16)
            whole = (KI - 1) * D
            sp.dma_start(idx_i[:, LUT_AT[2]:LUT_AT[2] + whole].rearrange("p (k n) -> p k n", n=D),
                         a["down_idx"][0:(KI - 1) * P, :].rearrange("(k p) n -> p k n", p=P)).then_inc(ld_lut, 16)
            sp.dma_start(idx_i[0:LAST, LUT_AT[2] + whole:LUT_END], a["down_idx"][(KI - 1) * P:INTER, :]).then_inc(ld_lut, 16)

            def load_tile(j):
                reached(sp, z_xn, j, 1, 0)
                sp.dma_start(x_in[:], a["u"][bass.ds(j * P, P), :]).then_inc(l_x, 16)
                reached(sp, z_g, j, GZ, -2)
                sp.dma_start(xy_in[:], xy_dram[bass.ds(j * P, P), :]).then_inc(l_xy, 16)

            def body(i, last):
                if not last:
                    load_tile(i + 1)
                reached(sp, v_fin, i, 1, 1)
                sp.dma_start(out[bass.ds(i * P, P), :], o_fin[:]).then_inc(st_out, 16)

            load_tile(0)
            tiles(sp, body)
            sp.wait_ge(st_out, 16 * TILES)

        @block.tensor
        def _(pe):
            def mm(o, lhsT, rhs, start, stop):
                return pe.matmul(o, lhsT, rhs, start=start, stop=stop)

            pe.wait_ge(ld_misc, 16 * MISC)
            pe.wait_ge(v_const, 2)
            pe.wait_ge(v_tern, 2)
            mm(bank[:, 0, 0:2], ones_m[:], scales[:, 0:2], True, True).then_inc(t_tern, 1)
            for n in range(8):
                k, q = n // 4, n % 4
                if n == 0:
                    pe.wait_ge(v_tern, 3)
                for t in range(4):
                    pe.wait_ge(v_xn, 4 * q + t + 1)
                    ins = pe.transpose(bank[:, n, t * P:(t + 1) * P], xn_all[:, 4 * q + t, k * P:(k + 1) * P], ident[:])
                ins.then_inc(t_xn, 1)
            pe.wait_ge(ld_gate, 48)
            for n in range(8):
                e, c = n // 4, n % 4
                pe.wait_ge(c_xn, 8 if n == 0 else 8)
                for k in range(KD):
                    ins = mm(bank[:, n, :], gate_wT[:, k, e * P:(e + 1) * P], xnT_all[:, k, c * 512:(c + 1) * 512], k == 0, k == KD - 1)
                ins.then_inc(t_gate, 1)
            pe.wait_ge(v_ug, 5)
            pe.wait_ge(c_gate, 8)
            for k in range(KD):
                ins = mm(bank[0:4, 0, 0:NB], lr_u[:, k, :], u_sum[:, k, :], k == 0, k == KD - 1)
            ins.then_inc(t_lr, 1)
            pe.wait_ge(c_lr, 1)
            for k in range(KD):
                ins = mm(bank[:, 1, k * NB:(k + 1) * NB], lr_v[:, k * P:(k + 1) * P], r42, True, True)
            ins.then_inc(t_lr, 1)
            for n in range(8):
                if n == 1:
                    pe.wait_ge(v_scan, 1)
                for t in range(2):
                    tile = 2 * n + t
                    for k in range(KD):
                        pe.wait_ge(v_scan, 1 + Y_STEPS * (2 * (tile // SEQ_TILES) + k + 1))
                        ins = pe.transpose(bank[:, n, t * D + k * P:t * D + (k + 1) * P], ys[:, k, tile * P:(tile + 1) * P], ident[:])
                ins.then_inc(t_y, 1)

            def l0_xnT(j):
                reached(pe, z_xn, j, 1, 1)
                reached(pe, z_x2, j, 1, 0)
                for k in range(KD):
                    ins = pe.transpose(bank[:, 4, k * P:(k + 1) * P], xn[:, k * P:(k + 1) * P], ident[:])
                ins.then_inc(z_t, 1)

            def l0_z(j):
                reached(pe, z_part, j, 5, 5)
                reached(pe, v_s2, j, GROUPS, 0 - GROUPS)
                for c in range(2):
                    n = 0
                    for s in range(3):
                        for k in range(KD):
                            ins = mm(bank[:, 4 + c, :], x_part[:, s, k * P:(k + 1) * P], t_syn[:, k, c * 512:(c + 1) * 512], n == 0, n == 5)
                            n += 1
                    ins.then_inc(z_mm, 1)

            def l0_hT(j):
                reached(pe, z_hid, j, 1, 1)
                for n in range(KN):
                    ins = pe.transpose(bank[:, n // 4, (n % 4) * P:(n % 4 + 1) * P], zw[:, n * P:(n + 1) * P], ident[:])
                ins.then_inc(z_hT, 1)

            def l0_out(j):
                reached(pe, z_hc, j, 1, 1)
                for n in range(KN):
                    ins = mm(bank[:, 2, 0:D], hT[:, n, :], t_out[:, n, :], n == 0, n == KN - 1)
                ins.then_inc(z_out, 1)

            def l0_xT(j):
                reached(pe, z_v, j, VZ, VZ)
                for k in range(KD):
                    ins = pe.transpose(bank[:, 4, k * P:(k + 1) * P], xn2[:, k * P:(k + 1) * P], ident[:])
                ins.then_inc(z_x2t, 1)

            pe.wait_ge(v_xy, 8)
            l0_xnT(0)
            l0_z(0)
            for n, (at, w) in enumerate(LUT_PARTS):
                first = 0 if n % 2 == 0 else 3
                pe.wait_ge(v_lut, 9)
                if n == 0:
                    pe.wait_ge(z_sb, 0 + 2)
                if n == 2:
                    pe.wait_ge(c_lut, 3)
                for k in range(LUT):
                    pe.wait_ge(v_hot, n * LUT + k + 1)
                    for s in range(3):
                        for c in range(3):
                            lo, hi = c * 512, min(w, (c + 1) * 512)
                            ins = mm(bank[:, first + c, 0:hi - lo], diag[:, s, k, :], hot[:, k % 2, lo:hi],
                                     k == 0 and s == 0, k == LUT - 1 and s == 2)
                    ins.then_inc(t_hot, 1)
            pe.wait_ge(c_lut, 9)
            l0_hT(0)
            l0_out(0)
            l0_xT(0)
            pe.wait_ge(ld_qk, 32)
            pe.wait_ge(ld_v, 16)
            pe.wait_ge(ld_g, 16)
            pe.wait_ge(v_wo, 1)

            def project(o, w, g):
                for k in range(KD):
                    ins = mm(o, xT[:, k, :], w[:, k, g * 512:(g + 1) * 512], k == 0, k == KD - 1)
                return ins

            def body(i, last):
                j = i + 1
                for g in range(-1, GROUPS + 1):
                    now, nxt, prv = 0 <= g < GROUPS, g + 1 < GROUPS, g > 0
                    u, n1, p1 = g, g + 1, g - 1
                    if g == -1:
                        reached(pe, z_x2, i, 1, 1)
                        if not last:
                            l0_xnT(j)
                        reached(pe, v_f, i, V_F, 0)
                        for k in range(KD):
                            ins = mm(bank[0:16, 3, 0:P], ws1[:, k, :], xT[:, k, :], k == 0, k == KD - 1)
                        ins.then_inc(p_s1, 1)
                    if now:
                        unit(pe, g_rope, i, u, 2, 2)
                        for h in range(2 * GH):
                            ins = pe.transpose(bank[:, h // GH, (h % GH) * P:(h % GH + 1) * P], qk[:, h * P:(h + 1) * P], ident[:])
                        ins.then_inc(p_qkT, 1)
                    if prv:
                        unit(pe, v_soft, i, p1, N_SOFT, N_SOFT)
                        unit(pe, v_s2, i, p1, 0)
                        for h in range(2):
                            ins = pe.transpose(bank[:, 5, h * P:(h + 1) * P], pr[:, h * P:(h + 1) * P], ident[:])
                        ins.then_inc(p_pT, 1)
                    if now:
                        unit(pe, c_es, i, u)
                        unit(pe, v_sc, i, u)
                        unit(pe, reset, i, 0, 3, 3) if False else reached(pe, reset, i, 3, 3)
                        mm(bank[:, 3, 0:256], tri[:], es[:, u % 2, :], True, False)
                        mm(bank[:, 3, 0:256], last_row[:], csum[:, u * 256:(u + 1) * 256], False, True).then_inc(p_cs, 1)
                        unit(pe, c_cs, i, u)
                        for h in range(2):
                            ins = pe.transpose(bank[:, 3, h * P:(h + 1) * P], es[:, u % 2, h * P:(h + 1) * P], ident[:])
                        ins.then_inc(p_esT, 1)
                        unit(pe, c_qkT, i, u, 2, 2)
                        if g == 0:
                            reached(pe, z_sb, j, 2, 0 if last else 2)
                        else:
                            unit(pe, v_soft, i, u - 1, 1, N_SOFT)
                        for h in range(GH):
                            ins = mm(bank[:, 4, h * P:(h + 1) * P], qkT[:, 512 + h * P:512 + (h + 1) * P], qkT[:, h * P:(h + 1) * P], True, True)
                        ins.then_inc(p_a, 1)
                    if prv:
                        unit(pe, c_pT, i, p1)
                        if g == 1:
                            unit(pe, c_ogT, i, p1, 0)
                        else:
                            unit(pe, c_ogT, i, p1, 0)
                        for h in range(GH):
                            lo, q = (h % 2) * M, h // 2
                            ins = mm(bank[:, 6 - h % 2, q * P:(q + 1) * P], esT[lo:lo + M, p1 % 2, q * P:(q + 1) * P], pT[lo:lo + M, q * P:(q + 1) * P], True, True)
                        ins.then_inc(p_w2, 1)
                    if nxt:
                        if g == -1:
                            reached(pe, v_f, i, V_F, 0)
                        else:
                            unit(pe, c_qkT, i, u, 2, 2)
                        project(bank[:, 0, :], wq, n1)
                        project(bank[:, 1, :], wk, n1).then_inc(p_qk, 1)
                    elif g == GROUPS - 1 and not last:
                        unit(pe, c_qkT, i, u, 2, 2)
                        l0_hT(j)
                    elif g == GROUPS:
                        reached(pe, c_esT, i, GROUPS, GROUPS)
                        if not last:
                            reached(pe, z_v, j, VZ, 1)
                        ffn(w_up, 2, p_up)
                    if now:
                        unit(pe, v_a, i, u)
                        unit(pe, v_su, i, u, 1 - GROUPS)
                        for h in range(GH):
                            s = (GH * u + h) * M
                            mm(bank[:, 4, h * M:(h + 1) * M], am[:, h * P:(h + 1) * P], es[:, u % 2, h * M:(h + 1) * M], True, False)
                            ins = mm(bank[:, 4, h * M:(h + 1) * M], qkT[:, h * P:(h + 1) * P], s_qk[:, s:s + M], False, True)
                        ins.then_inc(p_ok, 1)
                        if prv:
                            unit(pe, v_w2, i, p1)
                        else:
                            reached(pe, z_sb, j, 2, 0 if last else 2)
                            unit(pe, v_s2, i, u, 0)
                        for h in range(GH):
                            ins = mm(bank[:, 5, h * M:(h + 1) * M], qk[:, 512 + h * P:512 + (h + 1) * P], es[:, u % 2, h * M:(h + 1) * M], True, True)
                        ins.then_inc(p_su, 1)
                    if prv:
                        unit(pe, v_w2, i, p1)
                        unit(pe, c_v, i, p1)
                        unit(pe, v_s2, i, p1, 1 - GROUPS)
                        if now:
                            unit(pe, v_su, i, u)
                        for h in range(GH):
                            lo, q = (h % 2) * M, h // 2
                            w = slot(h) * P
                            mm(bank[:, 6 - h % 2, q * P:(q + 1) * P], wm[:, w:w + P], v_sb[:, p1 % 2, h * P:(h + 1) * P], True, False)
                            ins = mm(bank[:, 6 - h % 2, q * P:(q + 1) * P], pT[lo:lo + M, q * P:(q + 1) * P], s_v[lo:lo + M, 2 * p1 + q, :], False, True)
                        ins.then_inc(p_o, 1)
                        unit(pe, c_o, i, p1, 2, 2)
                        for h in range(GH):
                            lo, q = (h % 2) * M, h // 2
                            ins = mm(bank[lo:lo + M, 5, q * P:(q + 1) * P], es[:, p1 % 2, h * M:(h + 1) * M], v_sb[:, p1 % 2, h * P:(h + 1) * P], True, True)
                        ins.then_inc(p_s2, 1)
                    if nxt:
                        if g == -1:
                            reached(pe, v_f, i, V_F, 0)
                        else:
                            unit(pe, v_sg, i, u)
                        project(bank[:, 2, :], wv, n1).then_inc(p_v, 1)
                        reached(pe, c_s1, i, 1, 1)
                        if now:
                            unit(pe, c_esT, i, u)
                        mm(bank[:, 3, 0:256], s16[:], ws2[:, n1 * 256:(n1 + 1) * 256], True, True).then_inc(p_s, 1)
                        unit(pe, c_v, i, n1)
                        project(bank[:, 2, :], wg, n1).then_inc(p_g, 1)
                    elif g == GROUPS - 1:
                        if not last:
                            unit(pe, v_sg, i, u)
                            l0_out(j)
                            reached(pe, z_hc, j, 1, 1)
                        unit(pe, c_qkT, i, u, 2, 2)
                        ffn(w_gate, 0, p_gate)
                    if g == -1 and not last:
                        l0_z(j)
                    if prv:
                        unit(pe, v_og, i, p1)
                        for h in range(GH):
                            ins = pe.transpose(bank[:, 6, h * P:(h + 1) * P], o_sb[:, slot(h) * P:(slot(h) + 1) * P], ident[:])
                        ins.then_inc(p_ogT, 1)
                        if g == GROUPS:
                            reached(pe, v_f, i, V_F, V_F)
                            for c in range(KI):
                                r = P if c < KI - 1 else LAST
                                mm(bank[:, 7, 0:D], f_h[0:r, c, :], w_down[0:r, c, :], False, False)
                        unit(pe, c_ogT, i, p1)
                        if g == 1:
                            reached(pe, v_fin, i, 1, 0)
                        for h in range(GH):
                            ins = mm(bank[:, 7, 0:D], ogT[:, h * P:(h + 1) * P], wo[:, GH * p1 + h, :],
                                     g == 1 and h == 0, g == GROUPS and h == GH - 1)
                        if g == GROUPS:
                            ins.then_inc(p_fin, 1)
                        else:
                            ins.then_inc(p_wo, 1)
                if not last:
                    l0_xT(j)

            def ffn(w, first, done):
                for c in range(KI):
                    r = P if c < KI - 1 else LAST
                    for k in range(KD):
                        ins = mm(bank[0:r, first + c // 3, (c % 3) * P:(c % 3 + 1) * P], w[:, k, c * P:c * P + r], xT[:, k, :], k == 0, k == KD - 1)
                ins.then_inc(done, 1)

            tiles(pe, body)

        @block.scalar
        def _(act):
            def copy(o, i_, scale=1.0):
                return act.activation(o, i_, ACT.Copy, scale=scale)

            for n in range(8):
                act.wait_ge(t_xn, n + 1)
                if n == 0:
                    act.wait_ge(ld_misc, 16 * MISC)
                copy(xnT_all[:, n // 4, (n % 4) * 512:(n % 4 + 1) * 512], bank[:, n, :]).then_inc(c_xn, 1)
            act.activation(aa, cols[:, 0, :], ACT.Tanh).then_inc(c_aa, 1)
            for n in range(8):
                e = n // 4
                act.wait_ge(t_gate, n + 1)
                act.activation(ug[:, e, (n % 4) * 512:(n % 4 + 1) * 512], bank[:, n, :], ACT.Sigmoid,
                               bias=cols[:, 4, e:e + 1]).then_inc(c_gate, 1)
            act.wait_ge(t_lr, 1)
            copy(r42, bank[0:4, 0, 0:NB]).then_inc(c_lr, 1)

            def l0_xnT(j):
                reached(act, z_t, j, 1, 1)
                reached(act, z_part, j, 5, 0)
                copy(xnT[:], bank[:, 4, 0:D]).then_inc(z_c, 1)

            def l0_hT(j):
                reached(act, z_hT, j, 1, 1)
                copy(hT, bank[:, 0:2, :]).then_inc(z_hc, 1)

            def l0_xT(j):
                reached(act, z_x2t, j, 1, 1)
                reached(act, p_up, j, 1, 0)
                copy(xT[:], bank[:, 4, 0:D]).then_inc(z_x2, 1)

            l0_xnT(0)
            for n, (at, w) in enumerate(LUT_PARTS):
                act.wait_ge(t_hot, LUT * (n + 1))
                for c in range(3):
                    lo, hi = c * 512, min(w, (c + 1) * 512)
                    copy(w_lut[:, at + lo:at + hi], bank[:, (0 if n % 2 == 0 else 3) + c, 0:hi - lo], 0.5 if n == 2 else 1.0).then_inc(c_lut, 1)
            l0_hT(0)
            l0_xT(0)

            def body(i, last):
                j = i + 1
                for g in range(-1, GROUPS + 1):
                    now, nxt, prv = 0 <= g < GROUPS, g + 1 < GROUPS, g > 0
                    u, n1, p1 = g, g + 1, g - 1
                    if g == -1:
                        if not last:
                            l0_xnT(j)
                        reached(act, p_s1, i, 1, 1)
                        copy(s16[0:16, :], bank[0:16, 3, 0:P]).then_inc(c_s1, 1)
                    if now:
                        unit(act, p_qkT, i, u)
                        unit(act, p_ok, i, u, 0)
                        copy(qkT[:, 0:512], bank[:, 0, :]).then_inc(c_qkT, 1)
                        copy(qkT[:, 512:1024], bank[:, 1, :]).then_inc(c_qkT, 1)
                    if prv:
                        unit(act, p_pT, i, p1)
                        unit(act, p_o, i, p1, 0)
                        copy(pT, bank[:, 5, 0:256]).then_inc(c_pT, 1)
                    if now:
                        unit(act, p_cs, i, u)
                        copy(csum[:, u * 256:(u + 1) * 256], bank[:, 3, 0:256]).then_inc(c_cs, 1)
                        unit(act, p_esT, i, u)
                        unit(act, p_w2, i, u - 1, 0)
                        copy(esT[:, u % 2, :], bank[:, 3, 0:256]).then_inc(c_esT, 1)
                    if g == GROUPS - 1 and not last:
                        l0_hT(j)
                    if now:
                        unit(act, v_soft, i, u, 3, N_SOFT)
                        act.activation(ox, ox, ACT.Exp).then_inc(c_soft, 1)
                    if prv:
                        unit(act, p_o, i, p1)
                        unit(act, v_oss, i, p1, 0)
                        unit(act, p_ogT, i, p1, 0)
                        act.activation(osq, bank[:, 5:7, 0:256], ACT.Square).then_inc(c_o, 1)
                        copy(o_sb, bank[:, 5:7, 0:256]).then_inc(c_o, 1)
                    if nxt:
                        unit(act, p_v, i, n1)
                        unit(act, p_s2, i, n1 - 2)
                        copy(v_sb[:, n1 % 2, :], bank[:, 2, :]).then_inc(c_v, 1)
                        unit(act, v_sc, i, n1)
                        unit(act, p_s2, i, n1 - 2)
                        act.activation(es[:, n1 % 2, :], sc, ACT.Exp).then_inc(c_es, 1)
                        unit(act, p_g, i, n1)
                        unit(act, v_og, i, n1 - 2)
                        act.activation(sg[:, n1 % 2, :], bank[:, 2, :], ACT.Tanh, scale=0.5).then_inc(c_th, 1)
                    elif g == GROUPS - 1:
                        reached(act, p_gate, i, 1, 1)
                        reached(act, p_su, i, GROUPS, GROUPS)
                        act.activation(f_th[:, 0:KI - 1, :].rearrange("p k t -> p (k t)")[:, 0:384], bank[:, 0, 0:384], ACT.Tanh, scale=0.5).then_inc(c_fth, 1)
                        act.activation(f_th[:, 3:KI - 1, :].rearrange("p k t -> p (k t)"), bank[:, 1, 0:256], ACT.Tanh, scale=0.5).then_inc(c_fth, 1)
                        act.activation(f_th[0:LAST, KI - 1, :], bank[0:LAST, 1, 256:384], ACT.Tanh, scale=0.5).then_inc(c_fth, 1)
                    if prv:
                        unit(act, p_ogT, i, p1)
                        unit(act, p_wo_or_fin, i, p1) if False else wo_done(act, i, p1)
                        copy(ogT, bank[:, 6, :]).then_inc(c_ogT, 1)
                if not last:
                    l0_xT(j)

            def wo_done(eng, i, g):
                if g > 0:
                    reached(eng, p_wo, i, GROUPS - 1, g)
                else:
                    reached(eng, p_fin, i, 1, 0)

            tiles(act, body)

        @block.vector
        def _(dve):
            tt, ts, stt = dve.tensor_tensor, dve.tensor_scalar, dve.scalar_tensor_tensor
            dve.memset(half_neg[:], -0.5).then_inc(v_const, 1)
            dve.memset(ones_m[:], 1.0).then_inc(v_const, 1)
            dve.memset(s16[:], 1.0).then_inc(v_const, 1)
            dve.wait_ge(ld_misc, 16 * MISC)
            dve.tensor_copy(ident_b[:], ident[:]).then_inc(v_const, 1)
            n = 0
            for t in range(TILES):
                dve.wait_ge(ld_x[t // 4], 16)
                dve.bn_stats(stat1[:, t, :], x_all[:, t, :]).then_inc(v_stat, 1)
            for t in range(TILES):
                dve.wait_ge(v_stat, t + 1)
                dve.bn_aggr(mean1[:, t, :], stat1[:, t, :]).then_inc(v_stat, 1)
            dve.wait_ge(g_rstd, 2)
            for t in range(TILES):
                ts(xn_all[:, t, :], x_all[:, t, :], mean1[:, t, 0:1], rstd1[:, t:t + 1], ALU.subtract, ALU.mult).then_inc(v_xn, 1)
            dve.wait_ge(ld_syn, 32)
            out_flat = t_out[:, :, :].rearrange("p k n -> p (k n)")
            syn_flat = zbuf[:, :, :].rearrange("p a n -> p (a n)")
            dve.tensor_reduce(scales[:, 0:1], syn_flat, AX.X, ALU.add, apply_absolute_value=True).then_inc(v_tern, 1)
            dve.tensor_reduce(scales[:, 1:2], out_flat, AX.X, ALU.add, apply_absolute_value=True).then_inc(v_tern, 1)
            dve.wait_ge(t_tern, 1)
            ts(scales[:, 2:4], bank[:, 0, 0:2], 1.0 / (NSYN * D), None, ALU.mult).then_inc(v_tern, 1)
            dve.wait_ge(v_tern, 3)
            ts(scales[:, 4:6], scales[:, 2:4], 1e-8, 0.5, ALU.add, ALU.mult).then_inc(v_tern, 1)
            dve.wait_ge(v_tern, 4)
            ts(scales[:, 6:8], scales[:, 4:6], -1.0, None, ALU.mult).then_inc(v_tern, 1)
            dve.wait_ge(v_tern, 5)
            ts(tern_tmp, syn_flat, scales[:, 6:7], None, ALU.is_lt).then_inc(v_tern, 1)
            dve.wait_ge(v_tern, 6)
            stt(t_syn[:, :, :].rearrange("p k n -> p (k n)"), syn_flat, scales[:, 4:5], tern_tmp, ALU.is_gt, ALU.subtract).then_inc(v_tern, 1)
            dve.wait_ge(v_tern, 7)
            ts(tern_tmp, out_flat, scales[:, 7:8], None, ALU.is_lt).then_inc(v_tern, 1)
            dve.wait_ge(v_tern, 8)
            stt(out_flat, out_flat, scales[:, 5:6], tern_tmp, ALU.is_gt, ALU.subtract).then_inc(v_tern, 1)
            for n in range(4):
                e, s = n // NB, n % NB
                dve.wait_ge(c_gate, 2 * n + 2)
                r = ug[:, e, s * T:(s + 1) * T]
                tt(r, r, xnT_all[:, e, s * T:(s + 1) * T], ALU.mult).then_inc(v_ug, 1)
            dve.wait_ge(v_ug, 4)
            dve.tensor_reduce(u_sum, ug.rearrange("p k (s t) -> p k s t", s=NB), AX.X, ALU.add).then_inc(v_ug, 1)
            dve.wait_ge(c_aa, 1)
            ts(col_t[:, 0, :], aa, 1e-6, None, ALU.max).then_inc(v_ug, 1)
            dve.wait_ge(v_ug, 6)
            dve.reciprocal(col_t[:, 1, :], col_t[:, 0, :]).then_inc(v_ug, 1)
            dve.wait_ge(v_ug, 7)
            tt(col_t[:, 2, :], aa, col_t[:, 1, :], ALU.mult).then_inc(v_ug, 1)
            tt(col_t[:, 3, :], cols[:, 1, :], cols[:, 2, :], ALU.mult).then_inc(v_ug, 1)
            dve.wait_ge(t_lr, 2)
            dve.wait_ge(v_ug, 9)
            stt(d_eff, bank[:, 1, 0:KD * NB].rearrange("p (k s) -> p k s", k=KD), 1.0 / (T * 4.0),
                cols[:, 3, :, None].to_broadcast([P, KD, NB]), ALU.mult, ALU.add).then_inc(v_scan, 1)
            n = 1
            for s in range(NB):
                for e in range(KD):
                    u_r, y_r, b_r = ug[:, e, s * T:(s + 1) * T], ys[:, e, s * T:(s + 1) * T], bu[:, e, :]
                    if s > 0:
                        dve.wait_ge(v_scan, n - 2 * Y_STEPS + 3)
                    ts(b_r, u_r, col_t[:, 3, e:e + 1], None, ALU.mult).then_inc(v_scan, 1)
                    dve.wait_ge(v_scan, n + 1)
                    ts(b_r[:, 0:1], b_r[:, 0:1], col_t[:, 2, e:e + 1], None, ALU.mult).then_inc(v_scan, 1)
                    dve.wait_ge(v_scan, n + 2)
                    dve.tensor_tensor_scan(y_r, aa[:, e:e + 1].to_broadcast([P, T]), b_r, 0.0, ALU.mult, ALU.add).then_inc(v_scan, 1)
                    dve.wait_ge(v_scan, n + 3)
                    stt(y_r, u_r, d_eff[:, e, s:s + 1], y_r, ALU.mult, ALU.add).then_inc(v_scan, 1)
                    n += Y_STEPS
            for n in range(8):
                dve.wait_ge(t_y, n + 1)
                r = x_all[:, 2 * n:2 * n + 2, :].rearrange("p t d -> p (t d)")
                tt(r, r, bank[:, n, :], ALU.add).then_inc(v_xy, 1)
            dve.memset(idx_i[:, LUT_END - D:LUT_END], 0).then_inc(v_lut, 1)

            def l0_xn(j):
                reached(dve, l_x, j, 16, 16)
                reached(dve, z_t, j, 1, 0)
                reached(dve, z_xnb, j, 1, 0)
                ts(xn[:], x_in[:], mean1[:, bass.ds(j, 1), 0:1].rearrange("p a b -> p (a b)"), rstd1[:, bass.ds(j, 1)], ALU.subtract, ALU.mult).then_inc(z_xn, 1)

            def l0_zsb(j):
                reached(dve, z_hid, j, 1, 0)
                for c in range(2):
                    reached(dve, z_mm, j, 2, c + 1)
                    stt(z[:, c * 512:(c + 1) * 512], bank[:, 4 + c, :], scales[:, 2:3], b_syn[:, c * 512:(c + 1) * 512], ALU.mult, ALU.add).then_inc(z_sb, 1)

            def l0_top(j, steps):
                for n in steps:
                    r, strike = n // 2, n % 2
                    if n == 0:
                        reached(dve, z_sb, j, 2, 2)
                    else:
                        reached(dve, z_top, j, N_TOP, n)
                    src = z if r == 0 else zw
                    if strike:
                        if n == 1:
                            reached(dve, z_hT, j, 1, 0)
                        apart(dve)
                        dve.match_replace(out=zw, in_to_replace=top8[:, r % 2, :], in_values=src, imm_value=LOW).then_inc(z_top, 1)
                    else:
                        apart(dve)
                        dve.max(out=top8[:, r % 2, :], in_=src).then_inc(z_top, 1)

            def l0_hidden(j):
                reached(dve, z_top, j, N_TOP, N_TOP - 1)
                k = TOPK - 8 * (ROUNDS - 1) - 1
                ts(thr[:], top8[:, (ROUNDS - 1) % 2, k:k + 1], 0.0, None, ALU.max).then_inc(z_top, 1)
                reached(dve, z_top, j, N_TOP, N_TOP)
                stt(zw, z, thr[:, 0:1], z, ALU.is_ge, ALU.mult).then_inc(z_hid, 1)

            def l0_norm(j, part):
                par = j % 2
                if part == 0:
                    reached(dve, z_out, j, 1, 1)
                    reached(dve, z_xnb, j, 1, 1)
                    stt(r0[:], bank[:, 2, 0:D], scales[:, 3:4], xn_b[:], ALU.mult, ALU.add).then_inc(z_v, 1)
                    reached(dve, z_v, j, VZ, 1)
                    dve.bn_stats(stat[:, 0, :], r0[:]).then_inc(z_v, 1)
                    reached(dve, z_v, j, VZ, 2)
                    apart(dve)
                    dve.bn_aggr(mv[:, 0, :], stat[:, 0, :]).then_inc(z_v, 1)
                elif part == 1:
                    reached(dve, z_g, j, GZ, 2)
                    ts(r1[:], r0[:], mv[:, 0, 0:1], rs[:, 0, 1:2], ALU.subtract, ALU.mult).then_inc(z_v, 1)
                elif part == 2:
                    reached(dve, z_g, j, GZ, 5)
                    x = x1[:, bass.ds(par, 1), :].rearrange("p a d -> p (a d)")
                    dve.bn_stats(stat[:, 1, :], x).then_inc(z_v, 1)
                    reached(dve, z_v, j, VZ, 5)
                    apart(dve)
                    dve.bn_aggr(mv[:, 1, :], stat[:, 1, :]).then_inc(z_v, 1)
                else:
                    reached(dve, z_g, j, GZ, 7)
                    x = x1[:, bass.ds(par, 1), :].rearrange("p a d -> p (a d)")
                    ts(xn2[:], x, mv[:, 1, 0:1], rs[:, 1, 1:2], ALU.subtract, ALU.mult).then_inc(z_v, 1)

            l0_xn(0)
            l0_zsb(0)
            dve.tensor_copy(lut_b[:, 0, :], lut[:, 0, :]).then_inc(v_lut, 1)
            for s in (1, 2):
                dve.wait_ge(v_lut, 2 * s)
                tt(lut[:, s, :], lut[:, s - 1, :], lut_b[:, s - 1, :], ALU.subtract).then_inc(v_lut, 1)
                dve.wait_ge(v_lut, 2 * s + 1)
                dve.tensor_copy(lut_b[:, s, :], lut[:, s, :]).then_inc(v_lut, 1)
            for s in range(3):
                dve.wait_ge(v_lut, 6)
                tt(diag[:, s, :, :], ident_b[:, None, :].to_broadcast([P, LUT, P]), lut_b[:, s, :, None].to_broadcast([P, LUT, P]), ALU.mult).then_inc(v_lut, 1)
            dve.wait_ge(ld_lut, 64)
            dve.tensor_copy(idx_b, idx_i).then_inc(v_lut, 1)
            dve.wait_ge(v_lut, 10)
            for n, (at, w) in enumerate(LUT_PARTS):
                for k in range(LUT):
                    m = n * LUT + k
                    if m >= 2:
                        dve.wait_ge(t_hot, m - 1)
                    ts(hot[:, k % 2, 0:w], idx_b[:, at:at + w], float(k), None, ALU.is_equal).then_inc(v_hot, 1)
            l0_top(0, range(N_TOP - 1))
            l0_hidden(0)
            dve.wait_ge(ld_o, 16)
            wo_flat = wo[:, :, :].rearrange("p h n -> p (h n)")
            ts(wo_flat, wo_flat, gnorm[:, 0:1], 0.5, ALU.mult, ALU.mult).then_inc(v_wo, 1)
            for part in range(4):
                l0_norm(0, part)

            def zero_state():
                dve.memset(s_qk[:], 0.0).then_inc(reset, 1)
                dve.memset(s_v[:], 0.0).then_inc(reset, 1)
                dve.memset(csum[:], 0.0).then_inc(reset, 1)

            def rope(i, g):
                unit(dve, p_qk, i, g)
                unit(dve, g_rope, i, g, 0, 2)
                if g == 0:
                    reached(dve, rope_ld, i, 1, 1)
                    reached(dve, z_out, i, 1, 1)
                    reached(dve, p_fin, i, 1, 0)
                v = bank[:, 0:2, :].rearrange("p b (h a m) -> p (b h) a m", a=2, m=64)
                cos = rope_now[:, None, None, 0:64].to_broadcast([P, 2 * GH, 2, 64])
                sin = rope_now[:, None, None, 64:128].to_broadcast([P, 2 * GH, 2, 64])
                tt(t1.rearrange("p (h a m) -> p h a m", a=2, m=64), v, cos, ALU.mult).then_inc(v_rope, 1)
                tt(t2.rearrange("p (h a m) -> p h a m", a=2, m=64), v[:, :, ::-1, :], sin, ALU.mult).then_inc(v_rope, 1)

            def heads(x, n):
                return x.rearrange("p (h m) -> p h m", h=GH)

            def over(x, n):
                return x[:, :, None].to_broadcast([P, GH, n])

            def body(i, last):
                j = i + 1
                top = list(range(N_TOP - 1))
                for g in range(-1, GROUPS + 1):
                    now, nxt, prv = 0 <= g < GROUPS, g + 1 < GROUPS, g > 0
                    u, n1, p1 = g, g + 1, g - 1
                    if g == -1:
                        if not last:
                            l0_xn(j)
                        reached(dve, p_o, i, GROUPS, 0)
                        if isinstance(i, int):
                            if i % SEQ_TILES == 0:
                                zero_state()
                            else:
                                dve.sem_inc(reset, 3)
                        else:
                            apart(dve)
                            with dve.If(i == SEQ_TILES):
                                zero_state()
                            with dve.Else():
                                dve.sem_inc(reset, 3)
                    if now:
                        unit(dve, c_cs, i, u)
                        unit(dve, v_soft, i, u, 0, N_SOFT)
                        dve.reciprocal(enz, csum[:, u * 256:(u + 1) * 256]).then_inc(v_enz, 1)
                        unit(dve, p_a, i, u)
                        unit(dve, p_ok, i, u, 0)
                        tt(heads(am, P), heads(bank[:, 4, :], P), tri[:, None, :].to_broadcast([P, GH, P]), ALU.mult).then_inc(v_a, 1)
                    if prv:
                        unit(dve, p_w2, i, p1)
                        unit(dve, p_o, i, p1, 0)
                        tt(wm.rearrange("p (b q t) -> p b q t", b=2, q=2), bank[:, 5:7, 0:256].rearrange("p b (q t) -> p b q t", q=2),
                           tri[:, None, None, :].to_broadcast([P, 2, 2, P]), ALU.mult).then_inc(v_w2, 1)
                    if nxt:
                        rope(i, n1)
                    if g == GROUPS:
                        reached(dve, g_rope, i, 2 * GROUPS, 2 * GROUPS)
                        for n, (r, b, lo, w, k0) in enumerate(F_PARTS):
                            reached(dve, c_fth, i, 3, 3)
                            f = f_th[0:r, k0:k0 + w // P, :].rearrange("p k t -> p (k t)")
                            stt(f, f, 1.0, bank[0:r, b, lo:lo + w], ALU.add, ALU.mult).then_inc(v_f, 1)
                        for n, (r, b, lo, w, k0) in enumerate(F_PARTS):
                            reached(dve, p_up, i, 1, 1)
                            reached(dve, v_f, i, V_F, n + 1)
                            f = f_th[0:r, k0:k0 + w // P, :].rearrange("p k t -> p (k t)")
                            h = f_h[0:r, k0:k0 + w // P, :].rearrange("p k t -> p (k t)")
                            tt(h, f, bank[0:r, 2 + b, lo:lo + w], ALU.mult).then_inc(v_f, 1)
                    if now:
                        unit(dve, p_ok, i, u)
                        unit(dve, v_enz, i, u)
                        unit(dve, p_pT, i, u, 0)
                        stt(ox, bank[:, 4, 0:256], QK_SCALE, enz, ALU.mult, ALU.mult).then_inc(v_soft, 1)
                        unit(dve, v_soft, i, u, 1, N_SOFT)
                        dve.tensor_reduce(small[:, 0, :], heads(ox, M), AX.X, ALU.max).then_inc(v_soft, 1)
                        unit(dve, v_soft, i, u, 2, N_SOFT)
                        tt(heads(ox, M), heads(ox, M), over(small[:, 0, :], M), ALU.subtract).then_inc(v_soft, 1)
                        unit(dve, p_su, i, u)
                        s = s_qk[:, u * 256:(u + 1) * 256]
                        tt(s, s, bank[:, 5, 0:256], ALU.add).then_inc(v_su, 1)
                    if not last and now and g < GROUPS - 1:
                        l0_top(j, top[0:4])
                        top = top[4:]
                    if prv:
                        unit(dve, c_o, i, p1, 1, 2)
                        dve.tensor_reduce(small[:, 4, :], heads(osq, DK), AX.X, ALU.add).then_inc(v_oss, 1)
                    if now:
                        unit(dve, c_soft, i, u)
                        dve.tensor_reduce(small[:, 1, :], heads(ox, M), AX.X, ALU.add).then_inc(v_soft, 1)
                        unit(dve, v_soft, i, u, 4, N_SOFT)
                        dve.reciprocal(small[:, 2, :], small[:, 1, :]).then_inc(v_soft, 1)
                        tt(ox, ox, enz, ALU.mult).then_inc(v_soft, 1)
                        unit(dve, v_soft, i, u, 6, N_SOFT)
                        tt(heads(pr, M), heads(ox, M), over(small[:, 2, :], M), ALU.mult).then_inc(v_soft, 1)
                    if prv:
                        unit(dve, p_s2, i, p1)
                        s = s_v[:, 2 * p1:2 * p1 + 2, :]
                        tt(s, s, bank[:, 5, 0:256].rearrange("p (q n) -> p q n", q=2), ALU.add).then_inc(v_s2, 1)
                        unit(dve, g_r, i, p1, 2, 2)
                        unit(dve, v_sg, i, p1)
                        unit(dve, c_o, i, p1, 2, 2)
                        for h in range(GH):
                            w = slot(h)
                            o = o_sb[:, w * P:(w + 1) * P]
                            ins = stt(o, o, small[:, 5, w:w + 1], sg[:, p1 % 2, h * P:(h + 1) * P], ALU.mult, ALU.mult)
                            ins.then_inc(v_og4, 1)
                        unit(dve, v_og4, i, p1, 4, 4)
                        dve.nop().then_inc(v_og, 1)
                    if nxt:
                        unit(dve, p_s, i, n1)
                        unit(dve, c_es, i, n1, 0)
                        ts(sc, bank[:, 3, 0:256], -CLAMP, CLAMP, ALU.max, ALU.min).then_inc(v_sc, 1)
                        unit(dve, c_th, i, n1)
                        r = sg[:, n1 % 2, :]
                        stt(r, r, 1.0, bank[:, 2, :], ALU.add, ALU.mult).then_inc(v_sg, 1)
                    if g == -1 and not last:
                        l0_zsb(j)
                    if not last and now and g < GROUPS - 1:
                        m = len(top) if g == GROUPS - 2 else 4
                        l0_top(j, top[0:m])
                        top = top[m:]
                        if g == GROUPS - 2:
                            l0_hidden(j)
                    if not last and g == GROUPS - 1:
                        l0_norm(j, 0)
                    if not last and g == GROUPS:
                        for part in (1, 2, 3):
                            l0_norm(j, part)
                reached(dve, p_fin, i, 1, 1)
                reached(dve, st_out, i, 16, 0)
                x = x1[:, bass.ds(i % 2, 1), :].rearrange("p a d -> p (a d)")
                tt(o_fin[:], x, bank[:, 7, 0:D], ALU.add).then_inc(v_fin, 1)

            tiles(dve, body)

        @block.gpsimd
        def _(pool):
            tt, ts = pool.tensor_tensor, pool.tensor_scalar
            pool.wait_ge(v_stat, 2 * TILES)
            pool.wait_ge(v_const, 1)
            ts(rstd1[:], mean1[:, :, 1], LN_EPS, None, ALU.add).then_inc(g_rstd, 1)
            pool.wait_ge(g_rstd, 1)
            tt(rstd1[:], rstd1[:], half_neg[:], ALU.pow).then_inc(g_rstd, 1)

            def l0_parts(j):
                reached(pool, z_c, j, 1, 1)
                reached(pool, z_mm, j, 2, 0)
                for n in range(5):
                    if n > 0:
                        reached(pool, z_part, j, 5, n)
                    apart(pool)
                    if n % 2 == 0:
                        ins = pool.tensor_copy(x_part[:, n // 2, :], xnT[:])
                    else:
                        ins = tt(xnT[:], xnT[:], x_part[:, n // 2, :], ALU.subtract)
                    ins.then_inc(z_part, 1)
                reached(pool, z_xn, j, 1, 1)
                reached(pool, z_v, j, VZ, 1 - VZ)
                tt(xn_b[:], xn[:], rows[:, 0, :], ALU.add).then_inc(z_xnb, 1)

            def l0_norm(j, part):
                par = j % 2
                n = 0 if part == 0 else 5
                if part != 1:
                    reached(pool, z_v, j, VZ, 3 if part == 0 else 6)
                    q = 0 if part == 0 else 1
                    apart(pool)
                    ts(rs[:, q, 0:1], mv[:, q, 1:2], LN_EPS, None, ALU.add).then_inc(z_g, 1)
                    reached(pool, z_g, j, GZ, n + 1)
                    tt(rs[:, q, 1:2], rs[:, q, 0:1], half_neg[:, 0:1], ALU.pow).then_inc(z_g, 1)
                else:
                    reached(pool, z_v, j, VZ, 4)
                    tt(r2[:], r1[:], rows[:, 1, :], ALU.mult).then_inc(z_g, 1)
                    reached(pool, z_g, j, GZ, 3)
                    tt(r2[:], r2[:], rows[:, 2, :], ALU.add).then_inc(z_g, 1)
                    reached(pool, z_g, j, GZ, 4)
                    reached(pool, l_xy, j, 16, 16)
                    reached(pool, v_fin, j, 1, -1)
                    x = x1[:, bass.ds(par, 1), :].rearrange("p a d -> p (a d)")
                    tt(x, r2[:], xy_in[:], ALU.add).then_inc(z_g, 1)

            pool.wait_ge(ld_misc, 16 * MISC)
            l0_parts(0)
            for part in range(3):
                l0_norm(0, part)

            def body(i, last):
                j = i + 1
                for g in range(-1, GROUPS + 1):
                    nxt, prv = g + 1 < GROUPS, g > 0
                    n1, p1 = g + 1, g - 1
                    if g == -1:
                        reached(pool, v_rope, i, 2 * GROUPS, 0)
                        apart(pool)
                        pool.tensor_copy(rope_now[:], rope_tab[:, bass.ds(i % SEQ_TILES, 1), :].rearrange("p a n -> p (a n)")).then_inc(rope_ld, 1)
                        if not last:
                            l0_parts(j)
                    if nxt:
                        unit(pool, v_rope, i, n1, 2, 2)
                        unit(pool, p_su, i, n1, 0)
                        if g == -1:
                            reached(pool, v_f, i, V_F, 0)
                        v = lambda x, q: x.rearrange("p (h a m) -> p h a m", a=2, m=64)[:, :, q, :]
                        tt(v(qk, 0), v(t1, 0), v(t2, 0), ALU.subtract).then_inc(g_rope, 1)
                        tt(v(qk, 1), v(t1, 1), v(t2, 1), ALU.add).then_inc(g_rope, 1)
                    if prv:
                        unit(pool, v_oss, i, p1)
                        unit(pool, v_og, i, p1, 0)
                        apart(pool)
                        ts(small[:, 3, :], small[:, 4, :], 1.0 / DK, LN_EPS, ALU.mult, ALU.add).then_inc(g_r, 1)
                        unit(pool, g_r, i, p1, 1, 2)
                        tt(small[:, 5, :], small[:, 3, :], half_neg[:, 0:GH], ALU.pow).then_inc(g_r, 1)
                    if g == GROUPS - 1 and not last:
                        l0_norm(j, 0)
                    if g == GROUPS and not last:
                        l0_norm(j, 1)
                        l0_norm(j, 2)

            tiles(pool, body)


_OUT = (TILES * P, D)


def kernel(**inputs):
    import numpy as _np
    import concourse.bacc as _bacc
    from concourse import mybir as _mybir
    from concourse.bass_utils import run_bass_kernel_spmd as _run

    def arr(name):
        return _np.asarray(inputs[name])

    def col(name):
        return arr(name).reshape(KD, P).T

    pos = _np.arange(T, dtype=_np.float32)
    inv = _np.float32(1.0) / _np.float32(10000.0) ** (_np.arange(0, DK, 2, dtype=_np.float32) / _np.float32(DK))
    ang = pos[:, None] * inv[None, :]
    tri = _np.triu(_np.ones((P, P), _np.float32))
    last = _np.zeros((P, P), _np.float32)
    last[P - 1] = 1.0
    arrays = {
        "u": arr("L0_attn_u").reshape(TILES * P, D),
        "ident": _np.eye(P, dtype=_np.float32),
        "tri": tri,
        "last_row": last,
        "rope": _np.concatenate([_np.cos(ang), _np.sin(ang)], axis=1).astype(_np.float32),
        "cols": _np.stack([col("L0_attn_" + n) for n in ("a", "b", "c", "d", "gate_b")], axis=1),
        "gnorm": arr("L1_attn_g_norm_weight").reshape(DK, 1),
        "lut": arr("L1_ffn_lut").reshape(1, LUT),
        "gate_wT": arr("L0_attn_gate_w").T,
        "lr_u": arr("L0_attn_d_lr_u"),
        "lr_v": arr("L0_attn_d_lr_v"),
        "w_synT": arr("L0_ffn_W_syn").T,
        "w_outT": arr("L0_ffn_W_out").T,
        "b_syn": arr("L0_ffn_b_syn").reshape(1, NSYN),
        "b_out": arr("L0_ffn_b_out").reshape(1, D),
        "gamma": arr("L0_ffn_gamma").reshape(1, D),
        "beta": arr("L0_ffn_beta").reshape(1, D),
        "wqT": arr("L1_attn_Wq").T,
        "wkT": arr("L1_attn_Wk").T,
        "wvT": arr("L1_attn_Wv").T,
        "wgT": arr("L1_attn_Wg").T,
        "woT": arr("L1_attn_Wo").T,
        "ws1T": arr("L1_attn_Ws1").T,
        "ws2T": arr("L1_attn_Ws2").T,
        "bs2": arr("L1_attn_bs2").reshape(1, HEADS * M),
        "gate_idx": arr("L1_ffn_gate_idx").T,
        "up_idx": arr("L1_ffn_up_idx").T,
        "down_idx": arr("L1_ffn_down_idx").T,
    }
    arrays = {n: _np.ascontiguousarray(x) for n, x in arrays.items()}
    nc = _bacc.Bacc("TRN2", target_bir_lowering=False, num_devices=1)
    aps = {n: nc.dram_tensor("in_" + n, x.shape, _mybir.dt.from_np(x.dtype), kind="ExternalInput").ap() for n, x in arrays.items()}
    res = nc.dram_tensor("result", _OUT, F32, kind="ExternalOutput").ap()
    build(nc, aps, res)
    r = _run(nc, [{"in_" + n: x for n, x in arrays.items()}], core_ids=[0])
    return r.results[0]["result"].reshape(NB, T, D)
```

```python
from contextlib import ExitStack

import numpy as np
import concourse.bass as bass
from concourse import mybir

F32 = mybir.dt.float32
BF16 = mybir.dt.bfloat16
I32 = mybir.dt.int32
ALU = mybir.AluOpType
ACT = mybir.ActivationFunctionType
AX = mybir.AxisListType

P = 128
D = 256
KD = D // P
NB, T = 2, 1024
TILES = NB * T // P
SEQ_TILES = T // P
HEADS, DK, M = 16, 128, 64
GH = 4
GROUPS = HEADS // GH
HD = HEADS * DK
NSYN = 1024
KN = NSYN // P
TOPK = max(1, int(NSYN * (1.0 - 0.9)))
ROUNDS = (TOPK + 7) // 8
INTER = 688
KI = (INTER + P - 1) // P
LAST = INTER - (KI - 1) * P
LUT = 16
LN_EPS = 1e-5
CLAMP = 32.0
QK_SCALE = float(DK) ** -0.5
LOW = -3.0e38
LUT_AT = (0, KD * INTER, 2 * KD * INTER)
LUT_END = LUT_AT[2] + KI * D
ARENA = 12544
MISC = 11
Y_STEPS = 4
N_SOFT = 7
N_TOP = 2 * ROUNDS
LUT_PARTS = ((0, KD * INTER), (KD * INTER, KD * INTER), (2 * KD * INTER, KI * D))
F_PARTS = ((P, 0, 0, 3 * P, 0), (P, 1, 0, 2 * P, 3), (LAST, 1, 2 * P, P, KI - 1))
V_F = 2 * len(F_PARTS)
TOP_OF = {2: (0, 6), 3: (6, 14), 0: (14, 21), 1: (21, N_TOP - 1)}
TOP_HEAD = TOP_OF[3][1]
TOP0_AT = 27
Z_BANKS = (7, 6)
VZ = GZ = 7


def reached(eng, sem, tile, per_tile, nth):
    value = tile * per_tile + nth
    if isinstance(value, int) and value <= 0:
        return
    eng.wait_ge(sem, value)


def unit(eng, sem, tile, group, nth=1, per_unit=1):
    reached(eng, sem, tile, GROUPS * per_unit, group * per_unit + nth)


def slot(head):
    return 2 * (1 - head % 2) + head // 2


def o_slot(head):
    return 2 * (head % 2) + head // 2


def build(nc, a, out):
    with ExitStack() as ctx:
        def sb(name, shape, dt=F32):
            return ctx.enter_context(nc.sbuf_tensor(name, shape, dt))

        def sem(name):
            return ctx.enter_context(nc.semaphore(name))

        bank = ctx.enter_context(nc.psum_tensor("bank", [P, 8, 512], F32))

        wq = sb("wq", [P, KD, HD])
        wk = sb("wk", [P, KD, HD])
        wv = sb("wv", [P, KD, HD])
        wg = sb("wg", [P, KD, HD])
        wo = sb("wo", [P, HEADS, D])
        ws1 = sb("ws1", [P, KD, 16])
        ws2 = sb("ws2", [17, HEADS * M])
        w_lut = sb("w_lut", [P, LUT_END])
        w_gate = w_lut[:, 0:LUT_AT[1]].rearrange("p (k o) -> p k o", k=KD)
        w_up = w_lut[:, LUT_AT[1]:LUT_AT[2]].rearrange("p (k o) -> p k o", k=KD)
        w_down = w_lut[:, LUT_AT[2]:LUT_END].rearrange("p (k o) -> p k o", k=KI)
        t_syn = sb("t_syn", [P, KD, NSYN], BF16)
        t_out = sb("t_out", [P, KN, D])
        rope_tab = sb("rope_tab", [P, SEQ_TILES, 2 * 64])
        b_syn = sb("b_syn", [P, NSYN])
        rows = sb("rows", [P, 3, D])
        tri = sb("tri", [P, P])
        last_row = sb("last_row", [P, P])
        ident = sb("ident", [P, P])
        ident_b = sb("ident_b", [P, P], BF16)
        cols = sb("cols", [P, 6, KD])
        gnorm = sb("gnorm", [P, 1])
        half_neg = sb("half_neg", [P, TILES])
        mean1 = sb("mean1", [P, TILES, 2])
        rstd1 = sb("rstd1", [P, TILES])
        scales = sb("scales", [P, 8])

        s_qk = sb("s_qk", [P, HEADS * M])
        s_v = sb("s_v", [P, HEADS // 2, DK])
        csum = sb("csum", [P, HEADS * M])

        zbuf = sb("zbuf", [P, 2, NSYN])
        z = zbuf[:, 0, :]
        zw = zbuf[:, 1, :]
        x_in = sb("x_in", [P, D])
        xy_in = sb("xy_in", [P, D])
        xn = sb("xn", [P, D])
        xn_b = sb("xn_b", [P, D])
        xnT = sb("xnT", [P, D])
        x_part = sb("x_part", [P, 3, D], BF16)
        top8 = sb("top8", [P, 2, 8])
        thr = sb("thr", [P, 1])
        norm = sb("norm", [P, D])
        x1 = sb("x1", [P, 2, D])
        stat = sb("stat", [P, 2, 6])
        mv = sb("mv", [P, 2, 2])
        rs = sb("rs", [P, 2, 2])
        xT = sb("xT", [P, KD, P])
        s16 = sb("s16", [17, P])
        rope_now = sb("rope_now", [P, 2 * 64])
        o_fin = sb("o_fin", [P, D])

        arena = sb("arena", [P, ARENA])
        used = [0]

        def cut(words):
            v = arena[:, used[0]:used[0] + words]
            used[0] += words
            return v

        hT = cut(1024).rearrange("p (k t) -> p k t", k=KN)
        t1 = cut(1024)
        t2 = cut(1024)
        qk = cut(1024)
        qkT = cut(1024)
        v_sb = cut(1024).rearrange("p (b n) -> p b n", b=2)
        es = cut(512).rearrange("p (b n) -> p b n", b=2)
        esT = cut(512).rearrange("p (b n) -> p b n", b=2)
        enz = cut(256)
        am = cut(512)
        wm = cut(512)
        ox = cut(256)
        pr = cut(256)
        pT = cut(256)
        osq = cut(512)
        o_sb = cut(512)
        ogT = cut(512)
        sg = cut(1024).rearrange("p (b n) -> p b n", b=2)
        small = sb("small", [P, 6, GH])
        f_th = cut(KI * P).rearrange("p (k t) -> p k t", k=KI)
        assert used[0] <= ARENA

        x_all = wo[:, :, :].rearrange("p h n -> p (h n)").rearrange("p (t n) -> p t n", t=TILES)
        xn_all = wv[:, :, :].rearrange("p k n -> p (k n)").rearrange("p (t n) -> p t n", t=TILES)
        xnT_all = wg[:, :, :]
        ug = arena[:, 0:4096].rearrange("p (k n) -> p k n", k=KD)
        ys = arena[:, 4096:8192].rearrange("p (k n) -> p k n", k=KD)
        bu = arena[:, 8192:10240].rearrange("p (s n) -> p s n", s=2)
        gate_wT = arena[:, 10240:10752].rearrange("p (k n) -> p k n", k=KD)
        lr_u = o_fin[:, 246:254].rearrange("p (k n) -> p k n", k=KD)
        lr_v = arena[0:4, 10752:11008]
        ones_m = o_fin[:, 0:P]
        stat1 = o_fin[:, P:P + 6 * TILES].rearrange("p (t n) -> p t n", t=TILES)
        col_t = o_fin[:, 224:232].rearrange("p (s k) -> p s k", k=KD)
        u_sum = o_fin[:, 232:236].rearrange("p (k n) -> p k n", k=KD)
        d_eff = o_fin[:, 236:240].rearrange("p (k n) -> p k n", k=KD)
        aa = o_fin[:, 240:242]
        r42 = o_fin[0:4, 242:244]
        half_norm = o_fin[:, 244:245]
        idx_i = w_lut[:, :].bitcast(I32)
        idx_b = [wk[:, 0, 0:LUT_AT[2] // 2].bitcast(BF16)[:, 0:LUT_AT[1]],
                 wk[:, 0, 0:LUT_AT[2] // 2].bitcast(BF16)[:, LUT_AT[1]:LUT_AT[2]],
                 arena[:, 4096:4096 + KI * D // 2].bitcast(BF16)]
        hot = arena[:, ARENA - KI * D:ARENA].bitcast(BF16).rearrange("p (s n) -> p s n", s=2)
        diag = [x.bitcast(BF16).rearrange("p (k n) -> p k n", k=LUT)
                for x in (s_qk[:, :], s_v[:, :, :].rearrange("p h n -> p (h n)"), csum[:, :])]
        lut = rope_now[:, 0:48].rearrange("p (s k) -> p s k", s=3)
        lut_b = rope_now[:, 48:72].bitcast(BF16).rearrange("p (s k) -> p s k", s=3)
        syn_raw = zbuf[:, :, :].rearrange("p a n -> p (a n)").rearrange("p (k n) -> p k n", k=KD)
        tern_tmp = arena[:, 4096:6144]

        xy_dram = nc.dram_tensor("xy_scratch", (TILES * P, D), F32, kind="Internal").ap()

        ld_x = [sem(f"ld_x{n}") for n in range(4)]
        ld_misc = sem("ld_misc")
        ld_gate = sem("ld_gate")
        ld_syn = sem("ld_syn")
        ld_qk = sem("ld_qk")
        ld_v = sem("ld_v")
        ld_g = sem("ld_g")
        ld_o = sem("ld_o")
        ld_lut = sem("ld_lut")
        st_xy = sem("st_xy")
        v_stat = sem("v_stat")
        g_rstd = sem("g_rstd")
        v_xn = sem("v_xn")
        t_xn = sem("t_xn")
        c_xn = sem("c_xn")
        t_gate = sem("t_gate")
        c_gate = sem("c_gate")
        v_ug = sem("v_ug")
        t_lr = sem("t_lr")
        c_lr = sem("c_lr")
        v_scan = sem("v_scan")
        c_wo = sem("c_wo")
        ld_ident = sem("ld_ident")
        v_idx = sem("v_idx")
        v_deff = sem("v_deff")
        t_y = sem("t_y")
        v_xy = sem("v_xy")
        v_tern = sem("v_tern")
        t_tern = sem("t_tern")
        c_aa = sem("c_aa")
        v_const = sem("v_const")
        spare = sem("spare")
        v_lut = sem("v_lut")
        v_hot = sem("v_hot")
        t_hot = sem("t_hot")
        c_lut = sem("c_lut")

        l_x = sem("l_x")
        l_xy = sem("l_xy")
        z_xn = sem("z_xn")
        z_t = sem("z_t")
        z_c = sem("z_c")
        z_part = sem("z_part")
        z_xnb = sem("z_xnb")
        z_mm = sem("z_mm")
        z_sb = sem("z_sb")
        z_top = sem("z_top")
        z_hid = sem("z_hid")
        z_hT = sem("z_hT")
        z_hc = sem("z_hc")
        z_out = sem("z_out")
        z_v = sem("z_v")
        z_g = sem("z_g")
        z_x2t = sem("z_x2t")
        z_x2 = sem("z_x2")
        rope_ld = sem("rope_ld")
        reset_qk = sem("reset_qk")
        reset_v = sem("reset_v")
        p_down = sem("p_down")
        p_s1 = sem("p_s1")
        c_s1 = sem("c_s1")
        p_qk = sem("p_qk")
        v_rope = sem("v_rope")
        g_rope = sem("g_rope")
        p_v = sem("p_v")
        c_v = sem("c_v")
        p_s = sem("p_s")
        v_sc = sem("v_sc")
        c_es = sem("c_es")
        p_g = sem("p_g")
        c_th = sem("c_th")
        v_sg = sem("v_sg")
        p_qkT = sem("p_qkT")
        c_qkT = sem("c_qkT")
        p_cs = sem("p_cs")
        c_cs = sem("c_cs")
        v_enz = sem("v_enz")
        p_esT = sem("p_esT")
        c_esT = sem("c_esT")
        p_a = sem("p_a")
        v_a = sem("v_a")
        p_ok = sem("p_ok")
        p_su = sem("p_su")
        v_su = sem("v_su")
        v_soft = sem("v_soft")
        c_soft = sem("c_soft")
        p_pT = sem("p_pT")
        c_pT = sem("c_pT")
        p_w2 = sem("p_w2")
        v_w2 = sem("v_w2")
        p_o = sem("p_o")
        c_o = sem("c_o")
        v_oss = sem("v_oss")
        g_r = sem("g_r")
        v_og4 = sem("v_og4")
        v_og = sem("v_og")
        p_ogT = sem("p_ogT")
        c_ogT = sem("c_ogT")
        p_s2 = sem("p_s2")
        v_s2 = sem("v_s2")
        p_wo = sem("p_wo")
        v_fin = sem("v_fin")
        p_gate = sem("p_gate")
        p_up = sem("p_up")
        c_fth = sem("c_fth")
        v_f = sem("v_f")
        st_out = sem("st_out")

        block = ctx.enter_context(nc.Block())

        def apart(eng):
            eng.sem_inc(spare, 1)

        def tiles(eng, step):
            for g in range(GROUPS):
                step(0, g)
            with eng.Fori(1, TILES - 2) as i:
                for g in range(GROUPS):
                    step(i, g)
            for i in (TILES - 2, TILES - 1):
                for g in range(GROUPS):
                    step(i, g)
            step(TILES, 0)
            step(TILES, 1)

        def has_before(i):
            return not isinstance(i, int) or i > 0

        def parts(i, g):
            if not isinstance(i, int):
                return (True,) * 6
            n, end = GROUPS * i + g, GROUPS * TILES
            return 0 <= n < end, n + 1 < end, 0 < n <= end, 1 < n <= end + 1, i + 1 < TILES, i + 2 < TILES

        @block.sync
        def _(sp):
            x_t = a["u"].rearrange("(t p) d -> p t d", p=P)
            for n in range(4):
                sp.dma_start(x_all[:, 4 * n:4 * n + 4, :], x_t[:, 4 * n:4 * n + 4, :]).then_inc(ld_x[n], 16)
            sp.dma_start(ident[:], a["ident"]).then_inc(ld_ident, 16)
            sp.dma_start(lut[:, 0, :], a["lut"].to_broadcast([P, LUT])).then_inc(ld_ident, 16)
            sp.dma_start(syn_raw, a["w_synT"].rearrange("(k p) n -> p k n", p=P)).then_inc(ld_syn, 16)
            sp.dma_start(t_out[:], a["w_outT"].rearrange("(k p) n -> p k n", p=P)).then_inc(ld_syn, 16)
            sp.dma_start(gate_wT, a["gate_wT"].rearrange("(k p) n -> p k n", p=P)).then_inc(ld_gate, 16)
            sp.dma_start(cols[:, 0:5, :], a["cols"]).then_inc(ld_gate, 16)
            sp.dma_start(lr_u, a["lr_u"].rearrange("(k p) n -> p k n", p=P)).then_inc(ld_gate, 16)
            sp.dma_start(lr_v, a["lr_v"]).then_inc(ld_gate, 16)
            for n, name in enumerate(("gate_idx", "up_idx")):
                sp.dma_start(idx_i[:, LUT_AT[n]:LUT_AT[n + 1]].rearrange("p (k n) -> p k n", k=KD),
                             a[name].rearrange("(k p) n -> p k n", p=P)).then_inc(ld_lut, 16)
            whole = (KI - 1) * D
            sp.dma_start(idx_i[:, LUT_AT[2]:LUT_AT[2] + whole].rearrange("p (k n) -> p k n", n=D),
                         a["down_idx"][0:(KI - 1) * P, :].rearrange("(k p) n -> p k n", p=P)).then_inc(ld_lut, 16)
            sp.wait_ge(v_idx, 1)
            sp.dma_start(idx_i[0:LAST, LUT_AT[2] + whole:LUT_END], a["down_idx"][(KI - 1) * P:INTER, :]).then_inc(ld_lut, 16)

            def load_x(j):
                reached(sp, z_xn, j, 1, 0)
                sp.dma_start(x_in[:], a["u"][bass.ds(j * P, P), :]).then_inc(l_x, 16)

            def load_xy(j):
                reached(sp, z_g, j, GZ, -2)
                sp.dma_start(xy_in[:], xy_dram[bass.ds(j * P, P), :]).then_inc(l_xy, 16)

            load_x(0)
            for dst, src in (
                (b_syn[:], a["b_syn"].to_broadcast([P, NSYN])),
                (rows[:, 0, :], a["b_out"].to_broadcast([P, D])), (rows[:, 1, :], a["gamma"].to_broadcast([P, D])),
                (rows[:, 2, :], a["beta"].to_broadcast([P, D])), (gnorm[:], a["gnorm"]),
                (tri[:], a["tri"]), (last_row[:], a["last_row"]),
                (rope_tab[:], a["rope"].rearrange("(t p) n -> p t n", p=P)),
                (ws1[:], a["ws1T"].rearrange("(k p) n -> p k n", p=P)),
                (ws2[0:16, :], a["ws2T"]), (ws2[16:17, :], a["bs2"]),
            ):
                sp.dma_start(dst, src).then_inc(ld_misc, 16)
            wk_t = a["wkT"].rearrange("(k p) n -> p k n", p=P)
            sp.dma_start(wq[:], a["wqT"].rearrange("(k p) n -> p k n", p=P)).then_inc(ld_qk, 16)
            sp.dma_start(wk[:, 1, :], wk_t[:, 1, :]).then_inc(ld_qk, 16)
            sp.wait_ge(t_xn, 8)
            sp.dma_start(wv[:], a["wvT"].rearrange("(k p) n -> p k n", p=P)).then_inc(ld_v, 16)
            sp.wait_ge(t_gate, 8)
            sp.wait_ge(v_ug, 4)
            sp.dma_start(wg[:], a["wgT"].rearrange("(k p) n -> p k n", p=P)).then_inc(ld_g, 16)
            xy_t = xy_dram.rearrange("(t p) d -> p t d", p=P)
            for n in range(4):
                sp.wait_ge(v_xy, 2 * n + 2)
                sp.dma_start(xy_t[:, 4 * n:4 * n + 4, :], x_all[:, 4 * n:4 * n + 4, :]).then_inc(st_xy, 16)
            sp.wait_ge(st_xy, 64)
            sp.dma_start(wo[:], a["woT"].rearrange("(h p) n -> p h n", p=P)).then_inc(ld_o, 16)
            def step(i, g):
                now, nxt, prv, prv2, tile1, tile2 = parts(i, g)
                if g == 0 and tile2:
                    load_x(i + 2)
                if g == 1 and has_before(i):
                    reached(sp, v_fin, i, 1, 0)
                    sp.dma_start(out[bass.ds((i - 1) * P, P), :], o_fin[:]).then_inc(st_out, 16)
                if g == 2 and tile2:
                    load_xy(i + 2)

            load_xy(0)
            load_x(1)
            sp.wait_ge(v_hot, 2 * LUT)
            sp.dma_start(wk[:, 0, :], wk_t[:, 0, :]).then_inc(ld_qk, 16)
            load_xy(1)
            tiles(sp, step)
            sp.wait_ge(st_out, 16 * TILES)

        @block.tensor
        def _(pe):
            def mm(o, lhsT, rhs, start, stop):
                return pe.matmul(o, lhsT, rhs, start=start, stop=stop)

            def l0_xnT(j):
                reached(pe, z_xn, j, 1, 1)
                for k in range(KD):
                    ins = pe.transpose(bank[:, 5, k * P:(k + 1) * P], xn[:, k * P:(k + 1) * P], ident[:])
                ins.then_inc(z_t, 1)

            def l0_z(j):
                reached(pe, z_part, j, 5, 5)
                for c in range(2):
                    if c == 1:
                        reached(pe, z_hc, j, 1, 0)
                    n = 0
                    for s in range(3):
                        for k in range(KD):
                            ins = mm(bank[:, Z_BANKS[c], :], x_part[:, s, k * P:(k + 1) * P], t_syn[:, k, c * 512:(c + 1) * 512], n == 0, n == 5)
                            n += 1
                    ins.then_inc(z_mm, 1)

            def l0_hT(j):
                reached(pe, z_hid, j, 1, 1)
                for n in range(KN):
                    ins = pe.transpose(bank[:, 5 + n // 4, (n % 4) * P:(n % 4 + 1) * P], zw[:, n * P:(n + 1) * P], ident[:])
                ins.then_inc(z_hT, 1)

            def l0_out(j):
                reached(pe, z_hc, j, 1, 1)
                for n in range(KN):
                    ins = mm(bank[:, 3, 0:D], hT[:, n, :], t_out[:, n, :], n == 0, n == KN - 1)
                ins.then_inc(z_out, 1)

            def l0_xT(j):
                reached(pe, z_v, j, VZ, VZ)
                for k in range(KD):
                    ins = pe.transpose(bank[:, 3, k * P:(k + 1) * P], norm[:, k * P:(k + 1) * P], ident[:])
                ins.then_inc(z_x2t, 1)

            pe.wait_ge(ld_ident, 32)
            for n in range(8):
                k, q = n // 4, n % 4
                for t in range(4):
                    pe.wait_ge(v_xn, 4 * q + t + 1)
                    ins = pe.transpose(bank[:, n, t * P:(t + 1) * P], xn_all[:, 4 * q + t, k * P:(k + 1) * P], ident[:])
                ins.then_inc(t_xn, 1)
            pe.wait_ge(c_xn, 8)
            pe.wait_ge(v_const, 2)
            pe.wait_ge(v_tern, 2)
            mm(bank[:, 7, 0:2], ones_m, scales[:, 0:2], True, True).then_inc(t_tern, 1)
            pe.wait_ge(ld_gate, 64)
            for n in range(8):
                e, c = n // 4, n % 4
                if n == 7:
                    pe.wait_ge(v_tern, 3)
                for k in range(KD):
                    ins = mm(bank[:, n, :], gate_wT[:, k, e * P:(e + 1) * P], xnT_all[:, k, c * 512:(c + 1) * 512], k == 0, k == KD - 1)
                ins.then_inc(t_gate, 1)

            def table(*steps):
                for m in steps:
                    n, k = m // LUT, m % LUT
                    w = LUT_PARTS[n][1]
                    first = 0 if n % 2 == 0 else 3
                    if m == 0:
                        pe.wait_ge(v_lut, 8)
                        pe.wait_ge(c_gate, 3)
                    if m == 2 * LUT:
                        pe.wait_ge(c_lut, 3)
                    pe.wait_ge(v_hot, m + 1)
                    for s in range(3):
                        for c in range(3):
                            lo, hi = c * 512, min(w, (c + 1) * 512)
                            ins = mm(bank[:, first + c, 0:hi - lo], diag[s][:, k, :], hot[:, k % 2, lo:hi],
                                     k == 0 and s == 0, k == LUT - 1 and s == 2)
                    ins.then_inc(t_hot, 1)

            def y_back(*pairs):
                for n in pairs:
                    if n > 1:
                        pe.wait_ge(v_xy, n - 1)
                    for t in range(2):
                        tile = 2 * n + t
                        for k in range(KD):
                            pe.wait_ge(v_scan, Y_STEPS * (2 * (tile // SEQ_TILES) + k + 1))
                            ins = pe.transpose(bank[:, 6 + n % 2, t * D + k * P:t * D + (k + 1) * P], ys[:, k, tile * P:(tile + 1) * P], ident[:])
                    ins.then_inc(t_y, 1)

            table(0, 1, 2, 3)
            pe.wait_ge(v_ug, 5)
            pe.wait_ge(c_gate, 8)
            for k in range(KD):
                ins = mm(bank[0:4, 3, 0:NB], lr_u[:, k, :], u_sum[:, k, :], k == 0, k == KD - 1)
            ins.then_inc(t_lr, 1)
            pe.wait_ge(c_lr, 1)
            for k in range(KD):
                ins = mm(bank[:, 4, k * NB:(k + 1) * NB], lr_v[:, k * P:(k + 1) * P], r42, True, True)
            ins.then_inc(t_lr, 1)
            l0_xnT(0)
            table(4, 5, 6, 7, 8)
            l0_z(0)
            table(9, 10)
            reached(pe, z_sb, 0, 2, 2)
            y_back(0, 1, 2, 3)
            table(*range(11, LUT))
            y_back(4, 5, 6, 7)
            pe.wait_ge(v_deff, 1)
            pe.wait_ge(z_c, 1)
            table(*range(LUT, LUT + TOP0_AT))
            pe.wait_ge(c_lut, 6)
            l0_hT(0)
            table(LUT + TOP0_AT)
            l0_out(0)
            table(*range(LUT + TOP0_AT + 1, 3 * LUT))
            l0_xT(0)
            pe.wait_ge(z_hc, 1)
            l0_xnT(1)
            l0_z(1)
            pe.wait_ge(c_lut, 9)
            pe.wait_ge(ld_misc, 16 * MISC)
            pe.wait_ge(ld_qk, 48)
            pe.wait_ge(ld_v, 16)
            pe.wait_ge(ld_g, 16)
            pe.wait_ge(c_wo, 1)

            def project(o, w, g):
                for k in range(KD):
                    ins = mm(o, xT[:, k, :], w[:, k, g * 512:(g + 1) * 512], k == 0, k == KD - 1)
                return ins

            def step(i, g):
                now, nxt, prv, prv2, tile1, tile2 = parts(i, g)
                n1, p1, p2 = (g + 1) % GROUPS, (g - 1) % GROUPS, (g - 2) % GROUPS
                if now:
                    unit(pe, g_rope, i, g, 2, 2)
                    for h in range(2 * GH):
                        ins = pe.transpose(bank[:, h // GH, (h % GH) * P:(h % GH + 1) * P], qk[:, h * P:(h + 1) * P], ident[:])
                    ins.then_inc(p_qkT, 1)
                    unit(pe, c_es, i, g)
                    if g == 0:
                        reached(pe, reset_qk, i, 2, 2)
                    if g == 2 and tile1:
                        reached(pe, z_v, i + 1, VZ, 1)
                    mm(bank[:, 3, 0:256], tri[:], es[:, g % 2, :], True, False)
                    mm(bank[:, 3, 0:256], last_row[:], csum[:, g * 256:(g + 1) * 256], False, True).then_inc(p_cs, 1)
                if prv:
                    unit(pe, v_soft, i, g - 1, N_SOFT, N_SOFT)
                    unit(pe, v_s2, i, g - 2)
                    if g == 1 and tile2:
                        reached(pe, z_c, i + 2, 1, 1)
                    for h in range(2):
                        ins = pe.transpose(bank[:, 5, h * P:(h + 1) * P], pr[:, h * P:(h + 1) * P], ident[:])
                    ins.then_inc(p_pT, 1)
                if prv2:
                    unit(pe, v_og, i, g - 2)
                    if g == 2 and tile2:
                        reached(pe, z_sb, i + 2, 2, 2)
                    for h in range(GH):
                        ins = pe.transpose(bank[:, 6, h * P:(h + 1) * P], o_sb[:, o_slot(h) * P:(o_slot(h) + 1) * P], ident[:])
                    ins.then_inc(p_ogT, 1)
                if now:
                    unit(pe, c_cs, i, g)
                    for h in range(2):
                        ins = pe.transpose(bank[:, 3, h * P:(h + 1) * P], es[:, g % 2, h * P:(h + 1) * P], ident[:])
                    ins.then_inc(p_esT, 1)
                    unit(pe, c_qkT, i, g, 2, 2)
                if g == 0 and has_before(i):
                    reached(pe, v_f, i, V_F, 0)
                    for c in range(KI):
                        r = P if c < KI - 1 else LAST
                        ins = mm(bank[:, 2, 0:D], f_th[0:r, c, :], w_down[0:r, c, :], False, False)
                    ins.then_inc(p_down, 1)
                if g == 0 and now:
                    ffn(w_gate, 0, p_gate)
                if g == 3 and now:
                    ffn(w_up, 0, p_up)
                if now:
                    unit(pe, v_sg, i, g)
                    for h in range(GH):
                        ins = mm(bank[:, 4, h * P:(h + 1) * P], qkT[:, 512 + h * P:512 + (h + 1) * P], qkT[:, h * P:(h + 1) * P], True, True)
                    ins.then_inc(p_a, 1)
                if g == 3 and tile1:
                    unit(pe, c_esT, i, g)
                    l0_xT(i + 1)
                if prv2:
                    unit(pe, c_ogT, i, g - 2)
                    if p2 == 0:
                        reached(pe, v_fin, i, 1, 0)
                    for h in range(GH):
                        ins = mm(bank[:, 2, 0:D], ogT[:, h * P:(h + 1) * P], wo[:, GH * p2 + h, :],
                                 p2 == 0 and h == 0, p2 == GROUPS - 1 and h == GH - 1)
                    ins.then_inc(p_wo, 1)
                if prv:
                    unit(pe, c_pT, i, g - 1)
                    unit(pe, c_ogT, i, g - 2)
                    for h in range(GH):
                        lo, q = (h % 2) * M, h // 2
                        ins = mm(bank[:, 6 - h % 2, q * P:(q + 1) * P], esT[lo:lo + M, p1 % 2, q * P:(q + 1) * P], pT[lo:lo + M, q * P:(q + 1) * P], True, True)
                    ins.then_inc(p_w2, 1)
                if (g == 3 and tile1) or g == -1:
                    reached(pe, z_x2, i + 1 if g == 3 else i, 1, 1)
                    for k in range(KD):
                        ins = mm(bank[0:16, 3, 0:P], ws1[:, k, :], xT[:, k, :], k == 0, k == KD - 1)
                    ins.then_inc(p_s1, 1)
                if nxt:
                    if g == 0:
                        reached(pe, v_f, i, V_F, V_F // 2)
                    if g == 3:
                        reached(pe, v_f, i, V_F, V_F)
                    project(bank[:, 0, :], wq, n1)
                    project(bank[:, 1, :], wk, n1).then_inc(p_qk, 1)
                if now:
                    unit(pe, v_a, i, g)
                    unit(pe, v_su, i, g - GROUPS)
                    for h in range(GH):
                        s = (GH * g + h) * M
                        mm(bank[:, 4, h * M:(h + 1) * M], am[:, h * P:(h + 1) * P], es[:, g % 2, h * M:(h + 1) * M], True, False)
                        ins = mm(bank[:, 4, h * M:(h + 1) * M], qkT[:, h * P:(h + 1) * P], s_qk[:, s:s + M], False, True)
                    ins.then_inc(p_ok, 1)
                    unit(pe, v_w2, i, g - 1)
                    for h in range(GH):
                        ins = mm(bank[:, 5, h * M:(h + 1) * M], qk[:, 512 + h * P:512 + (h + 1) * P], es[:, g % 2, h * M:(h + 1) * M], True, True)
                    ins.then_inc(p_su, 1)
                if prv:
                    unit(pe, v_w2, i, g - 1)
                    unit(pe, v_s2, i, g - 1 - GROUPS)
                    if g == 1:
                        reached(pe, reset_v, i, 1, 1)
                    if now:
                        unit(pe, c_v, i, g)
                    else:
                        unit(pe, c_v, i, g - 1)
                    for h in range(GH):
                        lo, q, w = (h % 2) * M, h // 2, slot(h) * P
                        o = bank[:, 6 + h % 2, q * P:(q + 1) * P]
                        mm(o, wm[:, w:w + P], v_sb[:, p1 % 2, h * P:(h + 1) * P], True, False)
                        ins = mm(o, pT[lo:lo + M, q * P:(q + 1) * P], s_v[lo:lo + M, 2 * p1 + q, :], False, True)
                    ins.then_inc(p_o, 1)
                if nxt:
                    if g == 3:
                        reached(pe, c_s1, i + 1, 1, 1)
                    elif g == -1:
                        reached(pe, c_s1, i, 1, 1)
                    else:
                        unit(pe, c_esT, i, g)
                    mm(bank[:, 3, 0:256], s16[:], ws2[:, n1 * 256:(n1 + 1) * 256], True, True).then_inc(p_s, 1)
                if prv:
                    if now:
                        unit(pe, v_su, i, g)
                    for h in range(GH):
                        lo, q = (h % 2) * M, h // 2
                        ins = mm(bank[lo:lo + M, 5, q * P:(q + 1) * P], es[:, p1 % 2, h * M:(h + 1) * M], v_sb[:, p1 % 2, h * P:(h + 1) * P], True, True)
                    ins.then_inc(p_s2, 1)
                if nxt:
                    if now:
                        unit(pe, v_soft, i, g, 1, N_SOFT)
                    project(bank[:, 4, :], wg, n1).then_inc(p_g, 1)
                    if prv:
                        unit(pe, c_o, i, g - 1, 2, 2)
                    if g == -1:
                        reached(pe, z_sb, 1, 2, 2)
                    project(bank[:, 7, :], wv, n1).then_inc(p_v, 1)
                if g == 0 and tile2:
                    if prv:
                        unit(pe, v_s2, i, g - 1)
                    else:
                        unit(pe, v_su, i, g)
                    l0_xnT(i + 2)
                if g == 1:
                    if tile1:
                        unit(pe, c_o, i, g - 1, 2, 2)
                        unit(pe, v_s2, i, g - 1)
                        l0_hT(i + 1)
                    if tile2:
                        unit(pe, c_v, i, g + 1)
                        l0_z(i + 2)
                    if tile1:
                        unit(pe, v_sc, i, g + 1)
                        l0_out(i + 1)

            def ffn(w, first, done):
                for c in range(KI):
                    r = P if c < KI - 1 else LAST
                    for k in range(KD):
                        ins = mm(bank[0:r, first + c // 3, (c % 3) * P:(c % 3 + 1) * P], w[:, k, c * P:c * P + r], xT[:, k, :], k == 0, k == KD - 1)
                ins.then_inc(done, 1)

            step(0, -1)
            tiles(pe, step)

        @block.scalar
        def _(act):
            def copy(o, i_, scale=1.0):
                return act.activation(o, i_, ACT.Copy, scale=scale)

            for n in range(8):
                act.wait_ge(t_xn, n + 1)
                copy(xnT_all[:, n // 4, (n % 4) * 512:(n % 4 + 1) * 512], bank[:, n, :]).then_inc(c_xn, 1)
            act.wait_ge(ld_gate, 64)
            act.activation(aa, cols[:, 0, :], ACT.Tanh).then_inc(c_aa, 1)
            for n in range(8):
                e = n // 4
                act.wait_ge(t_gate, n + 1)
                act.activation(ug[:, e, (n % 4) * 512:(n % 4 + 1) * 512], bank[:, n, :], ACT.Sigmoid,
                               bias=cols[:, 4, e:e + 1]).then_inc(c_gate, 1)
            act.wait_ge(t_lr, 1)
            copy(r42, bank[0:4, 3, 0:NB]).then_inc(c_lr, 1)

            def l0_xnT(j):
                reached(act, z_t, j, 1, 1)
                reached(act, z_part, j, 5, 0)
                copy(xnT[:], bank[:, 5, 0:D]).then_inc(z_c, 1)

            def l0_hT(j):
                reached(act, z_hT, j, 1, 1)
                copy(hT, bank[:, 5:7, :]).then_inc(z_hc, 1)

            def l0_xT(j):
                reached(act, z_x2t, j, 1, 1)
                reached(act, p_up, j, 1, 0)
                copy(xT[:], bank[:, 3, 0:D]).then_inc(z_x2, 1)

            def table(n):
                at, w = LUT_PARTS[n]
                act.wait_ge(t_hot, LUT * (n + 1))
                for c in range(3):
                    lo, hi = c * 512, min(w, (c + 1) * 512)
                    copy(w_lut[:, at + lo:at + hi], bank[:, (0 if n % 2 == 0 else 3) + c, 0:hi - lo], 0.5 if n == 2 else 1.0).then_inc(c_lut, 1)

            l0_xnT(0)
            table(0)
            act.wait_ge(ld_o, 16)
            act.wait_ge(v_idx, 4)
            wo_flat = wo[:, :, :].rearrange("p h n -> p (h n)")
            act.activation(wo_flat, wo_flat, ACT.Copy, scale=half_norm).then_inc(c_wo, 1)
            table(1)
            l0_hT(0)
            table(2)
            l0_xT(0)
            l0_xnT(1)

            def step(i, g):
                now, nxt, prv, prv2, tile1, tile2 = parts(i, g)
                p1 = (g - 1) % GROUPS
                if now:
                    unit(act, p_qkT, i, g)
                    unit(act, p_ok, i, g - 1)
                    copy(qkT[:, 0:512], bank[:, 0, :]).then_inc(c_qkT, 1)
                    unit(act, p_cs, i, g)
                    copy(csum[:, g * 256:(g + 1) * 256], bank[:, 3, 0:256]).then_inc(c_cs, 1)
                    copy(qkT[:, 512:1024], bank[:, 1, :]).then_inc(c_qkT, 1)
                if prv:
                    unit(act, p_pT, i, g - 1)
                    unit(act, p_o, i, g - 2)
                    copy(pT, bank[:, 5, 0:256]).then_inc(c_pT, 1)
                if prv2:
                    unit(act, p_ogT, i, g - 2)
                    unit(act, p_wo, i, g - 3)
                    copy(ogT, bank[:, 6, :]).then_inc(c_ogT, 1)
                if now:
                    unit(act, p_esT, i, g)
                    unit(act, p_w2, i, g - 2)
                    copy(esT[:, g % 2, :], bank[:, 3, 0:256]).then_inc(c_esT, 1)
                if g == 0 and now:
                    reached(act, p_gate, i, 1, 1)
                    reached(act, p_down, i, 1, 0)
                    for r, b, lo, w, k0 in F_PARTS:
                        act.activation(f_th[0:r, k0:k0 + w // P, :].rearrange("p k t -> p (k t)"), bank[0:r, b, lo:lo + w],
                                       ACT.Tanh, scale=0.5).then_inc(c_fth, 1)
                if g == 3 and tile1:
                    l0_xT(i + 1)
                if (g == 3 and tile1) or g == -1:
                    reached(act, p_s1, i + 1 if g == 3 else i, 1, 1)
                    unit(act, p_s, i, g)
                    copy(s16[0:16, :], bank[0:16, 3, 0:P]).then_inc(c_s1, 1)
                if now:
                    unit(act, v_soft, i, g, 3, N_SOFT)
                    act.activation(ox, ox, ACT.Exp).then_inc(c_soft, 1)
                if prv:
                    unit(act, p_o, i, g - 1)
                    unit(act, v_oss, i, g - 2)
                    unit(act, p_ogT, i, g - 2)
                    act.activation(osq, bank[:, 6:8, 0:256], ACT.Square).then_inc(c_o, 1)
                    copy(o_sb, bank[:, 6:8, 0:256]).then_inc(c_o, 1)
                if nxt:
                    unit(act, v_sc, i, g + 1)
                    act.activation(es[:, (g + 1) % 2, :], es[:, (g + 1) % 2, :], ACT.Exp).then_inc(c_es, 1)
                    unit(act, p_v, i, g + 1)
                    unit(act, p_s2, i, g - 1)
                    copy(v_sb[:, (g + 1) % 2, :], bank[:, 7, :]).then_inc(c_v, 1)
                if g == 1 and tile1:
                    l0_hT(i + 1)
                if nxt:
                    unit(act, p_g, i, g + 1)
                    unit(act, v_og, i, g - 1)
                    act.activation(sg[:, (g + 1) % 2, :], bank[:, 4, :], ACT.Tanh, scale=0.5).then_inc(c_th, 1)
                if g == 0 and tile2:
                    l0_xnT(i + 2)

            step(0, -1)
            tiles(act, step)

        @block.vector
        def _(dve):
            tt, ts, stt = dve.tensor_tensor, dve.tensor_scalar, dve.scalar_tensor_tensor
            def l0_xn(j):
                reached(dve, l_x, j, 16, 16)
                reached(dve, z_t, j, 1, 0)
                reached(dve, z_xnb, j, 1, 0)
                ts(xn[:], x_in[:], mean1[:, bass.ds(j, 1), 0:1].rearrange("p a b -> p (a b)"), rstd1[:, bass.ds(j, 1)], ALU.subtract, ALU.mult).then_inc(z_xn, 1)

            def l0_zsb(j):
                reached(dve, z_hid, j, 1, 0)
                for c in range(2):
                    reached(dve, z_mm, j, 2, c + 1)
                    stt(z[:, c * 512:(c + 1) * 512], bank[:, Z_BANKS[c], :], scales[:, 2:3], b_syn[:, c * 512:(c + 1) * 512], ALU.mult, ALU.add).then_inc(z_sb, 1)

            def l0_top(j, steps):
                for n in steps:
                    r, strike = n // 2, n % 2
                    if n == 0:
                        reached(dve, z_sb, j, 2, 2)
                    else:
                        reached(dve, z_top, j, N_TOP, n)
                    src = z if r == 0 else zw
                    if strike:
                        if n == 1:
                            reached(dve, z_hT, j, 1, 0)
                        apart(dve)
                        dve.match_replace(out=zw, in_to_replace=top8[:, r % 2, :], in_values=src, imm_value=LOW).then_inc(z_top, 1)
                    else:
                        apart(dve)
                        dve.max(out=top8[:, r % 2, :], in_=src).then_inc(z_top, 1)

            def l0_hidden(j):
                reached(dve, z_top, j, N_TOP, N_TOP - 1)
                k = TOPK - 8 * (ROUNDS - 1) - 1
                ts(thr[:], top8[:, (ROUNDS - 1) % 2, k:k + 1], 0.0, None, ALU.max).then_inc(z_top, 1)
                reached(dve, z_top, j, N_TOP, N_TOP)
                stt(zw, z, thr[:, 0:1], z, ALU.is_ge, ALU.mult).then_inc(z_hid, 1)

            def l0_norm(j, part):
                par = j % 2
                if part == 0:
                    reached(dve, z_out, j, 1, 1)
                    reached(dve, z_xnb, j, 1, 1)
                    reached(dve, z_x2t, j, 1, 0)
                    stt(norm[:], bank[:, 3, 0:D], scales[:, 3:4], xn_b[:], ALU.mult, ALU.add).then_inc(z_v, 1)
                    reached(dve, z_v, j, VZ, 1)
                    dve.bn_stats(stat[:, 0, :], norm[:]).then_inc(z_v, 1)
                    reached(dve, z_v, j, VZ, 2)
                    apart(dve)
                    dve.bn_aggr(mv[:, 0, :], stat[:, 0, :]).then_inc(z_v, 1)
                elif part == 1:
                    reached(dve, z_g, j, GZ, 2)
                    ts(norm[:], norm[:], mv[:, 0, 0:1], rs[:, 0, 1:2], ALU.subtract, ALU.mult).then_inc(z_v, 1)
                elif part == 2:
                    reached(dve, z_g, j, GZ, 5)
                    x = x1[:, bass.ds(par, 1), :].rearrange("p a d -> p (a d)")
                    apart(dve)
                    dve.bn_stats(stat[:, 1, :], x).then_inc(z_v, 1)
                    reached(dve, z_v, j, VZ, 5)
                    apart(dve)
                    dve.bn_aggr(mv[:, 1, :], stat[:, 1, :]).then_inc(z_v, 1)
                else:
                    reached(dve, z_g, j, GZ, 7)
                    x = x1[:, bass.ds(par, 1), :].rearrange("p a d -> p (a d)")
                    ts(norm[:], x, mv[:, 1, 0:1], rs[:, 1, 1:2], ALU.subtract, ALU.mult).then_inc(z_v, 1)

            dve.memset(half_neg[:], -0.5).then_inc(v_const, 1)
            dve.memset(ones_m, 1.0).then_inc(v_const, 1)
            dve.memset(s16[:], 1.0).then_inc(v_const, 1)
            dve.memset(idx_i[:, LUT_END - D:LUT_END], 0).then_inc(v_idx, 1)
            for t in range(TILES):
                dve.wait_ge(ld_x[t // 4], 16)
                dve.bn_stats(stat1[:, t, :], x_all[:, t, :]).then_inc(v_stat, 1)
            for t in range(TILES):
                dve.wait_ge(v_stat, t + 1)
                dve.bn_aggr(mean1[:, t, :], stat1[:, t, :]).then_inc(v_stat, 1)
            dve.wait_ge(ld_ident, 32)
            dve.tensor_copy(ident_b[:], ident[:]).then_inc(v_const, 1)
            dve.tensor_copy(lut_b[:, 0, :], lut[:, 0, :]).then_inc(v_lut, 1)
            for s in (1, 2):
                dve.wait_ge(v_lut, 2 * s - 1)
                tt(lut[:, s, :], lut[:, s - 1, :], lut_b[:, s - 1, :], ALU.subtract).then_inc(v_lut, 1)
                dve.wait_ge(v_lut, 2 * s)
                dve.tensor_copy(lut_b[:, s, :], lut[:, s, :]).then_inc(v_lut, 1)
            dve.wait_ge(g_rstd, 2)
            for t in range(TILES):
                ts(xn_all[:, t, :], x_all[:, t, :], mean1[:, t, 0:1], rstd1[:, t:t + 1], ALU.subtract, ALU.mult).then_inc(v_xn, 1)
            dve.wait_ge(ld_syn, 32)
            out_flat = t_out[:, :, :].rearrange("p k n -> p (k n)")
            syn_flat = zbuf[:, :, :].rearrange("p a n -> p (a n)")
            dve.tensor_reduce(scales[:, 0:1], syn_flat, AX.X, ALU.add, apply_absolute_value=True).then_inc(v_tern, 1)
            dve.tensor_reduce(scales[:, 1:2], out_flat, AX.X, ALU.add, apply_absolute_value=True).then_inc(v_tern, 1)
            dve.wait_ge(t_tern, 1)
            ts(scales[:, 2:4], bank[:, 7, 0:2], 1.0 / (NSYN * D), None, ALU.mult).then_inc(v_tern, 1)
            dve.wait_ge(v_tern, 3)
            ts(scales[:, 4:6], scales[:, 2:4], 1e-8, 0.5, ALU.add, ALU.mult).then_inc(v_tern, 1)
            dve.wait_ge(v_tern, 4)
            ts(scales[:, 6:8], scales[:, 4:6], -1.0, None, ALU.mult).then_inc(v_tern, 1)
            dve.wait_ge(v_tern, 5)
            ts(tern_tmp, syn_flat, scales[:, 6:7], None, ALU.is_lt).then_inc(v_tern, 1)
            dve.wait_ge(v_tern, 6)
            stt(t_syn[:, :, :].rearrange("p k n -> p (k n)"), syn_flat, scales[:, 4:5], tern_tmp, ALU.is_gt, ALU.subtract).then_inc(v_tern, 1)
            dve.wait_ge(v_tern, 7)
            ts(tern_tmp, out_flat, scales[:, 7:8], None, ALU.is_lt).then_inc(v_tern, 1)
            dve.wait_ge(v_tern, 8)
            stt(out_flat, out_flat, scales[:, 5:6], tern_tmp, ALU.is_gt, ALU.subtract).then_inc(v_tern, 1)
            dve.wait_ge(v_lut, 5)
            dve.wait_ge(v_const, 4)
            for s in range(3):
                tt(diag[s], ident_b[:, None, :].to_broadcast([P, LUT, P]), lut_b[:, s, :, None].to_broadcast([P, LUT, P]), ALU.mult).then_inc(v_lut, 1)
            dve.wait_ge(ld_lut, 64)
            for n in range(2):
                dve.tensor_copy(idx_b[n], idx_i[:, LUT_AT[n]:LUT_AT[n + 1]]).then_inc(v_idx, 1)

            def one_hot(*steps):
                for m in steps:
                    n, k = m // LUT, m % LUT
                    w = LUT_PARTS[n][1]
                    if m == 0:
                        dve.wait_ge(v_idx, 3)
                    if m == 2 * LUT:
                        dve.wait_ge(v_idx, 5)
                    if m >= 2:
                        dve.wait_ge(t_hot, m - 1)
                    ts(hot[:, k % 2, 0:w], idx_b[n], float(k), None, ALU.is_equal).then_inc(v_hot, 1)

            for n in range(4):
                e, s = n // NB, n % NB
                dve.wait_ge(c_gate, 2 * n + 2)
                r = ug[:, e, s * T:(s + 1) * T]
                tt(r, r, xnT_all[:, e, s * T:(s + 1) * T], ALU.mult).then_inc(v_ug, 1)
                if n % 2 == 1:
                    one_hot(n // 2)
            dve.wait_ge(v_ug, 4)
            dve.tensor_reduce(u_sum, ug.rearrange("p k (s t) -> p k s t", s=NB), AX.X, ALU.add).then_inc(v_ug, 1)
            one_hot(2)
            dve.wait_ge(c_aa, 1)
            ts(col_t[:, 0, :], aa, 1e-6, None, ALU.max).then_inc(v_ug, 1)
            dve.wait_ge(v_ug, 6)
            dve.reciprocal(col_t[:, 1, :], col_t[:, 0, :]).then_inc(v_ug, 1)
            dve.wait_ge(v_ug, 7)
            tt(col_t[:, 2, :], aa, col_t[:, 1, :], ALU.mult).then_inc(v_ug, 1)
            tt(col_t[:, 3, :], cols[:, 1, :], cols[:, 2, :], ALU.mult).then_inc(v_ug, 1)
            l0_xn(0)
            one_hot(3)
            dve.wait_ge(v_ug, 9)
            n = 0
            for s in range(NB):
                for e in range(KD):
                    m = 4 + 3 * (NB * s + e)
                    u_r, y_r, b_r = ug[:, e, s * T:(s + 1) * T], ys[:, e, s * T:(s + 1) * T], bu[:, e, :]
                    if s > 0:
                        dve.wait_ge(v_scan, n - 2 * Y_STEPS + 3)
                    ts(b_r, u_r, col_t[:, 3, e:e + 1], None, ALU.mult).then_inc(v_scan, 1)
                    dve.wait_ge(v_scan, n + 1)
                    ts(b_r[:, 0:1], b_r[:, 0:1], col_t[:, 2, e:e + 1], None, ALU.mult).then_inc(v_scan, 1)
                    one_hot(m)
                    dve.wait_ge(v_scan, n + 2)
                    dve.tensor_tensor_scan(y_r, aa[:, e:e + 1].to_broadcast([P, T]), b_r, 0.0, ALU.mult, ALU.add).then_inc(v_scan, 1)
                    one_hot(m + 1)
                    if n == 0:
                        dve.wait_ge(t_lr, 2)
                        stt(d_eff, bank[:, 4, 0:KD * NB].rearrange("p (k s) -> p k s", k=KD), 1.0 / (T * 4.0),
                            cols[:, 3, :, None].to_broadcast([P, KD, NB]), ALU.mult, ALU.add).then_inc(v_deff, 1)
                        dve.wait_ge(v_deff, 1)
                    dve.wait_ge(v_scan, n + 3)
                    stt(y_r, u_r, d_eff[:, e, s:s + 1], y_r, ALU.mult, ALU.add).then_inc(v_scan, 1)
                    one_hot(m + 2)
                    n += Y_STEPS
                    if s == 0 and e == 1:
                        dve.wait_ge(ld_misc, 16 * MISC)
                        l0_zsb(0)
                    if s == 1:
                        for q in range(4 * e, 4 * e + 4):
                            dve.wait_ge(t_y, q + 1)
                            r = x_all[:, 2 * q:2 * q + 2, :].rearrange("p t d -> p (t d)")
                            tt(r, r, bank[:, 6 + q % 2, :], ALU.add).then_inc(v_xy, 1)
            ts(half_norm, gnorm[:, 0:1], 0.5, None, ALU.mult).then_inc(v_idx, 1)
            dve.tensor_copy(idx_b[2], idx_i[:, LUT_AT[2]:LUT_END]).then_inc(v_idx, 1)
            for n in range(N_TOP - 1):
                one_hot(LUT + n)
                l0_top(0, [n])
            one_hot(*range(LUT + N_TOP - 1, LUT + TOP0_AT))
            l0_hidden(0)
            one_hot(LUT + TOP0_AT, LUT + TOP0_AT + 1)
            l0_norm(0, 0)
            one_hot(LUT + TOP0_AT + 2)
            l0_norm(0, 1)
            one_hot(LUT + TOP0_AT + 3)
            l0_norm(0, 2)
            assert TOP0_AT + 4 == 2 * LUT - 1
            one_hot(LUT + TOP0_AT + 4)
            l0_norm(0, 3)
            l0_xn(1)
            l0_zsb(1)
            l0_top(1, range(TOP_HEAD))

            def renew(i, states, done):
                def zero():
                    for x in states:
                        dve.memset(x, 0.0).then_inc(done, 1)
                if isinstance(i, int):
                    if i % SEQ_TILES == 0:
                        zero()
                    else:
                        dve.sem_inc(done, len(states))
                else:
                    apart(dve)
                    with dve.If(i == SEQ_TILES):
                        zero()
                    with dve.Else():
                        dve.sem_inc(done, len(states))

            def rope(i, g):
                unit(dve, p_qk, i, g)
                unit(dve, g_rope, i, g, 0, 2)
                v = bank[:, 0:2, :].rearrange("p b (h a m) -> p (b h) a m", a=2, m=64)
                cos = rope_now[:, None, None, 0:64].to_broadcast([P, 2 * GH, 2, 64])
                sin = rope_now[:, None, None, 64:128].to_broadcast([P, 2 * GH, 2, 64])
                tt(t1.rearrange("p (h a m) -> p h a m", a=2, m=64), v, cos, ALU.mult).then_inc(v_rope, 1)
                tt(t2.rearrange("p (h a m) -> p h a m", a=2, m=64), v[:, :, ::-1, :], sin, ALU.mult).then_inc(v_rope, 1)

            def heads(x, n):
                return x.rearrange("p (h m) -> p h m", h=GH)

            def over(x, n):
                return x[:, :, None].to_broadcast([P, GH, n])

            def step(i, g):
                now, nxt, prv, prv2, tile1, tile2 = parts(i, g)
                p1 = (g - 1) % GROUPS
                j, top = None, []
                if (g in (2, 3) and tile2) or (g in (0, 1) and tile1):
                    j, top = i + (2 if g in (2, 3) else 1), list(range(*TOP_OF[g]))

                def some(n):
                    l0_top(j, top[:n])
                    del top[:n]

                if g == -1:
                    renew(0, [s_qk[:], csum[:]], reset_qk)
                if g == 2 and tile1:
                    l0_norm(i + 1, 0)
                if g == 2 and tile2:
                    l0_zsb(i + 2)
                if g == 0 and tile2:
                    l0_xn(i + 2)
                if now:
                    unit(dve, c_cs, i, g)
                    unit(dve, v_soft, i, g - 1, N_SOFT, N_SOFT)
                    dve.reciprocal(enz, csum[:, g * 256:(g + 1) * 256]).then_inc(v_enz, 1)
                if g == 0 and now:
                    for n, (r, b, lo, w, k0) in enumerate(F_PARTS):
                        reached(dve, c_fth, i, 3, 3)
                        f = f_th[0:r, k0:k0 + w // P, :].rearrange("p k t -> p (k t)")
                        stt(f, f, 1.0, bank[0:r, b, lo:lo + w], ALU.add, ALU.mult).then_inc(v_f, 1)
                if g == 3 and now:
                    for n, (r, b, lo, w, k0) in enumerate(F_PARTS):
                        reached(dve, p_up, i, 1, 1)
                        reached(dve, v_f, i, V_F, 3)
                        f = f_th[0:r, k0:k0 + w // P, :].rearrange("p k t -> p (k t)")
                        tt(f, f, bank[0:r, b, lo:lo + w], ALU.mult).then_inc(v_f, 1)
                if now:
                    unit(dve, p_a, i, g)
                    unit(dve, p_ok, i, g - 1)
                    tt(heads(am, P), heads(bank[:, 4, :], P), tri[:, None, :].to_broadcast([P, GH, P]), ALU.mult).then_inc(v_a, 1)
                if prv:
                    unit(dve, p_w2, i, g - 1)
                    unit(dve, p_o, i, g - 2)
                    tt(wm.rearrange("p (b q t) -> p b q t", b=2, q=2), bank[:, 5:7, 0:256].rearrange("p b (q t) -> p b q t", q=2),
                       tri[:, None, None, :].to_broadcast([P, 2, 2, P]), ALU.mult).then_inc(v_w2, 1)
                if g == 1 and has_before(i):
                    reached(dve, p_wo, i, GROUPS, 0)
                    reached(dve, st_out, i - 1, 16, 0)
                    x = x1[:, bass.ds((i + 1) % 2, 1), :].rearrange("p a d -> p (a d)")
                    tt(o_fin[:], x, bank[:, 2, 0:D], ALU.add).then_inc(v_fin, 1)
                some(2)
                if nxt:
                    if g in (3, -1):
                        reached(dve, rope_ld, i + 1 if g == 3 else i, 1, 1)
                    rope(i, g + 1)
                if now:
                    unit(dve, p_su, i, g)
                    s = s_qk[:, g * 256:(g + 1) * 256]
                    tt(s, s, bank[:, 5, 0:256], ALU.add).then_inc(v_su, 1)
                    unit(dve, p_ok, i, g)
                    unit(dve, v_enz, i, g)
                    stt(ox, bank[:, 4, 0:256], QK_SCALE, enz, ALU.mult, ALU.mult).then_inc(v_soft, 1)
                    unit(dve, v_soft, i, g, 1, N_SOFT)
                    dve.tensor_reduce(small[:, 0, :], heads(ox, M), AX.X, ALU.max).then_inc(v_soft, 1)
                    unit(dve, v_soft, i, g, 2, N_SOFT)
                    tt(heads(ox, M), heads(ox, M), over(small[:, 0, :], M), ALU.subtract).then_inc(v_soft, 1)
                if g == 3 and tile1:
                    reached(dve, p_ok, i, GROUPS, GROUPS)
                    reached(dve, c_cs, i, GROUPS, GROUPS)
                    renew(i + 1, [s_qk[:], csum[:]], reset_qk)
                if g == 2 and tile1:
                    l0_norm(i + 1, 1)
                if prv:
                    unit(dve, p_s2, i, g - 1)
                    s = s_v[:, 2 * p1:2 * p1 + 2, :]
                    tt(s, s, bank[:, 5, 0:256].rearrange("p (q n) -> p q n", q=2), ALU.add).then_inc(v_s2, 1)
                if nxt:
                    unit(dve, p_s, i, g + 1)
                    unit(dve, c_es, i, g)
                    unit(dve, p_s2, i, g - 1)
                    ts(es[:, (g + 1) % 2, :], bank[:, 3, 0:256], -CLAMP, CLAMP, ALU.max, ALU.min).then_inc(v_sc, 1)
                if g == 1 and tile1:
                    some(2)
                    l0_hidden(i + 1)
                if prv:
                    unit(dve, c_o, i, g - 1, 1, 2)
                    dve.tensor_reduce(small[:, 4, :], heads(osq, DK), AX.X, ALU.add).then_inc(v_oss, 1)
                if now:
                    unit(dve, c_soft, i, g)
                    dve.tensor_reduce(small[:, 1, :], heads(ox, M), AX.X, ALU.add).then_inc(v_soft, 1)
                    unit(dve, v_soft, i, g, 4, N_SOFT)
                    dve.reciprocal(small[:, 2, :], small[:, 1, :]).then_inc(v_soft, 1)
                    tt(ox, ox, enz, ALU.mult).then_inc(v_soft, 1)
                    unit(dve, v_soft, i, g, 6, N_SOFT)
                    unit(dve, p_pT, i, g - 1)
                    tt(heads(pr, M), heads(ox, M), over(small[:, 2, :], M), ALU.mult).then_inc(v_soft, 1)
                if g == 2 and tile1:
                    l0_norm(i + 1, 2)
                if prv:
                    unit(dve, g_r, i, g - 1, 2, 2)
                    unit(dve, v_sg, i, g - 1)
                    unit(dve, c_o, i, g - 1, 2, 2)
                    for h in range(GH):
                        w = o_slot(h)
                        o = o_sb[:, w * P:(w + 1) * P]
                        ins = stt(o, o, small[:, 5, w:w + 1], sg[:, p1 % 2, h * P:(h + 1) * P], ALU.mult, ALU.mult)
                        ins.then_inc(v_og4, 1)
                    unit(dve, v_og4, i, g - 1, 4, 4)
                    dve.sem_inc(v_og, 1)
                some(1)
                if nxt:
                    unit(dve, c_th, i, g + 1)
                    r = sg[:, (g + 1) % 2, :]
                    stt(r, r, 1.0, bank[:, 4, :], ALU.add, ALU.mult).then_inc(v_sg, 1)
                if g == 0 and now:
                    reached(dve, v_s2, i, GROUPS, 0)
                    renew(i, [s_v[:]], reset_v)
                if g == 2 and tile1:
                    l0_norm(i + 1, 3)
                some(len(top))

            step(0, -1)
            tiles(dve, step)

        @block.gpsimd
        def _(pool):
            tt, ts = pool.tensor_tensor, pool.tensor_scalar
            pool.wait_ge(v_stat, 2 * TILES)
            pool.wait_ge(v_const, 1)
            ts(rstd1[:], mean1[:, :, 1], LN_EPS, None, ALU.add).then_inc(g_rstd, 1)
            pool.wait_ge(g_rstd, 1)
            tt(rstd1[:], rstd1[:], half_neg[:], ALU.pow).then_inc(g_rstd, 1)

            def l0_parts(j):
                reached(pool, z_c, j, 1, 1)
                reached(pool, z_mm, j, 2, 0)
                for n in range(5):
                    if n > 0:
                        reached(pool, z_part, j, 5, n)
                    apart(pool)
                    if n % 2 == 0:
                        ins = pool.tensor_copy(x_part[:, n // 2, :], xnT[:])
                    else:
                        ins = tt(xnT[:], xnT[:], x_part[:, n // 2, :], ALU.subtract)
                    ins.then_inc(z_part, 1)

            def l0_xnb(j):
                reached(pool, z_xn, j, 1, 1)
                reached(pool, z_v, j, VZ, 1 - VZ)
                tt(xn_b[:], xn[:], rows[:, 0, :], ALU.add).then_inc(z_xnb, 1)

            def l0_norm(j, part):
                par = j % 2
                n = 0 if part == 0 else 5
                if part != 1:
                    reached(pool, z_v, j, VZ, 3 if part == 0 else 6)
                    q = 0 if part == 0 else 1
                    apart(pool)
                    ts(rs[:, q, 0:1], mv[:, q, 1:2], LN_EPS, None, ALU.add).then_inc(z_g, 1)
                    reached(pool, z_g, j, GZ, n + 1)
                    tt(rs[:, q, 1:2], rs[:, q, 0:1], half_neg[:, 0:1], ALU.pow).then_inc(z_g, 1)
                else:
                    reached(pool, z_v, j, VZ, 4)
                    tt(norm[:], norm[:], rows[:, 1, :], ALU.mult).then_inc(z_g, 1)
                    reached(pool, z_g, j, GZ, 3)
                    tt(norm[:], norm[:], rows[:, 2, :], ALU.add).then_inc(z_g, 1)
                    reached(pool, z_g, j, GZ, 4)
                    reached(pool, l_xy, j, 16, 16)
                    reached(pool, v_fin, j, 1, -1)
                    x = x1[:, bass.ds(par, 1), :].rearrange("p a d -> p (a d)")
                    tt(x, norm[:], xy_in[:], ALU.add).then_inc(z_g, 1)

            l0_parts(0)
            pool.wait_ge(ld_misc, 16 * MISC)
            l0_xnb(0)
            for part in range(3):
                l0_norm(0, part)
            l0_parts(1)
            l0_xnb(1)

            def rope_rows(t):
                pool.tensor_copy(rope_now[:], rope_tab[:, bass.ds(t % SEQ_TILES, 1), :].rearrange("p a n -> p (a n)")).then_inc(rope_ld, 1)

            def half(x, q):
                return x.rearrange("p (h a m) -> p h a m", a=2, m=64)[:, :, q, :]

            def step(i, g):
                now, nxt, prv, prv2, tile1, tile2 = parts(i, g)
                if g == -1:
                    rope_rows(0)
                if g == 3 and tile1:
                    unit(pool, v_rope, i, g, 2, 2)
                    apart(pool)
                    rope_rows(i + 1)
                if g == 1 and tile2:
                    l0_parts(i + 2)
                if g == 2 and tile1:
                    l0_norm(i + 1, 0)
                if nxt:
                    unit(pool, v_rope, i, g + 1, 2, 2)
                    unit(pool, p_su, i, g)
                    tt(half(qk, 0), half(t1, 0), half(t2, 0), ALU.subtract).then_inc(g_rope, 1)
                    tt(half(qk, 1), half(t1, 1), half(t2, 1), ALU.add).then_inc(g_rope, 1)
                if g == 2 and tile1:
                    l0_norm(i + 1, 1)
                if prv:
                    unit(pool, v_oss, i, g - 1)
                    unit(pool, v_og, i, g - 2)
                    apart(pool)
                    ts(small[:, 3, :], small[:, 4, :], 1.0 / DK, LN_EPS, ALU.mult, ALU.add).then_inc(g_r, 1)
                    unit(pool, g_r, i, g - 1, 1, 2)
                    tt(small[:, 5, :], small[:, 3, :], half_neg[:, 0:GH], ALU.pow).then_inc(g_r, 1)
                if g == 2 and tile1:
                    l0_norm(i + 1, 2)
                if g == 2 and tile2:
                    l0_xnb(i + 2)

            step(0, -1)
            tiles(pool, step)


_OUT = (TILES * P, D)


def kernel(**inputs):
    import numpy as _np
    import concourse.bacc as _bacc
    from concourse import mybir as _mybir
    from concourse.bass_utils import run_bass_kernel_spmd as _run

    def arr(name):
        return _np.asarray(inputs[name])

    def col(name):
        return arr(name).reshape(KD, P).T

    pos = _np.arange(T, dtype=_np.float32)
    inv = _np.float32(1.0) / _np.float32(10000.0) ** (_np.arange(0, DK, 2, dtype=_np.float32) / _np.float32(DK))
    ang = pos[:, None] * inv[None, :]
    tri = _np.triu(_np.ones((P, P), _np.float32))
    last = _np.zeros((P, P), _np.float32)
    last[P - 1] = 1.0
    arrays = {
        "u": arr("L0_attn_u").reshape(TILES * P, D),
        "ident": _np.eye(P, dtype=_np.float32),
        "tri": tri,
        "last_row": last,
        "rope": _np.concatenate([_np.cos(ang), _np.sin(ang)], axis=1).astype(_np.float32),
        "cols": _np.stack([col("L0_attn_" + n) for n in ("a", "b", "c", "d", "gate_b")], axis=1),
        "gnorm": arr("L1_attn_g_norm_weight").reshape(DK, 1),
        "lut": arr("L1_ffn_lut").reshape(1, LUT),
        "gate_wT": arr("L0_attn_gate_w").T,
        "lr_u": arr("L0_attn_d_lr_u"),
        "lr_v": arr("L0_attn_d_lr_v"),
        "w_synT": arr("L0_ffn_W_syn").T,
        "w_outT": arr("L0_ffn_W_out").T,
        "b_syn": arr("L0_ffn_b_syn").reshape(1, NSYN),
        "b_out": arr("L0_ffn_b_out").reshape(1, D),
        "gamma": arr("L0_ffn_gamma").reshape(1, D),
        "beta": arr("L0_ffn_beta").reshape(1, D),
        "wqT": arr("L1_attn_Wq").T,
        "wkT": arr("L1_attn_Wk").T,
        "wvT": arr("L1_attn_Wv").T,
        "wgT": arr("L1_attn_Wg").T,
        "woT": arr("L1_attn_Wo").T,
        "ws1T": arr("L1_attn_Ws1").T,
        "ws2T": arr("L1_attn_Ws2").T,
        "bs2": arr("L1_attn_bs2").reshape(1, HEADS * M),
        "gate_idx": arr("L1_ffn_gate_idx").T,
        "up_idx": arr("L1_ffn_up_idx").T,
        "down_idx": arr("L1_ffn_down_idx").T,
    }
    arrays = {n: _np.ascontiguousarray(x) for n, x in arrays.items()}
    nc = _bacc.Bacc("TRN2", target_bir_lowering=False, num_devices=1)
    aps = {n: nc.dram_tensor("in_" + n, x.shape, _mybir.dt.from_np(x.dtype), kind="ExternalInput").ap() for n, x in arrays.items()}
    res = nc.dram_tensor("result", _OUT, F32, kind="ExternalOutput").ap()
    build(nc, aps, res)
    r = _run(nc, [{"in_" + n: x for n, x in arrays.items()}], core_ids=[0])
    return r.results[0]["result"].reshape(NB, T, D)
```

```python
from contextlib import ExitStack

import numpy as np
import concourse.bass as bass
from concourse import mybir

F32 = mybir.dt.float32
BF16 = mybir.dt.bfloat16
F16 = mybir.dt.float16
I32 = mybir.dt.int32
ALU = mybir.AluOpType
ACT = mybir.ActivationFunctionType
AX = mybir.AxisListType

P = 128
D = 256
KD = D // P
NB, T = 2, 1024
TILES = NB * T // P
SEQ_TILES = T // P
HEADS, DK, M = 16, 128, 64
GH = 4
GROUPS = HEADS // GH
HD = HEADS * DK
NSYN = 1024
KN = NSYN // P
TOPK = max(1, int(NSYN * (1.0 - 0.9)))
ROUNDS = (TOPK + 7) // 8
INTER = 688
KI = (INTER + P - 1) // P
LAST = INTER - (KI - 1) * P
LUT = 16
LN_EPS = 1e-5
CLAMP = 32.0
QK_SCALE = float(DK) ** -0.5
LOW = -3.0e38
LUT_AT = (0, KD * INTER, 2 * KD * INTER)
LUT_END = LUT_AT[2] + KI * D
ARENA = 12544
MISC = 11
Y_STEPS = 4
N_SOFT = 4
N_TOP = 2 * ROUNDS
LUT_PARTS = ((0, KD * INTER), (KD * INTER, KD * INTER), (2 * KD * INTER, KI * D))
F_PARTS = ((P, 0, 0, 3 * P, 0), (P, 1, 0, 2 * P, 3), (LAST, 1, 2 * P, P, KI - 1))
V_F = 2 * len(F_PARTS)
TOP_OF = {2: (0, 7), 3: (7, 17), 0: (17, 23), 1: (23, N_TOP - 1)}
TOP_FIRST = 8
TOP0_AT = 27
Z_BANKS = (7, 6)
X_SCALE = 512.0
W_TOP = 2.0 ** 14
BLOCKS = 8
W_FIRST = ((2, 6), (1, 5), (0, 4), (3, 7))
VZ = GZ = 7


def reached(eng, sem, tile, per_tile, nth):
    value = tile * per_tile + nth
    if isinstance(value, int) and value <= 0:
        return
    eng.wait_ge(sem, value)


def unit(eng, sem, tile, group, nth=1, per_unit=1):
    reached(eng, sem, tile, GROUPS * per_unit, group * per_unit + nth)


def slot(head):
    return 2 * (1 - head % 2) + head // 2


def o_slot(head):
    return 2 * (head % 2) + head // 2


def build(nc, a, out):
    with ExitStack() as ctx:
        def sb(name, shape, dt=F32):
            return ctx.enter_context(nc.sbuf_tensor(name, shape, dt))

        def sem(name):
            return ctx.enter_context(nc.semaphore(name))

        bank = ctx.enter_context(nc.psum_tensor("bank", [P, 8, 512], F32))

        w_f32 = sb("w_f32", [P, BLOCKS, HD])
        w_f16 = w_f32[:, :, :].rearrange("p b n -> p (b n)").bitcast(F16).rearrange("p (b s n) -> p b s n", b=BLOCKS, s=2)
        wo = sb("wo", [P, HEADS, D])
        ws1 = sb("ws1", [P, KD, 16])
        ws2 = sb("ws2", [17, HEADS * M])
        w_lut = sb("w_lut", [P, LUT_END])
        w_gate = w_lut[:, 0:LUT_AT[1]].rearrange("p (k o) -> p k o", k=KD)
        w_up = w_lut[:, LUT_AT[1]:LUT_AT[2]].rearrange("p (k o) -> p k o", k=KD)
        w_down = w_lut[:, LUT_AT[2]:LUT_END].rearrange("p (k o) -> p k o", k=KI)
        t_syn = sb("t_syn", [P, KD, NSYN], BF16)
        t_out = sb("t_out", [P, KN, D])
        rope_tab = sb("rope_tab", [P, SEQ_TILES, 2 * 64])
        b_syn = sb("b_syn", [P, NSYN])
        rows = sb("rows", [P, 3, D])
        tri = sb("tri", [P, P])
        last_row = sb("last_row", [P, P])
        ident = sb("ident", [P, P])
        ident_b = sb("ident_b", [P, P], BF16)
        cols = sb("cols", [P, 6, KD])
        gnorm = sb("gnorm", [P, 1])
        half_neg = sb("half_neg", [P, TILES])
        mean1 = sb("mean1", [P, TILES, 2])
        rstd1 = sb("rstd1", [P, TILES])
        scales = sb("scales", [P, 8])

        s_qk = sb("s_qk", [P, HEADS * M])
        s_v = sb("s_v", [P, HEADS // 2, DK])
        csum = sb("csum", [P, HEADS * M])

        zbuf = sb("zbuf", [P, 2, NSYN])
        z = zbuf[:, 0, :]
        zw = zbuf[:, 1, :]
        x_in = sb("x_in", [P, D])
        xy_in = sb("xy_in", [P, D])
        xn = sb("xn", [P, D])
        xn_b = sb("xn_b", [P, D])
        xnT = sb("xnT", [P, D])
        x_part = sb("x_part", [P, 3, D], BF16)
        top8 = sb("top8", [P, 2, 8])
        thr = sb("thr", [P, 1])
        norm = sb("norm", [P, D])
        x1 = sb("x1", [P, 2, D])
        stat = sb("stat", [P, 2, 6])
        mv = sb("mv", [P, 2, 2])
        rs = sb("rs", [P, 2, 2])
        xT = sb("xT", [P, KD, P])
        x_f16 = sb("x_f16", [P, 2, KD * P], F16)
        s16 = sb("s16", [17, P])
        rope_now = sb("rope_now", [P, 2 * 64])
        o_fin = x_in

        arena = sb("arena", [P, ARENA])
        used = [0]

        def cut(words):
            v = arena[:, used[0]:used[0] + words]
            used[0] += words
            return v

        hT = cut(1024).rearrange("p (k t) -> p k t", k=KN)
        t1 = cut(1024)
        t2 = cut(1024)
        qk = cut(1024)
        qkT = cut(1024)
        v_sb = cut(1024).rearrange("p (b n) -> p b n", b=2)
        es = cut(512).rearrange("p (b n) -> p b n", b=2)
        esT = cut(512).rearrange("p (b n) -> p b n", b=2)
        enz = cut(256)
        am = cut(512)
        wm = cut(512)
        ox = cut(256)
        pr = cut(256)
        pT = cut(256)
        o_gated = cut(512)
        o_sb = cut(512)
        ogT = cut(512)
        sg = cut(1024).rearrange("p (b n) -> p b n", b=2)
        small = sb("small", [P, 6, GH])
        f_th = cut(KI * P).rearrange("p (k t) -> p k t", k=KI)
        assert used[0] <= ARENA

        x_all = wo[:, :, :].rearrange("p h n -> p (h n)").rearrange("p (t n) -> p t n", t=TILES)
        xn_all = w_f32[:, 4:6, :].rearrange("p k n -> p (k n)").rearrange("p (t n) -> p t n", t=TILES)
        xnT_all = w_f32[:, 6:8, :]
        ug = arena[:, 0:4096].rearrange("p (k n) -> p k n", k=KD)
        ys = arena[:, 4096:8192].rearrange("p (k n) -> p k n", k=KD)
        bu = arena[:, 8192:10240].rearrange("p (s n) -> p s n", s=2)
        gate_wT = arena[:, 10240:10752].rearrange("p (k n) -> p k n", k=KD)
        lr_u = x1[:, 1, 246:254].rearrange("p (k n) -> p k n", k=KD)
        lr_v = arena[0:4, 10752:11008]
        early = x1[:, 1, :]
        ones_m = early[:, 0:P]
        stat1 = early[:, P:P + 6 * TILES].rearrange("p (t n) -> p t n", t=TILES)
        col_t = early[:, 224:232].rearrange("p (s k) -> p s k", k=KD)
        u_sum = early[:, 232:236].rearrange("p (k n) -> p k n", k=KD)
        d_eff = early[:, 236:240].rearrange("p (k n) -> p k n", k=KD)
        aa = early[:, 240:242]
        r42 = early[0:4, 242:244]
        half_norm = early[:, 244:245]
        w_sq = stat[:, :, :].rearrange("p a n -> p (a n)")[:, 0:BLOCKS]
        w_sum = early[:, P:P + 1]
        w_pow = early[:, P + 1:P + 2]
        w_inv = early[:, P + 2:P + 3]
        w_scale = early[:, P + 3:P + 4]
        w_root = early[:, P + 4:P + 5]
        unscale = scales[:, 4:5]
        half_unscale = scales[:, 5:6]
        w_apart = [arena[:, 6912:8960], arena[:, 8960:11008]]
        idx_i = w_lut[:, :].bitcast(I32)
        idx_b = [w_f32[:, 2, 0:LUT_AT[2] // 2].bitcast(BF16)[:, 0:LUT_AT[1]],
                 w_f32[:, 2, 0:LUT_AT[2] // 2].bitcast(BF16)[:, LUT_AT[1]:LUT_AT[2]],
                 arena[:, 4096:4096 + KI * D // 2].bitcast(BF16)]
        hot = arena[:, ARENA - KI * D:ARENA].bitcast(BF16).rearrange("p (s n) -> p s n", s=2)
        diag = [x.bitcast(BF16).rearrange("p (k n) -> p k n", k=LUT)
                for x in (s_qk[:, :], s_v[:, :, :].rearrange("p h n -> p (h n)"), csum[:, :])]
        lut = rope_now[:, 0:48].rearrange("p (s k) -> p s k", s=3)
        lut_b = rope_now[:, 48:72].bitcast(BF16).rearrange("p (s k) -> p s k", s=3)
        syn_raw = zbuf[:, :, :].rearrange("p a n -> p (a n)").rearrange("p (k n) -> p k n", k=KD)
        tern_tmp = arena[:, 4096:6144]

        xy_dram = nc.dram_tensor("xy_scratch", (TILES * P, D), F32, kind="Internal").ap()

        ld_x = [sem(f"ld_x{n}") for n in range(4)]
        ld_misc = sem("ld_misc")
        ld_gate = sem("ld_gate")
        ld_syn = sem("ld_syn")
        ld_w = [sem(f"ld_w{n}") for n in range(BLOCKS)]
        ld_o = sem("ld_o")
        ld_lut = sem("ld_lut")
        st_xy = sem("st_xy")
        v_stat = sem("v_stat")
        g_rstd = sem("g_rstd")
        v_xn = sem("v_xn")
        t_xn = sem("t_xn")
        c_xn = sem("c_xn")
        t_gate = sem("t_gate")
        c_gate = sem("c_gate")
        v_ug = sem("v_ug")
        t_lr = sem("t_lr")
        c_lr = sem("c_lr")
        v_scan = sem("v_scan")
        g_pr = sem("g_pr")
        g_osg = sem("g_osg")
        c_scaled = sem("c_scaled")
        g_root = sem("g_root")
        z_lo = sem("z_lo")
        z_hi = sem("z_hi")
        c_rope = sem("c_rope")
        g_lo = sem("g_lo")
        v_lo = sem("v_lo")
        c_hi = sem("c_hi")
        v_scale = sem("v_scale")
        t_sq = sem("t_sq")
        c_sq = sem("c_sq")
        g_diag = sem("g_diag")
        c_wo = sem("c_wo")
        ld_ident = sem("ld_ident")
        v_idx = sem("v_idx")
        v_deff = sem("v_deff")
        t_y = sem("t_y")
        v_xy = sem("v_xy")
        v_tern = sem("v_tern")
        t_tern = sem("t_tern")
        c_aa = sem("c_aa")
        v_const = sem("v_const")
        spare = sem("spare")
        v_lut = sem("v_lut")
        v_hot = sem("v_hot")
        t_hot = sem("t_hot")
        c_lut = sem("c_lut")

        l_x = sem("l_x")
        l_xy = sem("l_xy")
        z_xn = sem("z_xn")
        z_t = sem("z_t")
        z_c = sem("z_c")
        z_part = sem("z_part")
        z_xnb = sem("z_xnb")
        z_mm = sem("z_mm")
        z_sb = sem("z_sb")
        z_top = sem("z_top")
        z_hid = sem("z_hid")
        z_hT = sem("z_hT")
        z_hc = sem("z_hc")
        z_out = sem("z_out")
        z_v = sem("z_v")
        z_g = sem("z_g")
        z_x2t = sem("z_x2t")
        z_x2 = sem("z_x2")
        rope_ld = sem("rope_ld")
        reset_qk = sem("reset_qk")
        reset_v = sem("reset_v")
        p_down = sem("p_down")
        p_s1 = sem("p_s1")
        c_s1 = sem("c_s1")
        p_qk = sem("p_qk")
        v_rope = sem("v_rope")
        g_rope = sem("g_rope")
        p_v = sem("p_v")
        c_v = sem("c_v")
        p_s = sem("p_s")
        v_sc = sem("v_sc")
        c_es = sem("c_es")
        p_g = sem("p_g")
        c_th = sem("c_th")
        v_sg = sem("v_sg")
        p_qkT = sem("p_qkT")
        c_qkT = sem("c_qkT")
        p_cs = sem("p_cs")
        c_cs = sem("c_cs")
        v_enz = sem("v_enz")
        p_esT = sem("p_esT")
        c_esT = sem("c_esT")
        p_a = sem("p_a")
        v_a = sem("v_a")
        p_ok = sem("p_ok")
        p_su = sem("p_su")
        v_su = sem("v_su")
        v_soft = sem("v_soft")
        c_soft = sem("c_soft")
        p_pT = sem("p_pT")
        c_pT = sem("c_pT")
        p_w2 = sem("p_w2")
        v_w2 = sem("v_w2")
        p_o = sem("p_o")
        c_o = sem("c_o")
        g_r = sem("g_r")
        v_og = sem("v_og")
        p_ogT = sem("p_ogT")
        c_ogT = sem("c_ogT")
        p_s2 = sem("p_s2")
        v_s2 = sem("v_s2")
        p_wo = sem("p_wo")
        v_fin = sem("v_fin")
        p_gate = sem("p_gate")
        p_up = sem("p_up")
        c_fth = sem("c_fth")
        v_f = sem("v_f")
        st_out = sem("st_out")

        block = ctx.enter_context(nc.Block())

        def apart(eng):
            eng.sem_inc(spare, 1)

        def tiles(eng, step):
            for g in range(GROUPS):
                step(0, g)
            with eng.Fori(1, TILES - 2) as i:
                for g in range(GROUPS):
                    step(i, g)
            for i in (TILES - 2, TILES - 1):
                for g in range(GROUPS):
                    step(i, g)
            step(TILES, 0)
            step(TILES, 1)

        def has_before(i):
            return not isinstance(i, int) or i > 0

        def parts(i, g):
            if not isinstance(i, int):
                return (True,) * 6
            n, end = GROUPS * i + g, GROUPS * TILES
            return 0 <= n < end, n + 1 < end, 0 < n <= end, 1 < n <= end + 1, i + 1 < TILES, i + 2 < TILES

        @block.sync
        def _(sp):
            x_t = a["u"].rearrange("(t p) d -> p t d", p=P)
            for n in range(4):
                sp.dma_start(x_all[:, 4 * n:4 * n + 4, :], x_t[:, 4 * n:4 * n + 4, :]).then_inc(ld_x[n], 16)
            sp.dma_start(ident[:], a["ident"]).then_inc(ld_ident, 16)
            sp.dma_start(lut[:, 0, :], a["lut"].to_broadcast([P, LUT])).then_inc(ld_ident, 16)
            sp.dma_start(syn_raw, a["w_synT"].rearrange("(k p) n -> p k n", p=P)).then_inc(ld_syn, 16)
            sp.dma_start(t_out[:], a["w_outT"].rearrange("(k p) n -> p k n", p=P)).then_inc(ld_syn, 16)
            sp.dma_start(gate_wT, a["gate_wT"].rearrange("(k p) n -> p k n", p=P)).then_inc(ld_gate, 16)
            sp.dma_start(cols[:, 0:5, :], a["cols"]).then_inc(ld_gate, 16)
            sp.dma_start(lr_u, a["lr_u"].rearrange("(k p) n -> p k n", p=P)).then_inc(ld_gate, 16)
            sp.dma_start(lr_v, a["lr_v"]).then_inc(ld_gate, 16)
            for n, name in enumerate(("gate_idx", "up_idx")):
                sp.dma_start(idx_i[:, LUT_AT[n]:LUT_AT[n + 1]].rearrange("p (k n) -> p k n", k=KD),
                             a[name].rearrange("(k p) n -> p k n", p=P)).then_inc(ld_lut, 16)
            whole = (KI - 1) * D
            sp.dma_start(idx_i[:, LUT_AT[2]:LUT_AT[2] + whole].rearrange("p (k n) -> p k n", n=D),
                         a["down_idx"][0:(KI - 1) * P, :].rearrange("(k p) n -> p k n", p=P)).then_inc(ld_lut, 16)
            sp.wait_ge(v_idx, 1)
            sp.dma_start(idx_i[0:LAST, LUT_AT[2] + whole:LUT_END], a["down_idx"][(KI - 1) * P:INTER, :]).then_inc(ld_lut, 16)

            def load_x(j):
                reached(sp, z_xn, j, 1, 0)
                sp.dma_start(x_in[:], a["u"][bass.ds(j * P, P), :]).then_inc(l_x, 16)

            def load_xy(j):
                reached(sp, z_g, j, GZ, -2)
                sp.dma_start(xy_in[:], xy_dram[bass.ds(j * P, P), :]).then_inc(l_xy, 16)

            load_x(0)
            for dst, src in (
                (b_syn[:], a["b_syn"].to_broadcast([P, NSYN])),
                (rows[:, 0, :], a["b_out"].to_broadcast([P, D])), (rows[:, 1, :], a["gamma"].to_broadcast([P, D])),
                (rows[:, 2, :], a["beta"].to_broadcast([P, D])), (gnorm[:], a["gnorm"]),
                (tri[:], a["tri"]), (last_row[:], a["last_row"]),
                (rope_tab[:], a["rope"].rearrange("(t p) n -> p t n", p=P)),
                (ws1[:], a["ws1T"].rearrange("(k p) n -> p k n", p=P)),
                (ws2[0:16, :], a["ws2T"]), (ws2[16:17, :], a["bs2"]),
            ):
                sp.dma_start(dst, src).then_inc(ld_misc, 16)

            def load_w(b):
                m, k = b // KD, b % KD
                dst = w_apart[b // 4] if b % 4 == 3 else w_f32[:, b, :]
                sp.dma_start(dst, a[("wqT", "wkT", "wvT", "wgT")[m]][k * P:(k + 1) * P, :]).then_inc(ld_w[b], 16)

            load_w(0)
            load_w(1)
            sp.wait_ge(t_xn, 8)
            load_w(4)
            load_w(5)
            sp.wait_ge(t_gate, 8)
            sp.wait_ge(v_ug, 4)
            load_w(6)
            load_x(1)
            sp.wait_ge(v_scan, 4 * Y_STEPS)
            sp.wait_ge(t_y, 8)
            load_w(3)
            load_w(7)
            xy_t = xy_dram.rearrange("(t p) d -> p t d", p=P)
            for n in range(4):
                sp.wait_ge(v_xy, 2 * n + 2)
                sp.dma_start(xy_t[:, 4 * n:4 * n + 4, :], x_all[:, 4 * n:4 * n + 4, :]).then_inc(st_xy, 16)
            sp.wait_ge(st_xy, 64)
            sp.dma_start(wo[:], a["woT"].rearrange("(h p) n -> p h n", p=P)).then_inc(ld_o, 16)

            def step(i, g):
                now, nxt, prv, prv2, tile1, tile2 = parts(i, g)
                if g == 0 and tile2:
                    reached(sp, st_out, i - 1, 16, 0)
                    apart(sp)
                    load_x(i + 2)
                if g == 1 and has_before(i):
                    reached(sp, v_fin, i, 1, 0)
                    sp.dma_start(out[bass.ds((i - 1) * P, P), :], o_fin[:]).then_inc(st_out, 16)
                if g == 2 and tile2:
                    load_xy(i + 2)

            load_xy(0)
            sp.wait_ge(v_hot, 2 * LUT)
            load_w(2)
            load_xy(1)
            tiles(sp, step)
            sp.wait_ge(st_out, 16 * TILES)

        @block.tensor
        def _(pe):
            def mm(o, lhsT, rhs, start, stop):
                return pe.matmul(o, lhsT, rhs, start=start, stop=stop)

            def l0_xnT(j):
                reached(pe, z_xn, j, 1, 1)
                for k in range(KD):
                    ins = pe.transpose(bank[:, 5, k * P:(k + 1) * P], xn[:, k * P:(k + 1) * P], ident[:])
                ins.then_inc(z_t, 1)

            def l0_z(j):
                reached(pe, z_part, j, 5, 5)
                for c in range(2):
                    if c == 1:
                        reached(pe, z_hc, j, 1, 0)
                    n = 0
                    for s in range(3):
                        for k in range(KD):
                            ins = mm(bank[:, Z_BANKS[c], :], x_part[:, s, k * P:(k + 1) * P], t_syn[:, k, c * 512:(c + 1) * 512], n == 0, n == 5)
                            n += 1
                    ins.then_inc(z_mm, 1)

            def l0_hT(j):
                reached(pe, z_hid, j, 1, 1)
                for n in range(KN):
                    ins = pe.transpose(bank[:, 5 + n // 4, (n % 4) * P:(n % 4 + 1) * P], zw[:, n * P:(n + 1) * P], ident[:])
                ins.then_inc(z_hT, 1)

            def l0_out(j):
                reached(pe, z_hc, j, 1, 1)
                for n in range(KN):
                    ins = mm(bank[:, 3, 0:D], hT[:, n, :], t_out[:, n, :], n == 0, n == KN - 1)
                ins.then_inc(z_out, 1)

            def l0_xT(j):
                reached(pe, z_v, j, VZ, VZ)
                for k in range(KD):
                    ins = pe.transpose(bank[:, 3, k * P:(k + 1) * P], norm[:, k * P:(k + 1) * P], ident[:])
                ins.then_inc(z_x2t, 1)

            pe.wait_ge(ld_ident, 32)
            for n in range(8):
                k, q = n // 4, n % 4
                for t in range(4):
                    pe.wait_ge(v_xn, 4 * q + t + 1)
                    ins = pe.transpose(bank[:, n, t * P:(t + 1) * P], xn_all[:, 4 * q + t, k * P:(k + 1) * P], ident[:])
                ins.then_inc(t_xn, 1)
            pe.wait_ge(c_xn, 8)
            pe.wait_ge(v_const, 2)
            pe.wait_ge(v_tern, 2)
            mm(bank[:, 7, 0:2], ones_m, scales[:, 0:2], True, True).then_inc(t_tern, 1)
            pe.wait_ge(ld_gate, 64)
            for n in range(8):
                e, c = n // 4, n % 4
                if n == 7:
                    pe.wait_ge(v_tern, 3)
                for k in range(KD):
                    ins = mm(bank[:, n, :], gate_wT[:, k, e * P:(e + 1) * P], xnT_all[:, k, c * 512:(c + 1) * 512], k == 0, k == KD - 1)
                ins.then_inc(t_gate, 1)

            def table(*steps):
                for m in steps:
                    n, k = m // LUT, m % LUT
                    w = LUT_PARTS[n][1]
                    first = 0 if n % 2 == 0 else 3
                    if m == 0:
                        pe.wait_ge(g_diag, 3)
                        pe.wait_ge(c_gate, 3)
                    if m == 2 * LUT:
                        pe.wait_ge(c_lut, 3)
                    pe.wait_ge(v_hot, m + 1)
                    for s in range(3):
                        for c in range(3):
                            lo, hi = c * 512, min(w, (c + 1) * 512)
                            ins = mm(bank[:, first + c, 0:hi - lo], diag[s][:, k, :], hot[:, k % 2, lo:hi],
                                     k == 0 and s == 0, k == LUT - 1 and s == 2)
                    ins.then_inc(t_hot, 1)

            def y_back(*pairs):
                for n in pairs:
                    if n > 1:
                        pe.wait_ge(v_xy, n - 1)
                    for t in range(2):
                        tile = 2 * n + t
                        for k in range(KD):
                            pe.wait_ge(v_scan, Y_STEPS * (2 * (tile // SEQ_TILES) + k + 1))
                            ins = pe.transpose(bank[:, 6 + n % 2, t * D + k * P:t * D + (k + 1) * P], ys[:, k, tile * P:(tile + 1) * P], ident[:])
                    ins.then_inc(t_y, 1)

            table(0, 1, 2, 3)
            pe.wait_ge(v_ug, 5)
            pe.wait_ge(c_gate, 8)
            for k in range(KD):
                ins = mm(bank[0:4, 3, 0:NB], lr_u[:, k, :], u_sum[:, k, :], k == 0, k == KD - 1)
            ins.then_inc(t_lr, 1)
            pe.wait_ge(c_lr, 1)
            for k in range(KD):
                ins = mm(bank[:, 4, k * NB:(k + 1) * NB], lr_v[:, k * P:(k + 1) * P], r42, True, True)
            ins.then_inc(t_lr, 1)
            l0_xnT(0)
            table(4, 5, 6, 7, 8)
            l0_z(0)
            table(9, 10)
            reached(pe, z_sb, 0, 2, 2)
            y_back(0, 1, 2, 3)
            table(*range(11, LUT))
            y_back(4, 5, 6, 7)
            pe.wait_ge(v_deff, 1)
            pe.wait_ge(z_c, 1)
            table(*range(LUT, 2 * LUT + 3))
            pe.wait_ge(c_lut, 6)
            l0_xnT(1)
            table(*range(2 * LUT + 3, 2 * LUT + 7))
            pe.wait_ge(c_sq, BLOCKS)
            mm(bank[:, 4, 0:BLOCKS], ones_m, w_sq, True, True).then_inc(t_sq, 1)
            table(*range(2 * LUT + 7, LUT + TOP0_AT))
            pe.wait_ge(z_c, 2)
            l0_hT(0)
            l0_z(1)
            table(LUT + TOP0_AT)
            l0_out(0)
            table(*range(LUT + TOP0_AT + 1, 3 * LUT))
            l0_xT(0)
            pe.wait_ge(c_lut, 9)
            pe.wait_ge(ld_misc, 16 * MISC)
            pe.wait_ge(v_lo, 4)
            pe.wait_ge(c_wo, 1)

            def project(o, m, g):
                n = 0
                for xs, ws in ((0, 0), (0, 1), (1, 0)):
                    for k in range(KD):
                        b = KD * m + k
                        ins = mm(o, x_f16[:, xs, k * P:(k + 1) * P], w_f16[:, b // 4 * 4 + (b + 1) % 4, ws, g * 512:(g + 1) * 512], n == 0, n == 5)
                        n += 1
                return ins

            def step(i, g):
                now, nxt, prv, prv2, tile1, tile2 = parts(i, g)
                n1, p1, p2 = (g + 1) % GROUPS, (g - 1) % GROUPS, (g - 2) % GROUPS
                if now:
                    unit(pe, g_rope, i, g, 2, 2)
                    for h in range(2 * GH):
                        ins = pe.transpose(bank[:, h // GH, (h % GH) * P:(h % GH + 1) * P], qk[:, h * P:(h + 1) * P], ident[:])
                    ins.then_inc(p_qkT, 1)
                    unit(pe, c_es, i, g)
                    if g == 0:
                        reached(pe, reset_qk, i, 2, 2)
                    if g == 2 and tile1:
                        reached(pe, z_v, i + 1, VZ, 1)
                    mm(bank[:, 3, 0:256], tri[:], es[:, g % 2, :], True, False)
                    mm(bank[:, 3, 0:256], last_row[:], csum[:, g * 256:(g + 1) * 256], False, True).then_inc(p_cs, 1)
                if prv:
                    unit(pe, v_soft, i, g - 1, N_SOFT, N_SOFT)
                    unit(pe, v_s2, i, g - 2)
                    if g == 1 and tile2:
                        reached(pe, z_c, i + 2, 1, 1)
                    for h in range(2):
                        ins = pe.transpose(bank[:, 5, h * P:(h + 1) * P], pr[:, h * P:(h + 1) * P], ident[:])
                    ins.then_inc(p_pT, 1)
                if now:
                    for h in range(2):
                        ins = pe.transpose(bank[:, 5, (2 + h) * P:(3 + h) * P], es[:, g % 2, h * P:(h + 1) * P], ident[:])
                    ins.then_inc(p_esT, 1)
                    unit(pe, c_qkT, i, g, 2, 2)
                if g == 0 and has_before(i):
                    reached(pe, v_f, i, V_F, 0)
                    for c in range(KI):
                        r = P if c < KI - 1 else LAST
                        ins = mm(bank[:, 2, 0:D], f_th[0:r, c, :], w_down[0:r, c, :], False, False)
                    ins.then_inc(p_down, 1)
                if g == 0 and now:
                    ffn(w_gate, 0, p_gate)
                if g == 3 and now:
                    ffn(w_up, 0, p_up)
                if now:
                    unit(pe, v_sg, i, g)
                    for h in range(GH):
                        ins = mm(bank[:, 4, h * P:(h + 1) * P], qkT[:, 512 + h * P:512 + (h + 1) * P], qkT[:, h * P:(h + 1) * P], True, True)
                    ins.then_inc(p_a, 1)
                if prv2:
                    unit(pe, v_og, i, g - 2)
                    if now:
                        unit(pe, c_cs, i, g)
                    for h in range(GH):
                        ins = pe.transpose(bank[:, 3, h * P:(h + 1) * P], o_gated[:, o_slot(h) * P:(o_slot(h) + 1) * P], ident[:])
                    ins.then_inc(p_ogT, 1)
                if prv:
                    unit(pe, c_pT, i, g - 1)
                    if now:
                        unit(pe, c_esT, i, g)
                    if g == 2 and tile2:
                        reached(pe, z_sb, i + 2, 2, 2)
                    for h in range(GH):
                        lo, q = (h % 2) * M, h // 2
                        ins = mm(bank[:, 6 - h % 2, q * P:(q + 1) * P], esT[lo:lo + M, p1 % 2, q * P:(q + 1) * P], pT[lo:lo + M, q * P:(q + 1) * P], True, True)
                    ins.then_inc(p_w2, 1)
                if g == 3 and tile1:
                    unit(pe, c_ogT, i, g - 2)
                    l0_xT(i + 1)
                if prv2:
                    unit(pe, c_ogT, i, g - 2)
                    if p2 == 0:
                        reached(pe, v_fin, i, 1, 0)
                    for h in range(GH):
                        ins = mm(bank[:, 2, 0:D], ogT[:, h * P:(h + 1) * P], wo[:, GH * p2 + h, :],
                                 p2 == 0 and h == 0, p2 == GROUPS - 1 and h == GH - 1)
                    ins.then_inc(p_wo, 1)
                if (g == 3 and tile1) or g == -1:
                    reached(pe, z_x2, i + 1 if g == 3 else i, 1, 1)
                    reached(pe, z_lo, i + 1 if g == 3 else i, 1, 1)
                    for k in range(KD):
                        ins = mm(bank[0:16, 3, 0:P], ws1[:, k, :], xT[:, k, :], k == 0, k == KD - 1)
                    ins.then_inc(p_s1, 1)
                if nxt:
                    if g == 0:
                        reached(pe, v_f, i, V_F, V_F // 2)
                    if g == 3:
                        reached(pe, v_f, i, V_F, V_F)
                    project(bank[:, 0, :], 0, n1)
                    project(bank[:, 1, :], 1, n1).then_inc(p_qk, 1)
                if now:
                    unit(pe, v_a, i, g)
                    unit(pe, v_su, i, g - GROUPS)
                    for h in range(GH):
                        s = (GH * g + h) * M
                        mm(bank[:, 4, h * M:(h + 1) * M], am[:, h * P:(h + 1) * P], es[:, g % 2, h * M:(h + 1) * M], True, False)
                        ins = mm(bank[:, 4, h * M:(h + 1) * M], qkT[:, h * P:(h + 1) * P], s_qk[:, s:s + M], False, True)
                    ins.then_inc(p_ok, 1)
                    unit(pe, c_esT, i, g)
                    unit(pe, v_w2, i, g - 1)
                    for h in range(GH):
                        ins = mm(bank[:, 5, h * M:(h + 1) * M], qk[:, 512 + h * P:512 + (h + 1) * P], es[:, g % 2, h * M:(h + 1) * M], True, True)
                    ins.then_inc(p_su, 1)
                if prv:
                    unit(pe, v_w2, i, g - 1)
                    unit(pe, v_s2, i, g - 1 - GROUPS)
                    if g == 1:
                        reached(pe, reset_v, i, 1, 1)
                    if now:
                        unit(pe, c_v, i, g)
                    else:
                        unit(pe, c_v, i, g - 1)
                    for h in range(GH):
                        lo, q, w = (h % 2) * M, h // 2, slot(h) * P
                        o = bank[:, 6 + h % 2, q * P:(q + 1) * P]
                        mm(o, wm[:, w:w + P], v_sb[:, p1 % 2, h * P:(h + 1) * P], True, False)
                        ins = mm(o, pT[lo:lo + M, q * P:(q + 1) * P], s_v[lo:lo + M, 2 * p1 + q, :], False, True)
                    ins.then_inc(p_o, 1)
                if nxt:
                    if g == 3:
                        reached(pe, c_s1, i + 1, 1, 1)
                    elif g == -1:
                        reached(pe, c_s1, i, 1, 1)
                    else:
                        unit(pe, c_cs, i, g)
                        unit(pe, c_ogT, i, g - 2)
                    mm(bank[:, 3, 0:256], s16[:], ws2[:, n1 * 256:(n1 + 1) * 256], True, True).then_inc(p_s, 1)
                if prv:
                    if now:
                        unit(pe, v_su, i, g)
                    for h in range(GH):
                        lo, q = (h % 2) * M, h // 2
                        ins = mm(bank[lo:lo + M, 5, q * P:(q + 1) * P], es[:, p1 % 2, h * M:(h + 1) * M], v_sb[:, p1 % 2, h * P:(h + 1) * P], True, True)
                    ins.then_inc(p_s2, 1)
                if nxt:
                    if g == -1:
                        pe.wait_ge(g_lo, 4)
                    if now:
                        unit(pe, v_soft, i, g, 1, N_SOFT)
                    project(bank[:, 4, :], 3, n1).then_inc(p_g, 1)
                    if prv:
                        unit(pe, c_o, i, g - 1, 1, 5)
                    if g == -1:
                        reached(pe, z_sb, 1, 2, 2)
                    project(bank[:, 7, :], 2, n1).then_inc(p_v, 1)
                if g == 0 and tile2:
                    if prv:
                        unit(pe, v_s2, i, g - 1)
                    else:
                        unit(pe, v_su, i, g)
                    l0_xnT(i + 2)
                if g == 1:
                    if tile1:
                        unit(pe, c_o, i, g - 1, 1, 5)
                        unit(pe, v_s2, i, g - 1)
                        l0_hT(i + 1)
                    if tile2:
                        unit(pe, c_v, i, g + 1)
                        l0_z(i + 2)
                    if tile1:
                        unit(pe, v_sc, i, g + 1)
                        l0_out(i + 1)

            def ffn(w, first, done):
                for c in range(KI):
                    r = P if c < KI - 1 else LAST
                    for k in range(KD):
                        ins = mm(bank[0:r, first + c // 3, (c % 3) * P:(c % 3 + 1) * P], w[:, k, c * P:c * P + r], xT[:, k, :], k == 0, k == KD - 1)
                ins.then_inc(done, 1)

            step(0, -1)
            tiles(pe, step)

        @block.scalar
        def _(act):
            def copy(o, i_, scale=1.0):
                return act.activation(o, i_, ACT.Copy, scale=scale)

            for n in range(8):
                act.wait_ge(t_xn, n + 1)
                copy(xnT_all[:, n // 4, (n % 4) * 512:(n % 4 + 1) * 512], bank[:, n, :]).then_inc(c_xn, 1)
            act.wait_ge(ld_gate, 64)
            act.activation(aa, cols[:, 0, :], ACT.Tanh).then_inc(c_aa, 1)
            for n in range(8):
                e = n // 4
                act.wait_ge(t_gate, n + 1)
                act.activation(ug[:, e, (n % 4) * 512:(n % 4 + 1) * 512], bank[:, n, :], ACT.Sigmoid,
                               bias=cols[:, 4, e:e + 1]).then_inc(c_gate, 1)
            act.wait_ge(t_lr, 1)
            copy(r42, bank[0:4, 3, 0:NB]).then_inc(c_lr, 1)

            def l0_xnT(j):
                reached(act, z_t, j, 1, 1)
                reached(act, z_part, j, 5, 0)
                copy(xnT[:], bank[:, 5, 0:D]).then_inc(z_c, 1)

            def l0_hT(j):
                reached(act, z_hT, j, 1, 1)
                copy(hT, bank[:, 5:7, :]).then_inc(z_hc, 1)

            def l0_xT(j):
                reached(act, z_x2t, j, 1, 1)
                reached(act, p_up, j, 1, 0)
                copy(xT[:], bank[:, 3, 0:D]).then_inc(z_x2, 1)
                unit(act, p_g, j, 0, 0)
                unit(act, p_v, j, 0, 0)
                copy(x_f16[:, 0, :], bank[:, 3, 0:D], X_SCALE).then_inc(z_hi, 1)

            def table(n):
                at, w = LUT_PARTS[n]
                act.wait_ge(t_hot, LUT * (n + 1))
                for c in range(3):
                    lo, hi = c * 512, min(w, (c + 1) * 512)
                    copy(w_lut[:, at + lo:at + hi], bank[:, (0 if n % 2 == 0 else 3) + c, 0:hi - lo], 0.5 if n == 2 else 1.0).then_inc(c_lut, 1)

            def squares(done, *blocks):
                for n, b in enumerate(blocks, done):
                    act.wait_ge(ld_w[b], 16)
                    if n > 0:
                        act.wait_ge(c_sq, n)
                    src = w_apart[b // 4] if b % 4 == 3 else w_f32[:, b, :]
                    act.activation(arena[:, 1024:3072], src, ACT.Square, accum_out=w_sq[:, b:b + 1]).then_inc(c_sq, 1)

            l0_xnT(0)
            table(0)
            act.wait_ge(v_scan, 4 * Y_STEPS)
            squares(0, 0, 1, 4, 5, 6, 3, 7)
            table(1)
            l0_xnT(1)
            squares(7, 2)
            def w_high(n, chains=(0, 1)):
                for b in [W_FIRST[n][c] for c in chains]:
                    if n > 0:
                        act.wait_ge(v_lo if b < 4 else g_lo, n)
                    src = w_apart[b // 4] if b % 4 == 3 else w_f32[:, b, :]
                    if b < 4:
                        act.activation(w_f16[:, (b + 1) % 4, 0, :], src, ACT.Copy, scale=w_scale).then_inc(c_hi, 1)
                    else:
                        act.activation(src, src, ACT.Copy, scale=w_scale).then_inc(c_scaled, 1)
                        act.wait_ge(c_scaled, n + 1)
                        copy(w_f16[:, 4 + (b + 1) % 4, 0, :], src).then_inc(c_hi, 1)

            act.wait_ge(v_scale, 8)
            w_high(0)
            act.activation(rope_tab[:], rope_tab[:], ACT.Copy, scale=unscale).then_inc(c_rope, 1)
            l0_hT(0)
            w_high(1)
            w_high(2)
            act.wait_ge(ld_o, 16)
            wo_flat = wo[:, :, :].rearrange("p h n -> p (h n)")
            act.activation(wo_flat, wo_flat, ACT.Copy, scale=half_norm).then_inc(c_wo, 1)
            w_high(3, [0])
            table(2)
            l0_xT(0)
            w_high(3, [1])

            def step(i, g):
                now, nxt, prv, prv2, tile1, tile2 = parts(i, g)
                p1 = (g - 1) % GROUPS
                if now:
                    unit(act, p_qkT, i, g)
                    unit(act, p_ok, i, g - 1)
                    copy(qkT[:, 0:512], bank[:, 0, :]).then_inc(c_qkT, 1)
                    copy(qkT[:, 512:1024], bank[:, 1, :]).then_inc(c_qkT, 1)
                    unit(act, p_cs, i, g)
                    copy(csum[:, g * 256:(g + 1) * 256], bank[:, 3, 0:256]).then_inc(c_cs, 1)
                if prv:
                    unit(act, p_pT, i, g - 1)
                    unit(act, p_o, i, g - 2)
                    if now:
                        unit(act, p_esT, i, g)
                    copy(pT, bank[:, 5, 0:256]).then_inc(c_pT, 1)
                if now:
                    unit(act, p_esT, i, g)
                    unit(act, p_w2, i, g - 2)
                    copy(esT[:, g % 2, :], bank[:, 5, 256:512]).then_inc(c_esT, 1)
                if prv2:
                    unit(act, p_ogT, i, g - 2)
                    unit(act, p_wo, i, g - 3)
                    copy(ogT, bank[:, 3, :]).then_inc(c_ogT, 1)
                if g == 0 and now:
                    reached(act, p_gate, i, 1, 1)
                    reached(act, p_down, i, 1, 0)
                    for r, b, lo, w, k0 in F_PARTS:
                        act.activation(f_th[0:r, k0:k0 + w // P, :].rearrange("p k t -> p (k t)"), bank[0:r, b, lo:lo + w],
                                       ACT.Tanh, scale=0.5).then_inc(c_fth, 1)
                if g == 3 and tile1:
                    l0_xT(i + 1)
                if (g == 3 and tile1) or g == -1:
                    reached(act, p_s1, i + 1 if g == 3 else i, 1, 1)
                    unit(act, p_s, i, g)
                    copy(s16[0:16, :], bank[0:16, 3, 0:P]).then_inc(c_s1, 1)
                if prv:
                    unit(act, p_o, i, g - 1)
                    unit(act, g_osg, i, g - 2)
                    unit(act, g_r, i, g - 2, 1, 2)
                    unit(act, c_o, i, g - 2, 5, 5)
                    copy(o_sb, bank[:, 6:8, 0:256]).then_inc(c_o, 1)
                if now:
                    unit(act, v_soft, i, g, 2, N_SOFT)
                    for h in range(GH):
                        x = ox[:, h * M:(h + 1) * M]
                        act.activation(x, x, ACT.Exp, bias=small[:, 0, h:h + 1], scale=-1.0, accum_out=small[:, 1, h:h + 1]).then_inc(c_soft, 1)
                if prv:
                    unit(act, c_o, i, g - 1, 1, 5)
                    for w in range(GH):
                        act.activation(am[:, w * P:(w + 1) * P], o_sb[:, w * P:(w + 1) * P], ACT.Square,
                                       accum_out=small[:, 4, w:w + 1]).then_inc(c_o, 1)
                if nxt:
                    unit(act, v_sc, i, g + 1)
                    act.activation(es[:, (g + 1) % 2, :], es[:, (g + 1) % 2, :], ACT.Exp).then_inc(c_es, 1)
                    unit(act, p_v, i, g + 1)
                    unit(act, p_s2, i, g - 1)
                    act.activation(v_sb[:, (g + 1) % 2, :], bank[:, 7, :], ACT.Copy, scale=unscale).then_inc(c_v, 1)
                if g == 1 and tile1:
                    l0_hT(i + 1)
                if nxt:
                    unit(act, p_g, i, g + 1)
                    unit(act, g_osg, i, g - 1)
                    act.activation(sg[:, (g + 1) % 2, :], bank[:, 4, :], ACT.Tanh, scale=half_unscale).then_inc(c_th, 1)
                if g == 0 and tile2:
                    l0_xnT(i + 2)

            step(0, -1)
            tiles(act, step)

        @block.vector
        def _(dve):
            tt, ts, stt = dve.tensor_tensor, dve.tensor_scalar, dve.scalar_tensor_tensor
            def l0_xn(j):
                reached(dve, l_x, j, 16, 16)
                reached(dve, z_t, j, 1, 0)
                reached(dve, z_xnb, j, 1, 0)
                ts(xn[:], x_in[:], mean1[:, bass.ds(j, 1), 0:1].rearrange("p a b -> p (a b)"), rstd1[:, bass.ds(j, 1)], ALU.subtract, ALU.mult).then_inc(z_xn, 1)

            def l0_zsb(j):
                reached(dve, z_hid, j, 1, 0)
                for c in range(2):
                    reached(dve, z_mm, j, 2, c + 1)
                    stt(z[:, c * 512:(c + 1) * 512], bank[:, Z_BANKS[c], :], scales[:, 2:3], b_syn[:, c * 512:(c + 1) * 512], ALU.mult, ALU.add).then_inc(z_sb, 1)

            def l0_top(j, steps):
                for n in steps:
                    r, strike = n // 2, n % 2
                    if n == 0:
                        reached(dve, z_sb, j, 2, 2)
                    else:
                        reached(dve, z_top, j, N_TOP, n)
                    src = z if r == 0 else zw
                    if strike:
                        if n == 1:
                            reached(dve, z_hT, j, 1, 0)
                        apart(dve)
                        dve.match_replace(out=zw, in_to_replace=top8[:, r % 2, :], in_values=src, imm_value=LOW).then_inc(z_top, 1)
                    else:
                        apart(dve)
                        dve.max(out=top8[:, r % 2, :], in_=src).then_inc(z_top, 1)

            def l0_hidden(j):
                reached(dve, z_top, j, N_TOP, N_TOP - 1)
                k = TOPK - 8 * (ROUNDS - 1) - 1
                ts(thr[:], top8[:, (ROUNDS - 1) % 2, k:k + 1], 0.0, None, ALU.max).then_inc(z_top, 1)
                reached(dve, z_top, j, N_TOP, N_TOP)
                stt(zw, z, thr[:, 0:1], z, ALU.is_ge, ALU.mult).then_inc(z_hid, 1)

            def l0_norm(j, part):
                par = j % 2
                if part == 0:
                    reached(dve, z_out, j, 1, 1)
                    reached(dve, z_xnb, j, 1, 1)
                    reached(dve, z_x2t, j, 1, 0)
                    stt(norm[:], bank[:, 3, 0:D], scales[:, 3:4], xn_b[:], ALU.mult, ALU.add).then_inc(z_v, 1)
                    reached(dve, z_v, j, VZ, 1)
                    dve.bn_stats(stat[:, 0, :], norm[:]).then_inc(z_v, 1)
                    reached(dve, z_v, j, VZ, 2)
                    apart(dve)
                    dve.bn_aggr(mv[:, 0, :], stat[:, 0, :]).then_inc(z_v, 1)
                elif part == 1:
                    reached(dve, z_g, j, GZ, 2)
                    ts(norm[:], norm[:], mv[:, 0, 0:1], rs[:, 0, 1:2], ALU.subtract, ALU.mult).then_inc(z_v, 1)
                elif part == 2:
                    reached(dve, z_g, j, GZ, 5)
                    x = x1[:, bass.ds(par, 1), :].rearrange("p a d -> p (a d)")
                    apart(dve)
                    dve.bn_stats(stat[:, 1, :], x).then_inc(z_v, 1)
                    reached(dve, z_v, j, VZ, 5)
                    apart(dve)
                    dve.bn_aggr(mv[:, 1, :], stat[:, 1, :]).then_inc(z_v, 1)
                else:
                    reached(dve, z_g, j, GZ, 7)
                    x = x1[:, bass.ds(par, 1), :].rearrange("p a d -> p (a d)")
                    ts(norm[:], x, mv[:, 1, 0:1], rs[:, 1, 1:2], ALU.subtract, ALU.mult).then_inc(z_v, 1)

            dve.memset(half_neg[:], -0.5).then_inc(v_const, 1)
            dve.memset(ones_m, 1.0).then_inc(v_const, 1)
            dve.memset(s16[:], 1.0).then_inc(v_const, 1)
            dve.memset(idx_i[:, LUT_END - D:LUT_END], 0).then_inc(v_idx, 1)
            for t in range(TILES):
                dve.wait_ge(ld_x[t // 4], 16)
                dve.bn_stats(stat1[:, t, :], x_all[:, t, :]).then_inc(v_stat, 1)
            for t in range(TILES):
                dve.wait_ge(v_stat, t + 1)
                dve.bn_aggr(mean1[:, t, :], stat1[:, t, :]).then_inc(v_stat, 1)
            dve.wait_ge(ld_ident, 32)
            dve.tensor_copy(ident_b[:], ident[:]).then_inc(v_const, 1)
            dve.tensor_copy(lut_b[:, 0, :], lut[:, 0, :]).then_inc(v_lut, 1)
            for s in (1, 2):
                dve.wait_ge(v_lut, 2 * s - 1)
                tt(lut[:, s, :], lut[:, s - 1, :], lut_b[:, s - 1, :], ALU.subtract).then_inc(v_lut, 1)
                dve.wait_ge(v_lut, 2 * s)
                dve.tensor_copy(lut_b[:, s, :], lut[:, s, :]).then_inc(v_lut, 1)
            dve.wait_ge(g_rstd, 2)
            for t in range(TILES):
                ts(xn_all[:, t, :], x_all[:, t, :], mean1[:, t, 0:1], rstd1[:, t:t + 1], ALU.subtract, ALU.mult).then_inc(v_xn, 1)
            dve.wait_ge(ld_syn, 32)
            out_flat = t_out[:, :, :].rearrange("p k n -> p (k n)")
            syn_flat = zbuf[:, :, :].rearrange("p a n -> p (a n)")
            dve.tensor_reduce(scales[:, 0:1], syn_flat, AX.X, ALU.add, apply_absolute_value=True).then_inc(v_tern, 1)
            dve.tensor_reduce(scales[:, 1:2], out_flat, AX.X, ALU.add, apply_absolute_value=True).then_inc(v_tern, 1)
            dve.wait_ge(t_tern, 1)
            ts(scales[:, 2:4], bank[:, 7, 0:2], 1.0 / (NSYN * D), None, ALU.mult).then_inc(v_tern, 1)
            dve.wait_ge(v_tern, 3)
            ts(scales[:, 4:6], scales[:, 2:4], 1e-8, 0.5, ALU.add, ALU.mult).then_inc(v_tern, 1)
            dve.wait_ge(v_tern, 4)
            ts(scales[:, 6:8], scales[:, 4:6], -1.0, None, ALU.mult).then_inc(v_tern, 1)
            dve.wait_ge(v_tern, 5)
            ts(tern_tmp, syn_flat, scales[:, 6:7], None, ALU.is_lt).then_inc(v_tern, 1)
            dve.wait_ge(v_tern, 6)
            stt(t_syn[:, :, :].rearrange("p k n -> p (k n)"), syn_flat, scales[:, 4:5], tern_tmp, ALU.is_gt, ALU.subtract).then_inc(v_tern, 1)
            dve.wait_ge(v_tern, 7)
            ts(tern_tmp, out_flat, scales[:, 7:8], None, ALU.is_lt).then_inc(v_tern, 1)
            dve.wait_ge(v_tern, 8)
            stt(out_flat, out_flat, scales[:, 5:6], tern_tmp, ALU.is_gt, ALU.subtract).then_inc(v_tern, 1)
            dve.wait_ge(ld_lut, 64)
            for n in range(2):
                dve.tensor_copy(idx_b[n], idx_i[:, LUT_AT[n]:LUT_AT[n + 1]]).then_inc(v_idx, 1)

            def one_hot(*steps):
                for m in steps:
                    n, k = m // LUT, m % LUT
                    w = LUT_PARTS[n][1]
                    if m == 0:
                        dve.wait_ge(v_idx, 3)
                    if m == 2 * LUT:
                        dve.wait_ge(v_idx, 4)
                    if m >= 2:
                        dve.wait_ge(t_hot, m - 1)
                    ts(hot[:, k % 2, 0:w], idx_b[n], float(k), None, ALU.is_equal).then_inc(v_hot, 1)

            for n in range(4):
                e, s = n // NB, n % NB
                dve.wait_ge(c_gate, 2 * n + 2)
                r = ug[:, e, s * T:(s + 1) * T]
                tt(r, r, xnT_all[:, e, s * T:(s + 1) * T], ALU.mult).then_inc(v_ug, 1)
                if n % 2 == 1:
                    one_hot(n // 2)
            dve.wait_ge(v_ug, 4)
            dve.tensor_reduce(u_sum, ug.rearrange("p k (s t) -> p k s t", s=NB), AX.X, ALU.add).then_inc(v_ug, 1)
            one_hot(2)
            dve.wait_ge(c_aa, 1)
            ts(col_t[:, 0, :], aa, 1e-6, None, ALU.max).then_inc(v_ug, 1)
            dve.wait_ge(v_ug, 6)
            dve.reciprocal(col_t[:, 1, :], col_t[:, 0, :]).then_inc(v_ug, 1)
            dve.wait_ge(v_ug, 7)
            tt(col_t[:, 2, :], aa, col_t[:, 1, :], ALU.mult).then_inc(v_ug, 1)
            tt(col_t[:, 3, :], cols[:, 1, :], cols[:, 2, :], ALU.mult).then_inc(v_ug, 1)
            l0_xn(0)
            one_hot(3)
            dve.wait_ge(v_ug, 9)
            n = 0
            for s in range(NB):
                for e in range(KD):
                    m = 4 + 3 * (NB * s + e)
                    u_r, y_r, b_r = ug[:, e, s * T:(s + 1) * T], ys[:, e, s * T:(s + 1) * T], bu[:, e, :]
                    if s > 0:
                        dve.wait_ge(v_scan, n - 2 * Y_STEPS + 3)
                    ts(b_r, u_r, col_t[:, 3, e:e + 1], None, ALU.mult).then_inc(v_scan, 1)
                    dve.wait_ge(v_scan, n + 1)
                    ts(b_r[:, 0:1], b_r[:, 0:1], col_t[:, 2, e:e + 1], None, ALU.mult).then_inc(v_scan, 1)
                    one_hot(m)
                    dve.wait_ge(v_scan, n + 2)
                    dve.tensor_tensor_scan(y_r, aa[:, e:e + 1].to_broadcast([P, T]), b_r, 0.0, ALU.mult, ALU.add).then_inc(v_scan, 1)
                    one_hot(m + 1)
                    if n == 0:
                        dve.wait_ge(t_lr, 2)
                        stt(d_eff, bank[:, 4, 0:KD * NB].rearrange("p (k s) -> p k s", k=KD), 1.0 / (T * 4.0),
                            cols[:, 3, :, None].to_broadcast([P, KD, NB]), ALU.mult, ALU.add).then_inc(v_deff, 1)
                        dve.wait_ge(v_deff, 1)
                    dve.wait_ge(v_scan, n + 3)
                    stt(y_r, u_r, d_eff[:, e, s:s + 1], y_r, ALU.mult, ALU.add).then_inc(v_scan, 1)
                    one_hot(m + 2)
                    n += Y_STEPS
                    if s == 0 and e == 1:
                        dve.wait_ge(ld_misc, 16 * MISC)
                        l0_zsb(0)
                    if s == 1:
                        for q in range(4 * e, 4 * e + 4):
                            dve.wait_ge(t_y, q + 1)
                            r = x_all[:, 2 * q:2 * q + 2, :].rearrange("p t d -> p (t d)")
                            tt(r, r, bank[:, 6 + q % 2, :], ALU.add).then_inc(v_xy, 1)
            dve.tensor_copy(idx_b[2], idx_i[:, LUT_AT[2]:LUT_END]).then_inc(v_idx, 1)
            def w_low(n):
                b = W_FIRST[n][0]
                dve.wait_ge(c_hi, 2 * n + 1)
                src = w_apart[0] if b == 3 else w_f32[:, b, :]
                hi, lo = (w_f16[:, (b + 1) % 4, q, :] for q in range(2))
                stt(lo, src, w_scale, hi, ALU.mult, ALU.subtract).then_inc(v_lo, 1)

            def x_low(j):
                reached(dve, z_hi, j, 1, 1)
                stt(x_f16[:, 1, :], bank[:, 3, 0:D], X_SCALE, x_f16[:, 0, :], ALU.mult, ALU.subtract).then_inc(z_lo, 1)

            for n in range(N_TOP - 1):
                one_hot(LUT + n)
                l0_top(0, [n])
                if n == LUT // 2:
                    l0_xn(1)
                if n == LUT + 7:
                    dve.wait_ge(t_sq, 1)
                    dve.tensor_reduce(w_sum, bank[:, 4, 0:BLOCKS], AX.X, ALU.add).then_inc(v_scale, 1)
                    dve.wait_ge(v_scale, 1)
                    ts(w_sum, w_sum, 1e-30, None, ALU.max).then_inc(v_scale, 1)
                    dve.wait_ge(g_root, 1)
                    ts(w_pow.bitcast(I32), w_root.bitcast(I32), 0x7F800000, None, ALU.bitwise_and).then_inc(v_scale, 1)
                    dve.wait_ge(v_scale, 3)
                    dve.reciprocal(w_inv, w_pow).then_inc(v_scale, 1)
                    ts(w_scale, w_pow, W_TOP, None, ALU.mult).then_inc(v_scale, 1)
                    dve.wait_ge(v_scale, 4)
                    ts(unscale, w_inv, 1.0 / (W_TOP * X_SCALE), None, ALU.mult).then_inc(v_scale, 1)
                    dve.wait_ge(v_scale, 6)
                    ts(half_unscale, unscale, 0.5, None, ALU.mult).then_inc(v_scale, 1)
                    dve.wait_ge(v_scale, 7)
                    tt(half_norm, gnorm[:, 0:1], half_unscale, ALU.mult).then_inc(v_scale, 1)
            one_hot(*range(LUT + N_TOP - 1, LUT + TOP0_AT))
            w_low(0)
            l0_hidden(0)
            one_hot(LUT + TOP0_AT, LUT + TOP0_AT + 1)
            w_low(1)
            l0_zsb(1)
            for part in range(3):
                one_hot(LUT + TOP0_AT + 2 + part)
                l0_norm(0, part)
                if part == 0:
                    w_low(2)
                l0_top(1, range(2 * part, 2 * part + 2))
            l0_norm(0, 3)
            w_low(3)
            x_low(0)
            l0_top(1, range(6, TOP_FIRST))

            def renew(i, states, done):
                def zero():
                    for x in states:
                        dve.memset(x, 0.0).then_inc(done, 1)
                if isinstance(i, int):
                    if i % SEQ_TILES == 0:
                        zero()
                    else:
                        dve.sem_inc(done, len(states))
                else:
                    apart(dve)
                    with dve.If(i == SEQ_TILES):
                        zero()
                    with dve.Else():
                        dve.sem_inc(done, len(states))

            def rope(i, g):
                unit(dve, p_qk, i, g)
                unit(dve, g_rope, i, g, 0, 2)
                v = bank[:, 0:2, :].rearrange("p b (h a m) -> p (b h) a m", a=2, m=64)
                cos = rope_now[:, None, None, 0:64].to_broadcast([P, 2 * GH, 2, 64])
                sin = rope_now[:, None, None, 64:128].to_broadcast([P, 2 * GH, 2, 64])
                tt(t1.rearrange("p (h a m) -> p h a m", a=2, m=64), v, cos, ALU.mult).then_inc(v_rope, 1)
                tt(t2.rearrange("p (h a m) -> p h a m", a=2, m=64), v[:, :, ::-1, :], sin, ALU.mult).then_inc(v_rope, 1)

            def heads(x, n):
                return x.rearrange("p (h m) -> p h m", h=GH)

            def over(x, n):
                return x[:, :, None].to_broadcast([P, GH, n])

            def step(i, g):
                now, nxt, prv, prv2, tile1, tile2 = parts(i, g)
                p1 = (g - 1) % GROUPS
                j, top = None, []
                if (g in (2, 3) and tile2) or (g in (0, 1) and tile1):
                    j, top = i + (2 if g in (2, 3) else 1), list(range(*TOP_OF[g]))

                def some(n):
                    l0_top(j, top[:n])
                    del top[:n]

                if g == -1:
                    j, top = 1, list(range(TOP_FIRST, TOP_OF[3][1]))
                if g == 2 and tile1:
                    l0_norm(i + 1, 0)
                if g == 2 and tile2:
                    l0_zsb(i + 2)
                if g == 0 and tile2:
                    l0_xn(i + 2)
                if g == 0 and now:
                    for n, (r, b, lo, w, k0) in enumerate(F_PARTS):
                        reached(dve, c_fth, i, 3, 3)
                        f = f_th[0:r, k0:k0 + w // P, :].rearrange("p k t -> p (k t)")
                        stt(f, f, 1.0, bank[0:r, b, lo:lo + w], ALU.add, ALU.mult).then_inc(v_f, 1)
                if g == 3 and now:
                    for n, (r, b, lo, w, k0) in enumerate(F_PARTS):
                        reached(dve, p_up, i, 1, 1)
                        reached(dve, v_f, i, V_F, 3)
                        f = f_th[0:r, k0:k0 + w // P, :].rearrange("p k t -> p (k t)")
                        tt(f, f, bank[0:r, b, lo:lo + w], ALU.mult).then_inc(v_f, 1)
                if now:
                    unit(dve, p_a, i, g)
                    unit(dve, p_ok, i, g - 1)
                    unit(dve, c_o, i, g - 2, 5, 5)
                    tt(heads(am, P), heads(bank[:, 4, :], P), tri[:, None, :].to_broadcast([P, GH, P]), ALU.mult).then_inc(v_a, 1)
                if prv:
                    unit(dve, p_w2, i, g - 1)
                    unit(dve, p_o, i, g - 2)
                    tt(wm.rearrange("p (b q t) -> p b q t", b=2, q=2), bank[:, 5:7, 0:256].rearrange("p b (q t) -> p b q t", q=2),
                       tri[:, None, None, :].to_broadcast([P, 2, 2, P]), ALU.mult).then_inc(v_w2, 1)
                if g == 3 and tile1:
                    x_low(i + 1)
                if now:
                    unit(dve, c_cs, i, g)
                    unit(dve, v_soft, i, g - 1, N_SOFT, N_SOFT)
                    dve.reciprocal(enz, csum[:, g * 256:(g + 1) * 256]).then_inc(v_enz, 1)
                if g >= 0:
                    some(2)
                if nxt:
                    if g in (3, -1):
                        reached(dve, rope_ld, i + 1 if g == 3 else i, 1, 1)
                    rope(i, g + 1)
                if now:
                    unit(dve, p_su, i, g)
                    s = s_qk[:, g * 256:(g + 1) * 256]
                    tt(s, s, bank[:, 5, 0:256], ALU.add).then_inc(v_su, 1)
                    unit(dve, p_ok, i, g)
                    unit(dve, v_enz, i, g)
                    stt(ox, bank[:, 4, 0:256], -QK_SCALE, enz, ALU.mult, ALU.mult).then_inc(v_soft, 1)
                    unit(dve, v_soft, i, g, 1, N_SOFT)
                    dve.tensor_reduce(small[:, 0, :], heads(ox, M), AX.X, ALU.min).then_inc(v_soft, 1)
                if g == 3 and tile1:
                    reached(dve, p_ok, i, GROUPS, GROUPS)
                    reached(dve, c_cs, i, GROUPS, GROUPS)
                    renew(i + 1, [s_qk[:], csum[:]], reset_qk)
                if g == 2 and tile1:
                    l0_norm(i + 1, 1)
                if prv:
                    unit(dve, p_s2, i, g - 1)
                    s = s_v[:, 2 * p1:2 * p1 + 2, :]
                    tt(s, s, bank[:, 5, 0:256].rearrange("p (q n) -> p q n", q=2), ALU.add).then_inc(v_s2, 1)
                if nxt:
                    unit(dve, p_s, i, g + 1)
                    unit(dve, c_es, i, g)
                    unit(dve, p_s2, i, g - 1)
                    ts(es[:, (g + 1) % 2, :], bank[:, 3, 0:256], -CLAMP, CLAMP, ALU.max, ALU.min).then_inc(v_sc, 1)
                if g == 1 and has_before(i):
                    reached(dve, p_wo, i, GROUPS, 0)
                    reached(dve, st_out, i - 1, 16, 0)
                    x = x1[:, bass.ds((i + 1) % 2, 1), :].rearrange("p a d -> p (a d)")
                    tt(o_fin[:], x, bank[:, 2, 0:D], ALU.add).then_inc(v_fin, 1)
                some(1)
                if g == 1 and tile1:
                    some(len(top))
                    l0_hidden(i + 1)
                if now:
                    unit(dve, c_soft, i, g, GH, GH)
                    dve.reciprocal(small[:, 2, :], small[:, 1, :]).then_inc(v_soft, 1)
                    unit(dve, v_soft, i, g, 3, N_SOFT)
                    if g == 2:
                        some(1)
                    unit(dve, g_pr, i, g)
                    tt(heads(pr, M), heads(pr, M), over(small[:, 2, :], M), ALU.mult).then_inc(v_soft, 1)
                if g == 2 and tile1:
                    l0_norm(i + 1, 2)
                some(1)
                if nxt:
                    unit(dve, c_th, i, g + 1)
                    r = sg[:, (g + 1) % 2, :]
                    stt(r, r, 1.0, bank[:, 4, :], ALU.add, ALU.mult).then_inc(v_sg, 1)
                if prv:
                    unit(dve, g_r, i, g - 1, 2, 2)
                    unit(dve, g_osg, i, g - 1)
                    tt(heads(o_gated, P), heads(o_gated, P), over(small[:, 5, :], P), ALU.mult).then_inc(v_og, 1)
                if g == 0 and now:
                    reached(dve, v_s2, i, GROUPS, 0)
                    renew(i, [s_v[:]], reset_v)
                if g == 2 and tile1:
                    l0_norm(i + 1, 3)
                if g == -1:
                    dve.wait_ge(t_hot, 3 * LUT)
                    renew(0, [s_qk[:], csum[:]], reset_qk)
                some(len(top))

            step(0, -1)
            tiles(dve, step)

        @block.gpsimd
        def _(pool):
            tt, ts = pool.tensor_tensor, pool.tensor_scalar
            pool.wait_ge(v_stat, 2 * TILES)
            pool.wait_ge(v_const, 1)
            ts(rstd1[:], mean1[:, :, 1], LN_EPS, None, ALU.add).then_inc(g_rstd, 1)
            pool.wait_ge(g_rstd, 1)
            tt(rstd1[:], rstd1[:], half_neg[:], ALU.pow).then_inc(g_rstd, 1)

            def l0_parts(j):
                reached(pool, z_c, j, 1, 1)
                reached(pool, z_mm, j, 2, 0)
                for n in range(5):
                    if n > 0:
                        reached(pool, z_part, j, 5, n)
                    apart(pool)
                    if n % 2 == 0:
                        ins = pool.tensor_copy(x_part[:, n // 2, :], xnT[:])
                    else:
                        ins = tt(xnT[:], xnT[:], x_part[:, n // 2, :], ALU.subtract)
                    ins.then_inc(z_part, 1)

            def l0_xnb(j):
                reached(pool, z_xn, j, 1, 1)
                reached(pool, z_v, j, VZ, 1 - VZ)
                tt(xn_b[:], xn[:], rows[:, 0, :], ALU.add).then_inc(z_xnb, 1)

            def l0_norm(j, part):
                par = j % 2
                n = 0 if part == 0 else 5
                if part != 1:
                    reached(pool, z_v, j, VZ, 3 if part == 0 else 6)
                    q = 0 if part == 0 else 1
                    apart(pool)
                    ts(rs[:, q, 0:1], mv[:, q, 1:2], LN_EPS, None, ALU.add).then_inc(z_g, 1)
                    reached(pool, z_g, j, GZ, n + 1)
                    tt(rs[:, q, 1:2], rs[:, q, 0:1], half_neg[:, 0:1], ALU.pow).then_inc(z_g, 1)
                else:
                    reached(pool, z_v, j, VZ, 4)
                    tt(norm[:], norm[:], rows[:, 1, :], ALU.mult).then_inc(z_g, 1)
                    reached(pool, z_g, j, GZ, 3)
                    tt(norm[:], norm[:], rows[:, 2, :], ALU.add).then_inc(z_g, 1)
                    reached(pool, z_g, j, GZ, 4)
                    reached(pool, l_xy, j, 16, 16)
                    reached(pool, v_fin, j, 1, -1)
                    x = x1[:, bass.ds(par, 1), :].rearrange("p a d -> p (a d)")
                    tt(x, norm[:], xy_in[:], ALU.add).then_inc(z_g, 1)

            pool.wait_ge(v_lut, 5)
            pool.wait_ge(v_const, 4)
            for s in range(3):
                tt(diag[s], ident_b[:, None, :].to_broadcast([P, LUT, P]), lut_b[:, s, :, None].to_broadcast([P, LUT, P]), ALU.mult).then_inc(g_diag, 1)
            l0_parts(0)
            pool.wait_ge(ld_misc, 16 * MISC)
            l0_xnb(0)
            l0_parts(1)
            pool.wait_ge(v_scale, 2)
            tt(w_root, w_sum, half_neg[:, 0:1], ALU.pow).then_inc(g_root, 1)
            def w_low(n):
                b = W_FIRST[n][1]
                pool.wait_ge(c_hi, 2 * n + 2)
                src = w_apart[1] if b == 7 else w_f32[:, b, :]
                hi, lo = (w_f16[:, 4 + (b + 1) % 4, q, :] for q in range(2))
                tt(lo, src, hi, ALU.subtract).then_inc(g_lo, 1)

            def rope_rows(t):
                pool.tensor_copy(rope_now[:], rope_tab[:, bass.ds(t % SEQ_TILES, 1), :].rearrange("p a n -> p (a n)")).then_inc(rope_ld, 1)

            w_low(0)
            w_low(1)
            l0_norm(0, 0)
            l0_norm(0, 1)
            l0_norm(0, 2)
            w_low(2)
            pool.wait_ge(c_rope, 1)
            rope_rows(0)
            w_low(3)
            l0_xnb(1)

            def half(x, q):
                return x.rearrange("p (h a m) -> p h a m", a=2, m=64)[:, :, q, :]

            def step(i, g):
                now, nxt, prv, prv2, tile1, tile2 = parts(i, g)
                if g == 3 and tile1:
                    unit(pool, v_rope, i, g, 2, 2)
                    apart(pool)
                    rope_rows(i + 1)
                if g == 1 and tile2:
                    l0_parts(i + 2)
                if g == 2 and tile1:
                    l0_norm(i + 1, 0)
                if nxt:
                    unit(pool, v_rope, i, g + 1, 2, 2)
                    unit(pool, p_su, i, g)
                    tt(half(qk, 0), half(t1, 0), half(t2, 0), ALU.subtract).then_inc(g_rope, 1)
                    tt(half(qk, 1), half(t1, 1), half(t2, 1), ALU.add).then_inc(g_rope, 1)
                if g == 2 and tile1:
                    l0_norm(i + 1, 1)
                if now:
                    unit(pool, c_soft, i, g, GH, GH)
                    unit(pool, p_pT, i, g - 1)
                    tt(pr, ox, enz, ALU.mult).then_inc(g_pr, 1)
                if prv:
                    unit(pool, c_o, i, g - 1, 1, 5)
                    unit(pool, v_sg, i, g - 1)
                    unit(pool, p_ogT, i, g - 2)
                    o, to = (x.rearrange("p (b q n) -> p b q n", b=2, q=2) for x in (o_sb, o_gated))
                    tt(to, o, sg[:, (g - 1) % 2, :].rearrange("p (q b n) -> p b q n", b=2, q=2), ALU.mult).then_inc(g_osg, 1)
                    unit(pool, c_o, i, g - 1, 5, 5)
                    unit(pool, v_og, i, g - 2)
                    apart(pool)
                    ts(small[:, 3, :], small[:, 4, :], 1.0 / DK, LN_EPS, ALU.mult, ALU.add).then_inc(g_r, 1)
                    unit(pool, g_r, i, g - 1, 1, 2)
                    tt(small[:, 5, :], small[:, 3, :], half_neg[:, 0:GH], ALU.pow).then_inc(g_r, 1)
                if g == 2 and tile1:
                    l0_norm(i + 1, 2)
                if g == 2 and tile2:
                    l0_xnb(i + 2)

            step(0, -1)
            tiles(pool, step)


_OUT = (TILES * P, D)


def kernel(**inputs):
    import numpy as _np
    import concourse.bacc as _bacc
    from concourse import mybir as _mybir
    from concourse.bass_utils import run_bass_kernel_spmd as _run

    def arr(name):
        return _np.asarray(inputs[name])

    def col(name):
        return arr(name).reshape(KD, P).T

    pos = _np.arange(T, dtype=_np.float32)
    inv = _np.float32(1.0) / _np.float32(10000.0) ** (_np.arange(0, DK, 2, dtype=_np.float32) / _np.float32(DK))
    ang = pos[:, None] * inv[None, :]
    tri = _np.triu(_np.ones((P, P), _np.float32))
    last = _np.zeros((P, P), _np.float32)
    last[P - 1] = 1.0
    arrays = {
        "u": arr("L0_attn_u").reshape(TILES * P, D),
        "ident": _np.eye(P, dtype=_np.float32),
        "tri": tri,
        "last_row": last,
        "rope": _np.concatenate([_np.cos(ang), _np.sin(ang)], axis=1).astype(_np.float32),
        "cols": _np.stack([col("L0_attn_" + n) for n in ("a", "b", "c", "d", "gate_b")], axis=1),
        "gnorm": arr("L1_attn_g_norm_weight").reshape(DK, 1),
        "lut": arr("L1_ffn_lut").reshape(1, LUT),
        "gate_wT": arr("L0_attn_gate_w").T,
        "lr_u": arr("L0_attn_d_lr_u"),
        "lr_v": arr("L0_attn_d_lr_v"),
        "w_synT": arr("L0_ffn_W_syn").T,
        "w_outT": arr("L0_ffn_W_out").T,
        "b_syn": arr("L0_ffn_b_syn").reshape(1, NSYN),
        "b_out": arr("L0_ffn_b_out").reshape(1, D),
        "gamma": arr("L0_ffn_gamma").reshape(1, D),
        "beta": arr("L0_ffn_beta").reshape(1, D),
        "wqT": arr("L1_attn_Wq").T,
        "wkT": arr("L1_attn_Wk").T,
        "wvT": arr("L1_attn_Wv").T,
        "wgT": arr("L1_attn_Wg").T,
        "woT": arr("L1_attn_Wo").T,
        "ws1T": arr("L1_attn_Ws1").T,
        "ws2T": arr("L1_attn_Ws2").T,
        "bs2": arr("L1_attn_bs2").reshape(1, HEADS * M),
        "gate_idx": arr("L1_ffn_gate_idx").T,
        "up_idx": arr("L1_ffn_up_idx").T,
        "down_idx": arr("L1_ffn_down_idx").T,
    }
    arrays = {n: _np.ascontiguousarray(x) for n, x in arrays.items()}
    nc = _bacc.Bacc("TRN2", target_bir_lowering=False, num_devices=1)
    aps = {n: nc.dram_tensor("in_" + n, x.shape, _mybir.dt.from_np(x.dtype), kind="ExternalInput").ap() for n, x in arrays.items()}
    res = nc.dram_tensor("result", _OUT, F32, kind="ExternalOutput").ap()
    build(nc, aps, res)
    r = _run(nc, [{"in_" + n: x for n, x in arrays.items()}], core_ids=[0])
    return r.results[0]["result"].reshape(NB, T, D)
```
